# Optimizing a Trainium2 kernel written in Bass

```python
import numpy as np
import jax
import jax.numpy as jnp

def _softmax(x, axis=-1):
    return jax.nn.softmax(x, axis=axis)

def _gelu(x):
    return jax.nn.gelu(x, approximate=True)

def _silu(x):
    return jax.nn.silu(x)

def _sigmoid(x):
    return jax.nn.sigmoid(x)

def _layernorm(x, axis=-1, eps=1e-05):
    m = jnp.mean(x, axis=axis, keepdims=True)
    v = jnp.var(x, axis=axis, keepdims=True)
    return (x - m) / jnp.sqrt(v + eps)

def _scatter_add(tgt, idx, src, axis=0):
    return tgt.at[idx].add(src)

def _segment_sum(src, seg, n):
    return jax.ops.segment_sum(src, seg, n)
kernel_name = 'mk_gnn_ffn_d2_gnn_r8_100db1'

def setup_inputs(seed: int=0):
    np.random.seed(seed)
    _w = jnp.asarray

    def _rec_inputs():
        import jax
        import jax.numpy as jnp
        _gk = jax.random.key(seed)
        x = -0.0003713 + 1 * jax.random.normal(jax.random.fold_in(_gk, 1), (6250, 256), jnp.float32)
        src = jax.random.randint(jax.random.fold_in(_gk, 2), (100000,), 0, 6250, jnp.int32)
        dst = jax.random.randint(jax.random.fold_in(_gk, 3), (100000,), 0, 6250, jnp.int32)
        _o = jnp.argsort(dst, stable=True)
        src = src[_o]
        dst = dst[_o]
        return (x, src, dst)
    x, src, dst = _rec_inputs()

    def _L0_gnn_setup():
        import jax, jax.numpy as jnp
        import numpy as np
        N_NODES = 6250

        def gcn_conv(x, src, dst, W, b):
            N = x.shape[0]
            h = x @ W
            ones = jnp.ones(dst.shape, dtype=h.dtype)
            deg = jax.ops.segment_sum(ones, dst, num_segments=N) + 1.0
            dinv = jax.lax.rsqrt(deg)
            norm = dinv[src] * dinv[dst]
            agg = jax.ops.segment_sum(h[src] * norm[:, None], dst, num_segments=N)
            agg = agg + h * (dinv * dinv)[:, None]
            return agg + b
        key = jax.random.key(seed)
        ks = jax.random.split(key, 8)
        in_dim, mid_dim, out_dim, fc_mid, proj_dim = (256, 128, 64, 128, 256)
        n_edges = 100000
        x = jax.random.normal(ks[0], (N_NODES, in_dim), dtype=jnp.float32)
        edge_index = jax.random.randint(ks[1], (2, n_edges), 0, N_NODES, dtype=jnp.int64)

        def glorot(k, fan_in, fan_out):
            lim = np.sqrt(6.0 / (fan_in + fan_out)).astype(np.float32)
            return jax.random.uniform(k, (fan_in, fan_out), jnp.float32, -lim, lim)
        return {'x': x, 'edge_index': edge_index, 'W1': glorot(ks[2], in_dim, mid_dim), 'b1': jnp.zeros((mid_dim,), jnp.float32), 'W2': glorot(ks[3], mid_dim, out_dim), 'b2': jnp.zeros((out_dim,), jnp.float32), 'fc1_w': glorot(ks[4], out_dim, fc_mid), 'fc1_b': jnp.zeros((fc_mid,), jnp.float32), 'fc2_w': glorot(ks[5], fc_mid, proj_dim), 'fc2_b': jnp.zeros((proj_dim,), jnp.float32)}
    _L0_gnn_all = _L0_gnn_setup()
    _L0_gnn_in = {k: v for k, v in _L0_gnn_all.items() if k in ('W1', 'b1', 'W2', 'b2', 'fc1_w', 'fc1_b', 'fc2_w', 'fc2_b')}
    del _L0_gnn_all

    def _L0_ffn_setup():
        import jax, jax.numpy as jnp
        import numpy as np
        B, A = (512, 8)
        IN, OUT = (256, 256)
        SH1, SH2 = (256, 128)
        EH1, EH2 = (128, 64)
        E, TOPK = (4, 2)

        def _shared_mlp(x, W1, b1, W2, b2, W3, b3):
            h = jax.nn.relu(x @ W1 + b1)
            h = jax.nn.relu(h @ W2 + b2)
            return h @ W3 + b3

        def _experts_mlp(x, eW1, eb1, eW2, eb2, eW3, eb3):
            h = jax.nn.relu(jnp.einsum('baf,efh->ebah', x, eW1) + eb1[:, None, None, :])
            h = jax.nn.relu(jnp.einsum('ebah,ehg->ebag', h, eW2) + eb2[:, None, None, :])
            o = jnp.einsum('ebag,ego->ebao', h, eW3) + eb3[:, None, None, :]
            return jnp.moveaxis(o, 0, -1)
        key = jax.random.key(seed)
        ks = jax.random.split(key, 16)
        s = 0.05
        return {'x': jax.random.normal(ks[0], (B, A, IN), jnp.float32), 'sW1': jax.random.normal(ks[1], (IN, SH1), jnp.float32) * s, 'sb1': jnp.zeros((SH1,), jnp.float32), 'sW2': jax.random.normal(ks[2], (SH1, SH2), jnp.float32) * s, 'sb2': jnp.zeros((SH2,), jnp.float32), 'sW3': jax.random.normal(ks[3], (SH2, OUT), jnp.float32) * s, 'sb3': jnp.zeros((OUT,), jnp.float32), 'eW1': jax.random.normal(ks[4], (E, IN, EH1), jnp.float32) * s, 'eb1': jnp.zeros((E, EH1), jnp.float32), 'eW2': jax.random.normal(ks[5], (E, EH1, EH2), jnp.float32) * s, 'eb2': jnp.zeros((E, EH2), jnp.float32), 'eW3': jax.random.normal(ks[6], (E, EH2, OUT), jnp.float32) * s, 'eb3': jnp.zeros((E, OUT), jnp.float32), 'gW': jax.random.normal(ks[7], (IN, E), jnp.float32) * s, 'gb': jnp.zeros((E,), jnp.float32)}
    _L0_ffn_all = _L0_ffn_setup()
    _L0_ffn_in = {k: v for k, v in _L0_ffn_all.items() if k in ('sW1', 'sb1', 'sW2', 'sb2', 'sW3', 'sb3', 'eW1', 'eb1', 'eW2', 'eb2', 'eW3', 'eb3', 'gW', 'gb')}
    del _L0_ffn_all

    def _L1_gnn_setup():
        import jax, jax.numpy as jnp
        import numpy as np
        N_NODES = 6250
        N_EDGES = 100000
        IN_FEATS = 256
        HID = 64
        HEADS = 4
        OUT = 64

        def _gat_layer(x, src, dst, W, a_s, a_d, b, num_nodes):
            H, F = a_s.shape
            h = (x @ W).reshape(num_nodes, H, F)
            al_s = jnp.einsum('nhf,hf->nh', h, a_s)
            al_d = jnp.einsum('nhf,hf->nh', h, a_d)
            e = jax.nn.leaky_relu(al_s[src] + al_d[dst], 0.2)
            emax = jax.ops.segment_max(e, dst, num_segments=num_nodes)
            emax = jnp.where(jnp.isfinite(emax), emax, 0.0)
            ee = jnp.exp(e - emax[dst])
            denom = jax.ops.segment_sum(ee, dst, num_segments=num_nodes)
            alpha = ee / (denom[dst] + 1e-16)
            out = jax.ops.segment_sum(alpha[:, :, None] * h[src], dst, num_segments=num_nodes)
            return out.reshape(num_nodes, H * F) + b
        key = jax.random.key(seed)
        ks = jax.random.split(key, 16)
        p = lambda k, shape: jax.random.normal(k, shape, dtype=jnp.float32) * 0.05
        return {'x': jax.random.normal(ks[0], (N_NODES, IN_FEATS), dtype=jnp.float32), 'edge_index': jax.random.randint(ks[1], (2, N_EDGES), 0, N_NODES), 'W0': p(ks[2], (IN_FEATS, HEADS * HID)), 'as0': p(ks[3], (HEADS, HID)), 'ad0': p(ks[4], (HEADS, HID)), 'b0': jnp.zeros((HEADS * HID,), jnp.float32), 'W1': p(ks[5], (HEADS * HID, HEADS * HID)), 'as1': p(ks[6], (HEADS, HID)), 'ad1': p(ks[7], (HEADS, HID)), 'b1': jnp.zeros((HEADS * HID,), jnp.float32), 'W2': p(ks[8], (HEADS * HID, HEADS * OUT)), 'as2': p(ks[9], (HEADS, OUT)), 'ad2': p(ks[10], (HEADS, OUT)), 'b2': jnp.zeros((HEADS * OUT,), jnp.float32)}
    _L1_gnn_all = _L1_gnn_setup()
    _L1_gnn_in = {k: v for k, v in _L1_gnn_all.items() if k in ('W0', 'as0', 'ad0', 'b0', 'W1', 'as1', 'ad1', 'b1', 'W2', 'as2', 'ad2', 'b2')}
    del _L1_gnn_all

    def _L1_ffn_setup():
        import jax, jax.numpy as jnp
        import numpy as np
        TOP_K = 2
        LN_EPS = 1e-05
        key = jax.random.key(seed)
        ks = jax.random.split(key, 8)
        B, S, D, E, H = (16, 1024, 256, 8, 1024)
        x = jax.random.normal(ks[0], (B, S, D), dtype=jnp.float32)
        Wr = jax.random.normal(ks[1], (D, E), dtype=jnp.float32) * 0.1
        br = jnp.zeros((E,), dtype=jnp.float32)
        ln_g = jnp.ones((E, D), dtype=jnp.float32)
        ln_b = jnp.zeros((E, D), dtype=jnp.float32)
        W1 = jax.random.normal(ks[2], (E, D, H), dtype=jnp.float32) * (1.0 / np.sqrt(D))
        b1 = jnp.zeros((E, H), dtype=jnp.float32)
        W2 = jax.random.normal(ks[3], (E, H, D), dtype=jnp.float32) * (1.0 / np.sqrt(H))
        b2 = jnp.zeros((E, D), dtype=jnp.float32)
        return {'x': x, 'Wr': Wr, 'br': br, 'ln_g': ln_g, 'ln_b': ln_b, 'W1': W1, 'b1': b1, 'W2': W2, 'b2': b2}
    _L1_ffn_all = _L1_ffn_setup()
    _L1_ffn_in = {k: v for k, v in _L1_ffn_all.items() if k in ('Wr', 'br', 'ln_g', 'ln_b', 'W1', 'b1', 'W2', 'b2')}
    del _L1_ffn_all
    return {'x': x, 'src': src, 'dst': dst, 'L0_gnn_W1': _L0_gnn_in['W1'], 'L0_gnn_b1': _L0_gnn_in['b1'], 'L0_gnn_W2': _L0_gnn_in['W2'], 'L0_gnn_b2': _L0_gnn_in['b2'], 'L0_gnn_fc1_w': _L0_gnn_in['fc1_w'], 'L0_gnn_fc1_b': _L0_gnn_in['fc1_b'], 'L0_gnn_fc2_w': _L0_gnn_in['fc2_w'], 'L0_gnn_fc2_b': _L0_gnn_in['fc2_b'], 'L0_ffn_sW1': _L0_ffn_in['sW1'], 'L0_ffn_sb1': _L0_ffn_in['sb1'], 'L0_ffn_sW2': _L0_ffn_in['sW2'], 'L0_ffn_sb2': _L0_ffn_in['sb2'], 'L0_ffn_sW3': _L0_ffn_in['sW3'], 'L0_ffn_sb3': _L0_ffn_in['sb3'], 'L0_ffn_eW1': _L0_ffn_in['eW1'], 'L0_ffn_eb1': _L0_ffn_in['eb1'], 'L0_ffn_eW2': _L0_ffn_in['eW2'], 'L0_ffn_eb2': _L0_ffn_in['eb2'], 'L0_ffn_eW3': _L0_ffn_in['eW3'], 'L0_ffn_eb3': _L0_ffn_in['eb3'], 'L0_ffn_gW': _L0_ffn_in['gW'], 'L0_ffn_gb': _L0_ffn_in['gb'], 'L1_gnn_W0': _L1_gnn_in['W0'], 'L1_gnn_as0': _L1_gnn_in['as0'], 'L1_gnn_ad0': _L1_gnn_in['ad0'], 'L1_gnn_b0': _L1_gnn_in['b0'], 'L1_gnn_W1': _L1_gnn_in['W1'], 'L1_gnn_as1': _L1_gnn_in['as1'], 'L1_gnn_ad1': _L1_gnn_in['ad1'], 'L1_gnn_b1': _L1_gnn_in['b1'], 'L1_gnn_W2': _L1_gnn_in['W2'], 'L1_gnn_as2': _L1_gnn_in['as2'], 'L1_gnn_ad2': _L1_gnn_in['ad2'], 'L1_gnn_b2': _L1_gnn_in['b2'], 'L1_ffn_Wr': _L1_ffn_in['Wr'], 'L1_ffn_br': _L1_ffn_in['br'], 'L1_ffn_ln_g': _L1_ffn_in['ln_g'], 'L1_ffn_ln_b': _L1_ffn_in['ln_b'], 'L1_ffn_W1': _L1_ffn_in['W1'], 'L1_ffn_b1': _L1_ffn_in['b1'], 'L1_ffn_W2': _L1_ffn_in['W2'], 'L1_ffn_b2': _L1_ffn_in['b2']}

def reference(x, src, dst, L0_gnn_W1, L0_gnn_b1, L0_gnn_W2, L0_gnn_b2, L0_gnn_fc1_w, L0_gnn_fc1_b, L0_gnn_fc2_w, L0_gnn_fc2_b, L0_ffn_sW1, L0_ffn_sb1, L0_ffn_sW2, L0_ffn_sb2, L0_ffn_sW3, L0_ffn_sb3, L0_ffn_eW1, L0_ffn_eb1, L0_ffn_eW2, L0_ffn_eb2, L0_ffn_eW3, L0_ffn_eb3, L0_ffn_gW, L0_ffn_gb, L1_gnn_W0, L1_gnn_as0, L1_gnn_ad0, L1_gnn_b0, L1_gnn_W1, L1_gnn_as1, L1_gnn_ad1, L1_gnn_b1, L1_gnn_W2, L1_gnn_as2, L1_gnn_ad2, L1_gnn_b2, L1_ffn_Wr, L1_ffn_br, L1_ffn_ln_g, L1_ffn_ln_b, L1_ffn_W1, L1_ffn_b1, L1_ffn_W2, L1_ffn_b2):
    import jax
    import jax.numpy as jnp

    def _L0_gnn_ref(x, edge_index, W1, b1, W2, b2, fc1_w, fc1_b, fc2_w, fc2_b):
        import jax, jax.numpy as jnp
        import numpy as np
        N_NODES = 6250

        def gcn_conv(x, src, dst, W, b):
            N = x.shape[0]
            h = x @ W
            ones = jnp.ones(dst.shape, dtype=h.dtype)
            deg = jax.ops.segment_sum(ones, dst, num_segments=N) + 1.0
            dinv = jax.lax.rsqrt(deg)
            norm = dinv[src] * dinv[dst]
            agg = jax.ops.segment_sum(h[src] * norm[:, None], dst, num_segments=N)
            agg = agg + h * (dinv * dinv)[:, None]
            return agg + b
        src, dst = (edge_index[0], edge_index[1])
        h = jax.nn.relu(gcn_conv(x, src, dst, W1, b1))
        h = jax.nn.relu(gcn_conv(h, src, dst, W2, b2))
        h = h @ fc1_w + fc1_b
        h = h @ fc2_w + fc2_b
        return h

    def _L0_ffn_ref(x, sW1, sb1, sW2, sb2, sW3, sb3, eW1, eb1, eW2, eb2, eW3, eb3, gW, gb):
        import jax, jax.numpy as jnp
        import numpy as np
        B, A = (512, 8)
        IN, OUT = (256, 256)
        SH1, SH2 = (256, 128)
        EH1, EH2 = (128, 64)
        E, TOPK = (4, 2)

        def _shared_mlp(x, W1, b1, W2, b2, W3, b3):
            h = jax.nn.relu(x @ W1 + b1)
            h = jax.nn.relu(h @ W2 + b2)
            return h @ W3 + b3

        def _experts_mlp(x, eW1, eb1, eW2, eb2, eW3, eb3):
            h = jax.nn.relu(jnp.einsum('baf,efh->ebah', x, eW1) + eb1[:, None, None, :])
            h = jax.nn.relu(jnp.einsum('ebah,ehg->ebag', h, eW2) + eb2[:, None, None, :])
            o = jnp.einsum('ebag,ego->ebao', h, eW3) + eb3[:, None, None, :]
            return jnp.moveaxis(o, 0, -1)
        all_out = _experts_mlp(x, eW1, eb1, eW2, eb2, eW3, eb3)
        shared = _shared_mlp(x, sW1, sb1, sW2, sb2, sW3, sb3)
        gates = jax.nn.softmax(x @ gW + gb, axis=-1)
        topv, topi = jax.lax.top_k(gates, TOPK)
        topw = jax.nn.softmax(topv, axis=-1)
        sel = jnp.take_along_axis(all_out, topi[:, :, None, :], axis=-1)
        gated = jnp.sum(sel * topw[:, :, None, :], axis=-1)
        return shared + gated

    def _L1_gnn_ref(x, edge_index, W0, as0, ad0, b0, W1, as1, ad1, b1, W2, as2, ad2, b2):
        import jax, jax.numpy as jnp
        import numpy as np
        N_NODES = 6250
        N_EDGES = 100000
        IN_FEATS = 256
        HID = 64
        HEADS = 4
        OUT = 64

        def _gat_layer(x, src, dst, W, a_s, a_d, b, num_nodes):
            H, F = a_s.shape
            h = (x @ W).reshape(num_nodes, H, F)
            al_s = jnp.einsum('nhf,hf->nh', h, a_s)
            al_d = jnp.einsum('nhf,hf->nh', h, a_d)
            e = jax.nn.leaky_relu(al_s[src] + al_d[dst], 0.2)
            emax = jax.ops.segment_max(e, dst, num_segments=num_nodes)
            emax = jnp.where(jnp.isfinite(emax), emax, 0.0)
            ee = jnp.exp(e - emax[dst])
            denom = jax.ops.segment_sum(ee, dst, num_segments=num_nodes)
            alpha = ee / (denom[dst] + 1e-16)
            out = jax.ops.segment_sum(alpha[:, :, None] * h[src], dst, num_segments=num_nodes)
            return out.reshape(num_nodes, H * F) + b
        n = x.shape[0]
        loop = jnp.arange(n, dtype=edge_index.dtype)
        src = jnp.concatenate([edge_index[0], loop])
        dst = jnp.concatenate([edge_index[1], loop])
        h = _gat_layer(x, src, dst, W0, as0, ad0, b0, n)
        h = _gat_layer(h, src, dst, W1, as1, ad1, b1, n)
        h = _gat_layer(h, src, dst, W2, as2, ad2, b2, n)
        return h

    def _L1_ffn_ref(x, Wr, br, ln_g, ln_b, W1, b1, W2, b2):
        import jax, jax.numpy as jnp
        import numpy as np
        TOP_K = 2
        LN_EPS = 1e-05
        B, S, D = x.shape
        N = B * S
        xt = x.reshape(N, D)
        logits = xt @ Wr + br
        probs = jax.nn.softmax(logits, axis=-1)
        top_p, top_idx = jax.lax.top_k(probs, TOP_K)
        weights = top_p / top_p.sum(axis=-1, keepdims=True)
        mu = xt.mean(axis=-1, keepdims=True)
        var = ((xt - mu) ** 2).mean(axis=-1, keepdims=True)
        xn = (xt - mu) * jax.lax.rsqrt(var + LN_EPS)
        xe = xn[None, :, :] * ln_g[:, None, :] + ln_b[:, None, :]
        h = jax.nn.gelu(jnp.einsum('end,edh->enh', xe, W1) + b1[:, None, :], approximate=False)
        y = jnp.einsum('enh,ehd->end', h, W2) + b2[:, None, :]
        y_tok = jnp.transpose(y, (1, 0, 2))
        sel = jnp.take_along_axis(y_tok, top_idx[:, :, None], axis=1)
        out = (weights[:, :, None] * sel).sum(axis=1)
        return out.reshape(B, S, D)
    edge_index = jnp.stack([src, dst])
    x = x + _L0_gnn_ref(_layernorm(x, axis=-1), edge_index, L0_gnn_W1, L0_gnn_b1, L0_gnn_W2, L0_gnn_b2, L0_gnn_fc1_w, L0_gnn_fc1_b, L0_gnn_fc2_w, L0_gnn_fc2_b)
    x = x + _L0_ffn_ref(_layernorm(x, axis=-1)[None], L0_ffn_sW1, L0_ffn_sb1, L0_ffn_sW2, L0_ffn_sb2, L0_ffn_sW3, L0_ffn_sb3, L0_ffn_eW1, L0_ffn_eb1, L0_ffn_eW2, L0_ffn_eb2, L0_ffn_eW3, L0_ffn_eb3, L0_ffn_gW, L0_ffn_gb)[0]
    x = x + _L1_gnn_ref(_layernorm(x, axis=-1), edge_index, L1_gnn_W0, L1_gnn_as0, L1_gnn_ad0, L1_gnn_b0, L1_gnn_W1, L1_gnn_as1, L1_gnn_ad1, L1_gnn_b1, L1_gnn_W2, L1_gnn_as2, L1_gnn_ad2, L1_gnn_b2)
    x = x + _L1_ffn_ref(_layernorm(x, axis=-1)[None], L1_ffn_Wr, L1_ffn_br, L1_ffn_ln_g, L1_ffn_ln_b, L1_ffn_W1, L1_ffn_b1, L1_ffn_W2, L1_ffn_b2)[0]
    return x

_drawn_inputs = setup_inputs


def setup_inputs(seed=0):
    import zlib

    import numpy as np

    out = dict(_drawn_inputs(seed))
    spreads = {'L0_gnn_b1': (0.0, 0.1),
     'L0_gnn_b2': (0.0, 0.1),
     'L0_gnn_fc1_b': (0.0, 0.1),
     'L0_gnn_fc2_b': (0.0, 0.1),
     'L0_ffn_sb1': (0.0, 0.1),
     'L0_ffn_sb2': (0.0, 0.1),
     'L0_ffn_sb3': (0.0, 0.1),
     'L0_ffn_eb1': (0.0, 0.355),
     'L0_ffn_eb2': (0.0, 0.1),
     'L0_ffn_eb3': (0.0, 0.1),
     'L0_ffn_gb': (0.0, 0.1),
     'L1_gnn_b0': (0.0, 0.1),
     'L1_gnn_b1': (0.0, 0.1),
     'L1_gnn_b2': (0.0, 0.1),
     'L1_ffn_br': (0.0, 0.1),
     'L1_ffn_ln_g': (1.0, 0.2),
     'L1_ffn_ln_b': (0.0, 0.1),
     'L1_ffn_b1': (0.0, 0.1),
     'L1_ffn_b2': (0.0, 0.1)}
    factors = {'L1_gnn_ad0': 48.336,
     'L1_gnn_as1': 25.629,
     'L1_gnn_ad1': 47.35,
     'L1_gnn_as2': 47.638,
     'L1_gnn_ad2': 64.0}
    for name, (base, spread) in spreads.items():
        noise = np.random.default_rng([zlib.crc32(name.encode()), seed]).standard_normal(out[name].shape)
        drawn = base * np.exp(spread * noise) if base else spread * noise
        out[name] = jnp.asarray(drawn.astype(out[name].dtype))
    for name, factor in factors.items():
        out[name] = (out[name] * factor).astype(out[name].dtype)
    return out
```

```python
from contextlib import ExitStack

import numpy as np

import concourse.bass as bass
from concourse import mybir
from concourse.alu_op_type import AluOpType as ALU

P = 128
N = 6250
E = 100000
D = 256
NT = (N + P - 1) // P
NP = NT * P
KT = (E + P - 1) // P
KC = (KT + P - 1) // P
KP = KC * P
NI = KT + NT - 1
HALF = 8
STEPS = -(-NI // (2 * HALF)) * 2
NIP = STEPS * HALF
IC = NIP // 2
PAD_DST = 8191
BIG = 1.0e30
BT = 7
NB = NT // BT
BN = BT * P
HB = BN // 2
HEADS, HID = 4, 64
GW = D + HEADS
MW = D + 2 * HEADS
LN_EPS = 1e-5

F32 = mybir.dt.float32
BF16 = mybir.dt.bfloat16
I32 = mybir.dt.int32
ACT = mybir.ActivationFunctionType
AX = mybir.AxisListType.X
assert NT % BT == 0 and IC <= 512 and HB <= 512 and STEPS % 2 == 0


class Chain:

    def __init__(self, eng, sem):
        self.eng, self.sem, self.base, self.n = eng, sem, 0, 0

    def mark(self, ins):
        self.n += 1
        ins.then_inc(self.sem, 1)
        return ins

    def wait(self):
        self.eng.wait_ge(self.sem, self.base + self.n)

    def link(self, ins):
        self.mark(ins)
        self.wait()

    def enter(self, i, per_turn):
        self.before, self.per_turn = self.base + self.n, per_turn
        self.base, self.n = self.before + i * per_turn, 0

    def leave(self, turns):
        assert self.n == self.per_turn, (self.n, self.per_turn)
        self.base, self.n = self.before + turns * self.per_turn, 0


class Ring:

    def __init__(self, full, empty, banks, per_turn):
        self.full, self.empty, self.banks, self.per_turn = full, empty, banks, per_turn
        self.fill_n = self.drain_n = 0

    def give_credit(self, eng):
        eng.sem_inc(self.empty, self.per_turn)

    def fill(self, pe, i):
        u, r = self.fill_n % self.per_turn, len(self.banks)
        last = u - r + self.per_turn if u >= r else max(
            (v for v in range(self.per_turn) if v % r == u % r), default=u)
        pe.wait_ge(self.empty, i * self.per_turn + last + 1)
        self.fill_n += 1
        return self.banks[u % r]

    def settle(self, eng, i):
        eng.wait_ge(self.empty, (i + 1) * self.per_turn + (self.drain_n - 1) % self.per_turn + 1)

    def drain(self, eng, i):
        u = self.drain_n % self.per_turn
        eng.wait_ge(self.full, i * self.per_turn + u + 1)
        self.drain_n += 1
        return self.banks[u % len(self.banks)]


def refine_rsqrt(ch, dve, y, v, tmp):
    ch.link(dve.tensor_tensor(tmp, y, y, ALU.mult))
    ch.link(dve.scalar_tensor_tensor(out=tmp, in0=tmp, scalar=-0.5, in1=v, op0=ALU.mult, op1=ALU.mult))
    ch.link(dve.scalar_tensor_tensor(out=y, in0=tmp, scalar=1.5, in1=y, op0=ALU.add, op1=ALU.mult))


class Net:
    pass


def over(ap, n):
    ap = ap.unsqueeze(len(ap.shape))
    return ap.broadcast_to(list(ap.shape[:-1]) + [n])


def mid(ap, n):
    ap = ap.unsqueeze(1)
    return ap.broadcast_to([ap.shape[0], n, ap.shape[2]])


class Stage:

    def __init__(self, nc, name):
        self.nc, self.name, self.ctx, self.sems = nc, name, ExitStack(), []

    def __enter__(self):
        return self

    def __exit__(self, *a):
        self.nc.clear_and_free_semaphores(self.sems)
        self.nc.all_engine_barrier()
        self.ctx.close()

    def sb(self, name, shape, dt=F32):
        return self.ctx.enter_context(self.nc.sbuf_tensor(f"{self.name}_{name}", shape, dt))

    def ps(self, name, shape, dt=F32):
        return self.ctx.enter_context(self.nc.psum_tensor(f"{self.name}_{name}", shape, dt))

    def banks(self, n, name="bank"):
        return [self.ps(f"{name}{i}", [P, 512]) for i in range(n)]

    def sem(self, name):
        self.sems.append(self.nc.alloc_semaphore(f"{self.name}_{name}"))
        return self.sems[-1]


def make_constants(nc, net):
    with Stage(nc, "const") as st:
        made = st.sem("made")
        with nc.Block() as block:
            @block.gpsimd
            def _(pool):
                pool.iota(net.iota[:], [[1, P]], base=0, channel_multiplier=0,
                          allow_small_or_imprecise_dtypes=True)
                pool.iota(net.part[:], [[P, KC]], base=0, channel_multiplier=1,
                          allow_small_or_imprecise_dtypes=True)
                pool.memset(net.ones[:], 1.0)
                pool.memset(net.ident[:], 0.0).then_inc(made, 1)
                pool.wait_ge(made, 1)
                pool.affine_select(out=net.ident[:], in_=net.ident[:], compare_op=ALU.not_equal, fill=1.0,
                                   base=0, pattern=[[-1, P]], channel_multiplier=1)


def load_edges(dst_of, src):
    whole = E // (P * P)
    yield dst_of[:, 0:whole, :], src[0:whole * P * P].rearrange("(c p e) -> p c e", p=P, e=P)
    rows = (E - whole * P * P) // P
    yield dst_of[0:rows, whole, :], src[whole * P * P:(whole * P + rows) * P].rearrange("(p e) -> p e", e=P)
    at, left = (whole * P + rows) * P, E % P
    yield dst_of[rows:rows + 1, whole, 0:left], src[at:at + left].rearrange("(p e) -> p e", p=1)


def prepare_edges(nc, net, src, dst):
    whole = E // (P * P)
    with Stage(nc, "edges") as st:
        src_i, dst_i = st.sb("src_i", [P, KC, P], I32), st.sb("dst_i", [P, KC, P], I32)
        prev_i, next_i = st.sb("prev_i", [P, KC, P], I32), st.sb("next_i", [P, KC, P], I32)
        low_i = st.sb("low_i", [P, KC, P], I32)
        src_f, dst_f = st.sb("src_f", [P, KC, P]), st.sb("dst_f", [P, KC, P])
        first_f = st.sb("first_f", [P, KC, P])
        hi_f, lo_f = st.sb("hi_f", [P, KC, P]), st.sb("lo_f", [P, KC, P])
        hi_t, lo_t = st.sb("hi_t", [P, KP]), st.sb("lo_t", [P, KP])
        d0, d127 = st.sb("d0", [HEADS, KP], I32), st.sb("d127", [HEADS, KP], I32)
        whole_run, link = st.sb("whole_run", [HEADS, KP]), st.sb("link", [HEADS, KP])
        one_hi, one_lo = st.sb("one_hi", [P, 2, HALF, NT], BF16), st.sb("one_lo", [P, 2, HALF, P], BF16)
        zero = st.sb("zero", [P, P], BF16)
        count, per_tile = st.sb("count", [P, NT]), st.sb("per_tile", [P, 1])
        degree, spare = st.sb("degree", [P, NT]), st.sb("spare", [P, NT])
        below = st.sb("below", [P, P])
        kf_i, kf, first_item = st.sb("kf_i", [P, 1], I32), st.sb("kf", [P, 1]), st.sb("first_item", [P, 1])
        iota_i, begun = st.sb("iota_i", [P, NIP]), st.sb("begun", [NT, NIP])
        item_f = st.sb("item_f", [P, KC, NIP])
        t_all, k_all = st.sb("t_all", [P, NIP]), st.sb("k_all", [P, NIP])
        bank = st.banks(8)
        padded, loaded, rows = st.sem("padded"), st.sem("loaded"), st.sem("rows")
        ready, turned, copied = st.sem("ready"), st.sem("turned"), st.sem("copied")
        onehot, counted, chain, root = st.sem("onehot"), st.sem("counted"), st.sem("chain"), st.sem("root")
        pe_done, rooted = st.sem("pe_done"), st.sem("rooted")

        with nc.allow_non_contiguous_dma(reason="a few columns, once"), nc.Block() as block:
            @block.gpsimd
            def _(pool):
                pool.iota(iota_i[:], [[1, NIP]], base=0, channel_multiplier=0,
                          allow_small_or_imprecise_dtypes=True).then_inc(padded, 1)
                for t, v in ((src_i, 0), (dst_i, PAD_DST), (prev_i, PAD_DST), (next_i, PAD_DST),
                             (d0, PAD_DST), (d127, PAD_DST)):
                    pool.memset(t[:], v).then_inc(padded, 1)
                pool.memset(zero[:], 0.0).then_inc(padded, 1)

            @block.sync
            def _(sp):
                sp.wait_ge(padded, 7)
                n = 0
                for t, a in ((src_i, src), (dst_i, dst)):
                    for o, i in load_edges(t, a):
                        sp.dma_start(o, i).then_inc(loaded, 16)
                        n += 1
                sp.dma_start(d0[:, 0:KT], dst_column(dst, 0, KT)).then_inc(loaded, 16)
                sp.dma_start(d127[:, 0:E // P], dst_column(dst, P - 1, E // P)).then_inc(loaded, 16)
                sp.wait_ge(loaded, 16 * (n + 2))
                sp.dma_start(next_i[:, :, 0:P - 1], dst_i[:, :, 1:P]).then_inc(rows, 16)
                sp.dma_start(prev_i[:, :, 1:P], dst_i[:, :, 0:P - 1]).then_inc(rows, 16)
                sp.dma_start(prev_i[1:P, 0, 0:1], dst[0:(P - 1) * P].rearrange("(p e) -> p e", e=P)[:, P - 1:P])\
                    .then_inc(rows, 16)
                for c in range(1, KC):
                    n = min(P, KT - c * P)
                    sp.dma_start(prev_i[0:n, c, 0:1], bass.AP(dst.tensor, c * P * P - 1, [[P, n], [1, 1]]))\
                        .then_inc(rows, 16)

            @block.vector
            def _(dve):
                ch = Chain(dve, chain)
                dve.wait_ge(loaded, 16 * 8)
                dve.wait_ge(padded, 8)
                ch.link(dve.tensor_scalar(low_i[:], dst_i[:], 7, None, ALU.arith_shift_right))
                ch.link(dve.tensor_copy(hi_f[:], low_i[:]))
                ch.link(dve.tensor_scalar(low_i[:], dst_i[:], 127, None, ALU.bitwise_and))
                ch.link(dve.tensor_copy(lo_f[:], low_i[:]))
                ch.mark(dve.tensor_copy(dst_f[:], dst_i[:]))
                dve.tensor_copy(src_f[:], src_i[:]).then_inc(ready, 1)
                dve.wait_ge(ready, 1)
                for c in range(3 * KC):
                    dve.wait_ge(turned, c + 1)
                    t = (hi_t, lo_t, net.src_col)[c // KC]
                    dve.tensor_copy(t[:, c % KC * P:(c % KC + 1) * P], bank[c % 8][:, 0:P]).then_inc(copied, 1)
                dve.wait_ge(copied, 3 * KC)
                def one_hots(i, h, col):
                    dve.tensor_tensor(one_hi[:, h], over(hi_t[:, col], NT), mid(net.iota[:, 0:NT], HALF),
                                      ALU.is_equal)
                    dve.tensor_tensor(one_lo[:, h], over(lo_t[:, col], P), mid(net.iota[:], HALF),
                                      ALU.is_equal).then_inc(onehot, 1)

                for h in range(2):
                    one_hots(0, h, slice(h * HALF, (h + 1) * HALF))
                with dve.Fori(1, KT // (2 * HALF) + 1) as i:
                    for h in range(2):
                        dve.wait_ge(counted, 2 * i - 1 + h)
                        one_hots(i, h, bass.ds(i * (2 * HALF) + h * HALF, HALF))
                dve.wait_ge(pe_done, 1)
                ch.link(dve.tensor_copy(count[:], bank[0][:, 0:NT]))
                ch.link(dve.tensor_scalar(net.has_edge[:], count[:], 0.0, None, ALU.is_gt))
                ch.link(dve.tensor_scalar(degree[:], count[:], 1.0, None, ALU.add))
                ch.link(dve.reciprocal(net.dinv[:], degree[:]))
                dve.tensor_scalar(below[:], net.iota[:], net.part[:, 0:1], None, ALU.is_gt).then_inc(root, 1)
                dve.wait_ge(rooted, 1)
                refine_rsqrt(ch, dve, net.dinv[:], degree[:], spare[:])
                dve.wait_ge(pe_done, 2)
                dve.tensor_copy(per_tile[0:NT, :], bank[1][0:NT, 0:1]).then_inc(root, 1)
                dve.wait_ge(pe_done, 3)
                ch.link(dve.tensor_copy(kf_i[:], bank[2][:, 0:1]))
                ch.link(dve.tensor_scalar(kf_i[:], kf_i[:], 7, None, ALU.arith_shift_right))
                ch.link(dve.tensor_copy(kf[:], kf_i[:]))
                ch.link(dve.tensor_scalar(first_item[:], kf[:], float(KT - 1), net.part[:, 0:1], ALU.min, ALU.add))
                dve.tensor_scalar(begun[:], iota_i[0:NT, :], first_item[0:NT, 0:1], None, ALU.is_ge)\
                    .then_inc(root, 1)
                dve.wait_ge(pe_done, 4)
                for s in range(2):
                    ch.link(dve.tensor_scalar(t_all[:, s * IC:(s + 1) * IC], bank[3 + s][:, 0:IC], -1.0, None,
                                              ALU.add))
                ch.mark(dve.tensor_copy(net.t_of[:, 0:NIP], t_all[0:1, :]))
                ch.mark(dve.memset(net.t_of[:, NIP:NIP + HALF], NT - 1))
                ch.mark(dve.memset(net.dloc[:, NIP:NIP + HALF], -1.0))
                ch.link(dve.tensor_tensor(k_all[:], iota_i[:], t_all[:], ALU.subtract))
                dve.wait_ge(rows, 16 * (3 + KC - 1))
                ch.link(dve.tensor_tensor(first_f[:], dst_i[:], prev_i[:], ALU.not_equal))
                for c in range(KC):
                    last = dve.tensor_scalar(item_f[:, c, :], k_all[:], net.part[:, c:c + 1], None,
                                             ALU.is_equal)
                last.then_inc(root, 1)
                dve.wait_ge(root, 4)
                ch.mark(dve.tensor_copy(net.item_of[:], item_f[:]))
                ch.link(dve.tensor_scalar(net.run_start[:], first_f[:], -BIG, None, ALU.mult))
                ch.mark(dve.memset(net.run_start[:, :, 0:1], -BIG))
                ch.link(dve.tensor_tensor(net.run_end[:], dst_i[:], next_i[:], ALU.not_equal))
                ch.link(dve.tensor_scalar(net.run_end[:], net.run_end[:], -BIG, None, ALU.mult))
                ch.mark(dve.memset(net.run_end[:, :, P - 1:P], -BIG))
                for m, at in ((net.not_first_run, 0), (net.not_last_run, P - 1)):
                    ch.link(dve.tensor_tensor(m[:], dst_f[:], dst_f[:, :, at:at + 1].broadcast_to([P, KC, P]),
                                              ALU.not_equal))
                    ch.mark(dve.tensor_scalar(m[:], m[:], -BIG, None, ALU.mult))
                ch.link(dve.tensor_tensor(whole_run[:], d0[:], d127[:], ALU.not_equal))
                ch.link(dve.tensor_scalar(whole_run[:], whole_run[:], -BIG, None, ALU.mult))
                ch.link(dve.tensor_tensor(link[:, 1:KP], d0[:, 1:KP], d127[:, 0:KP - 1], ALU.not_equal))
                ch.link(dve.tensor_scalar(net.link_left[:, 1:KP], link[:, 1:KP], -BIG, None, ALU.mult))
                ch.mark(dve.tensor_scalar(net.link_right[:, 0:KP - 1], link[:, 1:KP], -BIG, None, ALU.mult))
                ch.mark(dve.memset(net.link_left[:, 0:1], -BIG))
                ch.mark(dve.memset(net.link_right[:, KP - 1:KP], -BIG))
                ch.mark(dve.memset(net.pass_left[:, 0:1], -BIG))
                ch.link(dve.memset(net.pass_right[:, KP - 1:KP], -BIG))
                ch.link(dve.tensor_tensor(net.pass_left[:, 1:KP], whole_run[:, 0:KP - 1],
                                          net.link_left[:, 1:KP], ALU.min))
                ch.link(dve.tensor_tensor(net.pass_right[:, 0:KP - 1], whole_run[:, 1:KP],
                                          net.link_right[:, 0:KP - 1], ALU.min))
                for n in range(6):
                    what, s = n // 2, n % 2
                    cols = slice(s * IC, (s + 1) * IC)
                    dve.wait_ge(pe_done, 5 + n)
                    b = bank[n % 8][:, 0:IC]
                    if what == 0:
                        ch.mark(dve.tensor_copy(net.src_of[:, cols], b))
                    elif what == 1:
                        ch.mark(dve.scalar_tensor_tensor(out=net.dloc[:, cols], in0=t_all[:, cols],
                                                         scalar=-float(P), in1=b, op0=ALU.mult, op1=ALU.add))
                    else:
                        ch.mark(dve.tensor_copy(net.first_of[:, cols], b))
                ch.wait()

            @block.scalar
            def _(act):
                act.wait_ge(root, 1)
                act.activation(net.dinv[:], net.dinv[:], ACT.Sqrt).then_inc(rooted, 1)

            @block.tensor
            def _(pe):
                pe.wait_ge(ready, 1)
                for c in range(3 * KC):
                    if c >= 8:
                        pe.wait_ge(copied, c - 7)
                    pe.transpose(bank[c % 8][:, 0:P], (hi_f, lo_f, src_f)[c // KC][:, c % KC, :], net.ident[:])\
                        .then_inc(turned, 1)
                pe.wait_ge(padded, 8)
                pe.wait_ge(copied, 3 * KC)
                counts = bank[0][:, 0:NT]
                pe.matmul(counts, zero[:], zero[:, 0:NT], start=True, stop=False, skip_group_check=True)
                with pe.Fori(0, KT // (2 * HALF) + 1) as i:
                    for h in range(2):
                        pe.wait_ge(onehot, 2 * i + h + 1)
                        for j in range(HALF):
                            mm = pe.matmul(counts, one_lo[:, h, j, :], one_hi[:, h, j, :], start=False,
                                           stop=False, skip_group_check=True)
                        mm.then_inc(counted, 1)
                pe.matmul(counts, zero[:], zero[:, 0:NT], start=False, stop=True, skip_group_check=True)\
                    .then_inc(pe_done, 1)
                pe.wait_ge(root, 1)
                pe.matmul(bank[1][0:NT, 0:1], count[:], net.ones[:, 0:1], start=True, stop=True)\
                    .then_inc(pe_done, 1)
                pe.wait_ge(root, 2)
                pe.matmul(bank[2][:, 0:1], below[0:NT, :], per_tile[0:NT, :], start=True, stop=True)\
                    .then_inc(pe_done, 1)
                pe.wait_ge(root, 3)
                for s in range(2):
                    mm = pe.matmul(bank[3 + s][:, 0:IC], net.ones[0:NT, :], begun[:, s * IC:(s + 1) * IC],
                                   start=True, stop=True)
                mm.then_inc(pe_done, 1)
                pe.wait_ge(root, 4)
                for n in range(6):
                    rows_of, s = (src_f, dst_f, first_f)[n // 2], n % 2
                    for c in range(KC):
                        mm = pe.matmul(bank[n][:, 0:IC], rows_of[:, c, :],
                                       item_f[:, c, s * IC:(s + 1) * IC], start=c == 0, stop=c == KC - 1)
                    mm.then_inc(pe_done, 1)


def dst_column(dst, at, n):
    return bass.AP(dst.tensor, dst.offset + at, [[0, HEADS], [P, n], [1, 1]])


def alloc_edges(nc, net, ctx):
    def sb(name, shape, dt=F32):
        return ctx.enter_context(nc.sbuf_tensor(name, shape, dt))

    net.has_edge = sb("has_edge", [P, NT])
    net.dinv = sb("dinv", [P, NT])
    net.src_col = sb("src_col", [P, KP], I32)
    net.src_of = sb("src_of", [P, NIP], I32)
    net.dloc = sb("dloc", [P, NIP + HALF])
    net.first_of = sb("first_of", [P, NIP], BF16)
    net.t_of = sb("t_of", [1, NIP + HALF], I32)
    net.item_of = sb("item_of", [P, KC, NIP], BF16)
    net.run_start = sb("run_start", [P, KC, P], BF16)
    net.run_end = sb("run_end", [P, KC, P], BF16)
    net.not_first_run = sb("not_first_run", [P, KC, P], BF16)
    net.not_last_run = sb("not_last_run", [P, KC, P], BF16)
    net.link_left = sb("link_left", [HEADS, KP], BF16)
    net.link_right = sb("link_right", [HEADS, KP], BF16)
    net.pass_left = sb("pass_left", [HEADS, KP], BF16)
    net.pass_right = sb("pass_right", [HEADS, KP], BF16)


def gather_items(pool, net, table, slots, width, index, gathered, indexed, go, freed, least):
    def turn(i, first):
        for h in range(2):
            if not first:
                pool.wait_ge(gathered[h], P * i)
                pool.wait_ge(freed, least(i * 2 + h))
            pool.tensor_copy(index[:, h, :], net.src_of[:, bass.ds(i * (2 * HALF) + h * HALF, HALF)])\
                .then_inc(indexed, 1)
            pool.wait_ge(indexed, i * 2 + h + 1)
            pool.sem_inc(go, 1)
            for j in range(HALF):
                pool.indirect_dma_start(slots[:, h, j, 0:width], None, table,
                                        bass.IndirectOffsetOnAxis(ap=index[:, h, j:j + 1], axis=0))\
                    .then_inc(gathered[h], 16)

    turn(0, True)
    with pool.Fori(1, STEPS // 2) as i:
        turn(i, False)


def gcn_pass(nc, net, name, table, width):
    with Stage(nc, name) as st:
        index = st.sb("index", [P, 2, HALF], I32)
        rows, onehot = st.sb("rows", [P, 2, HALF, width]), st.sb("onehot", [P, 2, HALF, P])
        bank = st.banks(HALF)
        gathered = [st.sem("gathered0"), st.sem("gathered1")]
        indexed, go, made, summed, added = (st.sem(x) for x in ("indexed", "go", "made", "summed", "added"))

        with nc.Block() as block:
            @block.gpsimd
            def _(pool):
                gather_items(pool, net, table, rows, width, index, gathered, indexed, go, summed,
                             lambda q: (q - 1) * HALF)

            @block.vector
            def _(dve):
                tile = [dve.alloc_register(f"{name}_t{j}") for j in range(HALF)]

                def one_hot(col, h):
                    dve.tensor_tensor(onehot[:, h], over(net.dloc[:, col], P), mid(net.iota[:], HALF),
                                      ALU.is_equal).then_inc(made, 1)

                def accumulate(q, first):
                    dve.load(tile, net.t_of[0:1, bass.ds(q * HALF, HALF)])
                    for j in range(HALF):
                        dve.wait_ge(summed, q * HALF + j + 1)
                        if not (first and j == 0):
                            dve.wait_ge(added, q * HALF + j)
                        acc = net.acc[:, bass.ds(dve.snap(tile[j], min_val=0, max_val=NT - 1) * MW, width)]
                        dve.tensor_tensor(acc, acc, bank[j][:, 0:width], ALU.add).then_inc(added, 1)

                one_hot(slice(0, HALF), 0)
                one_hot(slice(HALF, 2 * HALF), 1)
                accumulate(0, True)
                with dve.Fori(0, STEPS // 2 - 1) as i:
                    for h in range(2):
                        one_hot(bass.ds(i * (2 * HALF) + (2 + h) * HALF, HALF), h)
                        accumulate(i * 2 + h + 1, False)
                accumulate(STEPS - 1, False)

            @block.tensor
            def _(pe):
                def turn(i, first):
                    for h in range(2):
                        pe.wait_ge(made, i * 2 + h + 1)
                        pe.wait_ge(gathered[h], P * i + P)
                        for j in range(HALF):
                            if not first or h:
                                pe.wait_ge(added, (i * 2 + h - 1) * HALF + j + 1)
                            pe.matmul(bank[j][:, 0:width], onehot[:, h, j, :], rows[:, h, j, :],
                                      start=True, stop=True).then_inc(summed, 1)

                turn(0, True)
                with pe.Fori(1, STEPS // 2) as i:
                    turn(i, False)


def layer_stats(nc, net, name):
    with Stage(nc, name) as st:
        stats, aggr = st.sb("stats", [P, NT, 6]), st.sb("aggr", [P, NT, 2])
        var, spare = st.sb("var", [P, NT]), st.sb("spare", [P, NT])
        chain, ready, rooted = st.sem("chain"), st.sem("ready"), st.sem("rooted")
        with nc.Block() as block:
            @block.vector
            def _(dve):
                ch = Chain(dve, chain)
                for t in range(NT):
                    ch.mark(dve.bn_stats(stats[:, t, :], net.x[:, t * D:(t + 1) * D]))
                ch.wait()
                for t in range(NT):
                    ch.mark(dve.bn_aggr(aggr[:, t, :], stats[:, t, :]))
                ch.wait()
                ch.mark(dve.tensor_copy(net.mean[:], aggr[:, :, 0]))
                ch.link(dve.tensor_scalar(var[:], aggr[:, :, 1], LN_EPS, None, ALU.add))
                dve.reciprocal(net.rstd[:], var[:]).then_inc(ready, 1)
                dve.wait_ge(rooted, 1)
                refine_rsqrt(ch, dve, net.rstd[:], var[:], spare[:])

            @block.scalar
            def _(act):
                act.wait_ge(ready, 1)
                act.activation(net.rstd[:], net.rstd[:], ACT.Sqrt).then_inc(rooted, 1)


def project(nc, net, name, prep, w_in, weight, w_out, table, bias=None, logits=None):
    kc = w_in // P
    per_in = -(-kc * BT // 4)
    per = 512 // w_out if w_out > P else 4
    per_out = -(-BT // per)
    tw = w_out + (HEADS if logits else 0)
    with Stage(nc, name) as st:
        xn, xt = st.sb("xn", [P, BT, w_in]), st.sb("xt", [P, kc, BN])
        w_sb = st.sb("w", [P, kc, w_out])
        b_sb = st.sb("b", [P, w_in]) if bias is not None else None
        outb = st.sb("out", [P, BT, tw])
        part = st.sb("part", [P, 3, BT])
        if logits:
            a_sb, prod = st.sb("a", [P, 2, w_out]), st.sb("prod", [P, BT, w_out])
            lg = st.sb("lg", [P, BT, 2 * HEADS])
        loaded, xn_ready, xt_ready = st.sem("loaded"), st.sem("xn_ready"), st.sem("xt_ready")
        chain, out_ready, stored, out_free = (st.sem(x) for x in ("chain", "out_ready", "stored", "out_free"))
        turned = Ring(st.sem("turned"), st.sem("turned_free"), st.banks(4, "t"), per_in)
        product = Ring(st.sem("product"), st.sem("product_free"), st.banks(4, "m"), per_out)
        n_loads = 1 + (bias is not None) + 2 * bool(logits)

        with nc.allow_non_contiguous_dma(reason="weights, once"), nc.Block() as block:
            @block.sync
            def _(sp):
                sp.dma_start(w_sb[:], weight.rearrange("(c k) m -> k c m", k=P)).then_inc(loaded, 16)
                if bias is not None:
                    sp.dma_start(b_sb[:], bias.partition_broadcast(P)).then_inc(loaded, 16)
                if logits:
                    for s in range(2):
                        sp.dma_start(a_sb[:, s, :], logits[s].rearrange("h f -> (h f)").partition_broadcast(P))\
                            .then_inc(loaded, 16)
                sp.sem_inc(out_free, 1)
                view = table.rearrange("(t p) w -> p t w", p=P)
                with sp.Fori(0, NB) as b:
                    sp.wait_ge(out_ready, b + 1)
                    sp.dma_start(view[:, bass.ds(b * BT, BT), :], outb[:]).then_inc(stored, 16)
                    if logits:
                        sp.dma_start(logits[2].rearrange("(t p) w -> p t w", p=P)[:, bass.ds(b * BT, BT), :],
                                     lg[:, :, 0:HEADS]).then_inc(stored, 16)
                    sp.wait_ge(stored, (b + 1) * (32 if logits else 16))
                    sp.sem_inc(out_free, 1)

            @block.vector
            def _(dve):
                ch = Chain(dve, chain)
                product.give_credit(dve)
                dve.wait_ge(loaded, 16 * n_loads)

                def prepare(b):
                    if prep == "norm":
                        ch.mark(dve.tensor_copy(part[:, 0, :], net.mean[:, bass.ds(b * BT, BT)]))
                        ch.link(dve.tensor_copy(part[:, 1, :], net.rstd[:, bass.ds(b * BT, BT)]))
                        for j in range(BT):
                            last = dve.tensor_scalar(xn[:, j, :], net.x[:, bass.ds(b * (BT * D) + j * D, D)],
                                                     part[:, 0, j:j + 1], part[:, 1, j:j + 1],
                                                     ALU.subtract, ALU.mult)
                    elif prep == "relu":
                        ch.link(dve.tensor_copy(part[:, 0, :], net.dinv[:, bass.ds(b * BT, BT)]))
                        for j in range(BT):
                            ch.mark(dve.scalar_tensor_tensor(
                                out=xn[:, j, :], in0=net.acc[:, bass.ds(b * (BT * MW) + j * MW, w_in)],
                                scalar=part[:, 0, j:j + 1], in1=b_sb[:], op0=ALU.mult, op1=ALU.add))
                        ch.wait()
                        last = dve.tensor_scalar(xn[:], xn[:], 0.0, None, ALU.max)
                    else:
                        for j in range(BT):
                            last = dve.tensor_copy(xn[:, j, :], net.acc[:, bass.ds(b * (BT * MW) + j * MW, w_in)])
                    last.then_inc(xn_ready, 1)

                marks_prep = {"norm": 2, "relu": 1 + BT, "copy": 0}[prep]

                def finish(b):
                    dve.wait_ge(out_free, b + 1)
                    if not logits:
                        ch.link(dve.tensor_copy(part[:, 2, :], net.dinv[:, bass.ds(b * BT, BT)]))
                    for u in range(per_out):
                        bank = product.drain(dve, b)
                        j0, n = u * per, min(per, BT - u * per)
                        src = bank[:, 0:n * w_out].rearrange("p (j w) -> p j w", w=w_out)
                        if logits:
                            dve.tensor_copy(outb[:, j0:j0 + n, 0:w_out], src).then_inc(product.empty, 1)
                        else:
                            dve.tensor_tensor(outb[:, j0:j0 + n, :], src, over(part[:, 2, j0:j0 + n], w_out),
                                              ALU.mult).then_inc(product.empty, 1)
                    dve.wait_ge(product.empty, (b + 2) * per_out)
                    if logits:
                        for s in range(2):
                            ch.link(dve.tensor_tensor(prod[:], outb[:, :, 0:w_out], mid(a_sb[:, s, :], BT),
                                                      ALU.mult))
                            ch.link(dve.tensor_reduce(lg[:, :, s * HEADS:(s + 1) * HEADS],
                                                      prod[:].rearrange("p j (h f) -> p j h f", f=HID), AX,
                                                      ALU.add))
                        ch.mark(dve.tensor_copy(net.logit[:, bass.ds(b * (BT * 2 * HEADS), BT * 2 * HEADS)],
                                                lg[:].rearrange("p j a -> p (j a)")))
                        dve.tensor_copy(outb[:, :, w_out:tw], lg[:, :, 0:HEADS]).then_inc(out_ready, 1)
                    else:
                        for j in range(BT):
                            last = dve.tensor_copy(net.acc[:, bass.ds(b * (BT * MW) + j * MW, w_out)],
                                                   outb[:, j, :])
                        last.then_inc(out_ready, 1)

                marks_finish = 5 if logits else 1
                prepare(0)
                with dve.Fori(0, NB - 1) as b:
                    ch.enter(b, marks_prep + marks_finish)
                    dve.wait_ge(turned.full, (b + 1) * per_in)
                    prepare(b + 1)
                    finish(b)
                    ch.leave(NB - 1)
                finish(NB - 1)
                if logits:
                    dve.wait_ge(turned.full, NB * per_in)
                    dve.memset(net.acc[:], 0.0)

            @block.scalar
            def _(act):
                turned.give_credit(act)
                flat = xt[:].rearrange("p c n -> p (c n)")
                with act.Fori(0, NB) as b:
                    for u in range(per_in):
                        n = min(4, kc * BT - 4 * u) * P
                        bank = turned.drain(act, b)
                        act.activation(flat[:, u * 512:u * 512 + n], bank[:, 0:n], ACT.Copy)\
                            .then_inc(turned.empty, 1)

            @block.tensor
            def _(pe):
                pe.wait_ge(loaded, 16 * n_loads)
                with pe.Fori(0, NB) as b:
                    pe.wait_ge(xn_ready, b + 1)
                    for u in range(per_in):
                        bank = turned.fill(pe, b)
                        for m in range(4 * u, min(4 * u + 4, kc * BT)):
                            mm = pe.transpose(bank[:, m % 4 * P:(m % 4 + 1) * P],
                                              xn[:, m % BT, m // BT * P:(m // BT + 1) * P], net.ident[:])
                        mm.then_inc(turned.full, 1)
                    pe.wait_ge(turned.empty, (b + 2) * per_in)
                    for u in range(per_out):
                        bank = product.fill(pe, b)
                        for j in range(u * per, min(u * per + per, BT)):
                            at = (j - u * per) * w_out
                            for c in range(kc):
                                mm = pe.matmul(bank[:, at:at + w_out], xt[:, c, j * P:(j + 1) * P],
                                               w_sb[:, c, :], start=c == 0, stop=c == kc - 1)
                        mm.then_inc(product.full, 1)


def alloc_nodes(nc, net, ctx):
    def sb(name, shape, dt=F32):
        return ctx.enter_context(nc.sbuf_tensor(name, shape, dt))

    net.acc = sb("acc", [P, NT * MW])
    net.logit = sb("logit", [P, NT * 2 * HEADS])
    net.mean = sb("mean", [P, NT])
    net.rstd = sb("rstd", [P, NT])
    net.peak = sb("peak", [P, NIP, HEADS])


def load_nodes(nc, net, name, x, n):
    with Stage(nc, name) as st:
        cleared, loaded = st.sem("cleared"), st.sem("loaded")
        full = n // P
        with nc.Block() as block:
            @block.gpsimd
            def _(pool):
                pool.memset(net.x[:, (NT - 1) * D:NT * D], 0.0).then_inc(cleared, 1)

            @block.sync
            def _(sp):
                sp.wait_ge(cleared, 1)
                for t0 in range(0, full, BT):
                    t1 = min(full, t0 + BT)
                    sp.dma_start(net.x[:, t0 * D:t1 * D].rearrange("p (t w) -> p t w", w=D),
                                 x[t0 * P:t1 * P, :].rearrange("(t p) w -> p t w", p=P)).then_inc(loaded, 16)
                if n % P:
                    sp.dma_start(net.x[0:n % P, full * D:(full + 1) * D], x[full * P:n, :]).then_inc(loaded, 16)
                sp.wait_ge(loaded, 16 * (-(-full // BT) + (n % P > 0)))


def save_nodes(nc, net, name, x, n):
    with Stage(nc, name) as st:
        saved = st.sem("saved")
        full = n // P
        with nc.Block() as block:
            @block.sync
            def _(sp):
                for t0 in range(0, full, BT):
                    t1 = min(full, t0 + BT)
                    sp.dma_start(x[t0 * P:t1 * P, :].rearrange("(t p) w -> p t w", p=P),
                                 net.x[:, t0 * D:t1 * D].rearrange("p (t w) -> p t w", w=D)).then_inc(saved, 16)
                if n % P:
                    sp.dma_start(x[full * P:n, :], net.x[0:n % P, full * D:(full + 1) * D]).then_inc(saved, 16)
                sp.wait_ge(saved, 16 * (-(-full // BT) + (n % P > 0)))


def fc_layers(nc, net, bias, w1, b1, w2, b2):
    h, m = w1.shape
    with Stage(nc, "fc") as st:
        bias_sb, part = st.sb("bias", [P, h]), st.sb("part", [P, BT])
        w1_sb, w2_sb = st.sb("w1", [h, m]), st.sb("w2", [m, D])
        b1_sb, b2_sb = st.sb("b1", [m, 1]), st.sb("b2", [1, D])
        rows, ht, ft = st.sb("rows", [P, BT, h]), st.sb("ht", [h, BN]), st.sb("ft", [m, BN])
        loaded, ready, chain, begun = st.sem("loaded"), st.sem("ready"), st.sem("chain"), st.sem("begun")
        cols = Ring(st.sem("cols"), st.sem("cols_free"), st.banks(4, "c"), 4)
        outs = Ring(st.sem("outs"), st.sem("outs_free"), st.banks(4, "o"), 4)

        with nc.allow_non_contiguous_dma(reason="a bias, once"), nc.Block() as block:
            @block.sync
            def _(sp):
                for o, i in ((bias_sb, bias.partition_broadcast(P)), (w1_sb, w1), (w2_sb, w2),
                             (b1_sb, b1.rearrange("(k o) -> k o", o=1)), (b2_sb, b2.rearrange("(o k) -> o k", o=1))):
                    sp.dma_start(o[:], i).then_inc(loaded, 16)

            @block.vector
            def _(dve):
                ch = Chain(dve, chain)
                outs.give_credit(dve)
                dve.wait_ge(loaded, 80)

                def prepare(b):
                    ch.link(dve.tensor_copy(part[:], net.dinv[:, bass.ds(b * BT, BT)]))
                    for j in range(BT):
                        ch.mark(dve.scalar_tensor_tensor(
                            out=rows[:, j, :], in0=net.acc[:, bass.ds(b * (BT * MW) + j * MW, h)],
                            scalar=part[:, j:j + 1], in1=bias_sb[:], op0=ALU.mult, op1=ALU.add))
                    ch.wait()
                    dve.tensor_scalar(rows[:], rows[:], 0.0, None, ALU.max).then_inc(ready, 1)

                def finish(b):
                    for u in range(4):
                        bank = outs.drain(dve, b)
                        n = min(2, BT - 2 * u)
                        x = net.x[:, bass.ds(b * (BT * D) + 2 * u * D, n * D)]
                        dve.tensor_tensor(x, x, bank[:, 0:n * D], ALU.add).then_inc(outs.empty, 1)

                prepare(0)
                with dve.Fori(0, NB - 1) as b:
                    ch.enter(b, 1 + BT)
                    dve.wait_ge(cols.full, b * 4 + 2)
                    prepare(b + 1)
                    finish(b)
                    ch.leave(NB - 1)
                finish(NB - 1)

            @block.scalar
            def _(act):
                cols.give_credit(act)
                act.wait_ge(loaded, 80)
                with act.Fori(0, NB) as b:
                    for u in range(2):
                        n = min(4, BT - 4 * u) * P
                        act.activation(ht[:, u * 512:u * 512 + n], cols.drain(act, b)[0:h, 0:n], ACT.Copy)\
                            .then_inc(cols.empty, 1)
                    for u in range(2):
                        act.activation(ft[:, u * HB:(u + 1) * HB], cols.drain(act, b)[0:m, 0:HB], ACT.Identity,
                                       bias=b1_sb[:]).then_inc(cols.empty, 1)

            @block.tensor
            def _(pe):
                pe.wait_ge(loaded, 80)
                with pe.Fori(0, NB) as b:
                    pe.wait_ge(ready, b + 1)
                    for u in range(2):
                        bank = cols.fill(pe, b)
                        pe.sem_inc(begun, 1)
                        for j in range(4 * u, min(4 * u + 4, BT)):
                            mm = pe.transpose(bank[0:h, j % 4 * P:(j % 4 + 1) * P], rows[:, j, :], net.ident[:])
                        mm.then_inc(cols.full, 1)
                    pe.wait_ge(cols.empty, b * 4 + 4 + 2)
                    for u in range(2):
                        pe.matmul(cols.fill(pe, b)[0:m, 0:HB], w1_sb[:], ht[:, u * HB:(u + 1) * HB],
                                  start=True, stop=True).then_inc(cols.full, 1)
                    pe.wait_ge(cols.empty, b * 4 + 4 + 4)
                    for u in range(4):
                        bank = outs.fill(pe, b)
                        for j in range(2 * u, min(2 * u + 2, BT)):
                            o = bank[:, (j - 2 * u) * D:(j - 2 * u + 1) * D]
                            pe.matmul(o, ft[:, j * P:(j + 1) * P], w2_sb[:], start=True, stop=False)
                            mm = pe.matmul(o, net.ones[0:1, :], b2_sb[:], start=False, stop=True)
                        mm.then_inc(outs.full, 1)


class Gate:
    marks = 15

    def __init__(self, st, ne, again):
        self.ne, self.again = ne, again
        self.p, self.q = st.sb("gate_p", [P, BT, ne]), st.sb("gate_q", [P, BT, ne])
        self.ex, self.ex2 = st.sb("gate_ex", [P, BT, ne]), st.sb("gate_ex2", [P, BT, ne])
        self.row, self.low = st.sb("gate_row", [P, BT]), st.sb("gate_low", [P, ne, ne])
        self.above, self.same = st.sb("gate_above", [P, BT, ne, ne]), st.sb("gate_same", [P, BT, ne, ne])
        self.bias = st.sb("gate_bias", [P, ne])
        self.shifted, self.raised = st.sem("gate_shifted"), st.sem("gate_raised")
        self.calls = 1 + again

    def order(self, ch, dve, net):
        for e in range(self.ne):
            ch.mark(dve.tensor_scalar(self.low[:, e, :], net.iota[:, 0:self.ne], float(e), None, ALU.is_lt))
        ch.wait()

    def weights(self, ch, dve, i, logits, drained):
        p, q, row, ne = self.p, self.q, self.row, self.ne
        dve.tensor_tensor(p[:], logits.rearrange("p (j e) -> p j e", e=ne), mid(self.bias[:], BT), ALU.add)\
            .then_inc(drained.empty, 1)
        drained.settle(dve, i)
        ch.link(dve.tensor_reduce(row[:], p[:], AX, ALU.max))
        dve.tensor_tensor(p[:], p[:], over(row[:], ne), ALU.subtract).then_inc(self.shifted, 1)
        dve.wait_ge(self.raised, i * self.calls + 1)
        ch.link(dve.tensor_reduce(row[:], self.ex[:], AX, ALU.add))
        ch.link(dve.reciprocal(row[:], row[:]))
        ch.link(dve.tensor_tensor(p[:], self.ex[:], over(row[:], ne), ALU.mult))
        one, other = p[:].unsqueeze(3).broadcast_to([P, BT, ne, ne]), p[:].unsqueeze(2).broadcast_to([P, BT, ne, ne])
        ch.mark(dve.tensor_tensor(self.above[:], other, one, ALU.is_gt))
        ch.link(dve.tensor_tensor(self.same[:], other, one, ALU.is_equal))
        ch.link(dve.tensor_tensor(self.same[:], self.same[:],
                                  self.low[:].unsqueeze(1).broadcast_to([P, BT, ne, ne]), ALU.mult))
        ch.link(dve.tensor_tensor(self.above[:], self.above[:], self.same[:], ALU.add))
        ch.link(dve.tensor_reduce(q[:], self.above[:], AX, ALU.add))
        ch.link(dve.tensor_scalar(q[:], q[:], 1.5, None, ALU.is_lt))
        if self.again:
            ch.link(dve.tensor_reduce(row[:], p[:], AX, ALU.max))
            dve.tensor_tensor(p[:], p[:], over(row[:], ne), ALU.subtract).then_inc(self.shifted, 1)
            dve.wait_ge(self.raised, i * self.calls + 2)
            ch.link(dve.tensor_tensor(q[:], q[:], self.ex2[:], ALU.mult))
        else:
            ch.mark(dve.tensor_copy(row[:], row[:]))
            ch.link(dve.tensor_tensor(q[:], q[:], p[:], ALU.mult))
        ch.link(dve.tensor_reduce(row[:], q[:], AX, ALU.add))
        ch.link(dve.reciprocal(row[:], row[:]))
        ch.link(dve.tensor_tensor(q[:], q[:], over(row[:], ne), ALU.mult))

    def raise_(self, act, i):
        act.wait_ge(self.shifted, i * self.calls + 1)
        act.activation(self.ex[:], self.p[:], ACT.Exp).then_inc(self.raised, 1)
        if self.again:
            act.wait_ge(self.shifted, i * self.calls + 2)
            act.activation(self.ex2[:], self.p[:], ACT.Exp).then_inc(self.raised, 1)


def small_mixture(nc, net, w):
    ne, e1, e2 = w["eW2"].shape
    s1, s2 = w["sW2"].shape
    sc = s1 // P
    with Stage(nc, "mix") as st:
        gate = Gate(st, ne, True)
        part = st.sb("part", [P, 2, BT])
        xn, xt = st.sb("xn", [P, BT, D]), st.sb("xt", [P, 2, BN])
        gw = st.sb("gw", [P, 2, ne])
        sw1, sw2, sw3 = st.sb("sw1", [P, 2, s1]), st.sb("sw2", [P, sc, s2]), st.sb("sw3", [s2, D])
        sb1, sb2, sb3 = st.sb("sb1", [P, sc]), st.sb("sb2", [s2, 1]), st.sb("sb3", [1, D])
        ew1, ew2, ew3 = st.sb("ew1", [P, ne, 2, e1]), st.sb("ew2", [e1, ne, e2]), st.sb("ew3", [e2, ne, D])
        eb1, eb2, eb3 = st.sb("eb1", [e1, ne]), st.sb("eb2", [e2, ne]), st.sb("eb3", [ne, D])
        st1, st2 = st.sb("st1", [P, sc, HB]), st.sb("st2", [s2, BN])
        h1, h2 = st.sb("h1", [e1, BN]), st.sb("h2", [e2, BN])
        wt = st.sb("wt", [ne, BN])
        loaded, ready, chain, weighed = st.sem("loaded"), st.sem("ready"), st.sem("chain"), st.sem("weighed")
        n_cols = 4 + 2 * (sc + 1) + 2 + 4 * ne
        cols = Ring(st.sem("cols"), st.sem("cols_free"), st.banks(4, "c"), n_cols)
        outs = Ring(st.sem("outs"), st.sem("outs_free"), st.banks(4, "o"), 1 + 4 + 4 * ne)
        loads = [
            (gw[:], w["gW"].rearrange("(c k) e -> k c e", k=P)), (gate.bias[:], w["gb"].partition_broadcast(P)),
            (sw1[:], w["sW1"].rearrange("(c k) m -> k c m", k=P)), (sw2[:], w["sW2"].rearrange("(c k) m -> k c m", k=P)),
            (sw3[:], w["sW3"]), (sb1[:], w["sb1"].rearrange("(c k) -> k c", k=P)),
            (sb2[:], w["sb2"].rearrange("(k o) -> k o", o=1)), (sb3[:], w["sb3"].rearrange("(o k) -> o k", o=1)),
            (ew2[:], w["eW2"].rearrange("e k m -> k e m")), (ew3[:], w["eW3"].rearrange("e k m -> k e m")),
            (eb1[:], w["eb1"].rearrange("e k -> k e")), (eb2[:], w["eb2"].rearrange("e k -> k e")),
            (eb3[:], w["eb3"]),
        ] + [(ew1[:, e], w["eW1"][e].rearrange("(c k) m -> k c m", k=P)) for e in range(ne)]

        with nc.allow_non_contiguous_dma(reason="biases, once"), nc.Block() as block:
            @block.sync
            def _(sp):
                for o, i in loads:
                    sp.dma_start(o, i).then_inc(loaded, 16)

            @block.vector
            def _(dve):
                ch = Chain(dve, chain)
                outs.give_credit(dve)
                dve.wait_ge(loaded, 16 * len(loads))
                gate.order(ch, dve, net)

                def prepare(b):
                    ch.mark(dve.tensor_copy(part[:, 0, :], net.mean[:, bass.ds(b * BT, BT)]))
                    ch.link(dve.tensor_copy(part[:, 1, :], net.rstd[:, bass.ds(b * BT, BT)]))
                    for j in range(BT):
                        last = dve.tensor_scalar(xn[:, j, :], net.x[:, bass.ds(b * (BT * D) + j * D, D)],
                                                 part[:, 0, j:j + 1], part[:, 1, j:j + 1], ALU.subtract, ALU.mult)
                    last.then_inc(ready, 1)

                def finish(b, before):
                    gate.weights(ch, dve, b, outs.drain(dve, b)[:, 0:BT * ne], outs)
                    dve.sem_inc(weighed, 1)
                    before()
                    for e in range(-1, ne):
                        for u in range(4):
                            bank = outs.drain(dve, b)
                            n = min(2, BT - 2 * u)
                            if e < 0:
                                x = net.x[:, bass.ds(b * (BT * D) + 2 * u * D, n * D)]
                                dve.tensor_tensor(x, x, bank[:, 0:n * D], ALU.add).then_inc(outs.empty, 1)
                                continue
                            for j in range(2 * u, 2 * u + n):
                                x = net.x[:, bass.ds(b * (BT * D) + j * D, D)]
                                last = dve.scalar_tensor_tensor(
                                    out=x, in0=bank[:, (j - 2 * u) * D:(j - 2 * u + 1) * D],
                                    scalar=gate.q[:, j, e:e + 1], in1=x, op0=ALU.mult, op1=ALU.add)
                            last.then_inc(outs.empty, 1)
                        outs.settle(dve, b)

                def ahead(b):
                    dve.wait_ge(cols.full, b * n_cols + 4)
                    prepare(b + 1)

                prepare(0)
                with dve.Fori(0, NB - 1) as b:
                    ch.enter(b, Gate.marks + 2)
                    finish(b, lambda: ahead(b))
                    ch.leave(NB - 1)
                finish(NB - 1, lambda: None)

            @block.scalar
            def _(act):
                cols.give_credit(act)
                act.wait_ge(loaded, 16 * len(loads))
                flat = xt[:].rearrange("p c n -> p (c n)")

                def relu(b, out, k, bias, n=HB):
                    act.activation(out, cols.drain(act, b)[0:k, 0:n], ACT.Relu, bias=bias).then_inc(cols.empty, 1)

                with act.Fori(0, NB) as b:
                    for u in range(4):
                        n = min(4, 2 * BT - 4 * u) * P
                        act.activation(flat[:, u * 512:u * 512 + n], cols.drain(act, b)[:, 0:n], ACT.Copy)\
                            .then_inc(cols.empty, 1)
                    for s in range(2):
                        for c in range(sc):
                            relu(b, st1[:, c, :], P, sb1[:, c:c + 1])
                        relu(b, st2[:, s * HB:(s + 1) * HB], s2, sb2[:])
                    gate.raise_(act, b)
                    for u in range(2):
                        n = min(4, BT - 4 * u) * P
                        act.activation(wt[:, u * 512:u * 512 + n], cols.drain(act, b)[0:ne, 0:n], ACT.Copy)\
                            .then_inc(cols.empty, 1)
                    for e in range(ne):
                        for s in range(2):
                            relu(b, h1[:, s * HB:(s + 1) * HB], e1, eb1[:, e:e + 1])
                        for s in range(2):
                            relu(b, h2[:, s * HB:(s + 1) * HB], e2, eb2[:, e:e + 1])

            @block.tensor
            def _(pe):
                pe.wait_ge(loaded, 16 * len(loads))

                def columns(b, out, lhs, rhs):
                    bank = cols.fill(pe, b)
                    for c, (l, r) in enumerate(zip(lhs, rhs)):
                        mm = pe.matmul(bank[0:out, 0:HB], l, r, start=c == 0, stop=c == len(lhs) - 1)
                    mm.then_inc(cols.full, 1)

                def drained(b, n):
                    pe.wait_ge(cols.empty, (b + 1) * n_cols + n)

                with pe.Fori(0, NB) as b:
                    pe.wait_ge(ready, b + 1)
                    for u in range(4):
                        bank = cols.fill(pe, b)
                        for m in range(4 * u, min(4 * u + 4, 2 * BT)):
                            mm = pe.transpose(bank[:, m % 4 * P:(m % 4 + 1) * P],
                                              xn[:, m % BT, m // BT * P:(m // BT + 1) * P], net.ident[:])
                        mm.then_inc(cols.full, 1)
                    drained(b, 4)
                    bank = outs.fill(pe, b)
                    for j in range(BT):
                        for c in range(2):
                            mm = pe.matmul(bank[:, j * ne:(j + 1) * ne], xt[:, c, j * P:(j + 1) * P], gw[:, c, :],
                                           start=c == 0, stop=c == 1)
                    mm.then_inc(outs.full, 1)
                    n = 4
                    for s in range(2):
                        xs = [xt[:, c, s * HB:(s + 1) * HB] for c in range(2)]
                        for m in range(sc):
                            columns(b, P, [sw1[:, c, m * P:(m + 1) * P] for c in range(2)], xs)
                        n += sc
                        drained(b, n)
                        columns(b, s2, [sw2[:, c, :] for c in range(sc)], [st1[:, c, :] for c in range(sc)])
                        n += 1
                    pe.wait_ge(weighed, b + 1)
                    for u in range(2):
                        bank = cols.fill(pe, b)
                        for j in range(4 * u, min(4 * u + 4, BT)):
                            mm = pe.transpose(bank[0:ne, j % 4 * P:(j % 4 + 1) * P], gate.q[:, j, :], net.ident[:])
                        mm.then_inc(cols.full, 1)
                    n += 2
                    drained(b, n)
                    for u in range(4):
                        bank = outs.fill(pe, b)
                        for j in range(2 * u, min(2 * u + 2, BT)):
                            o = bank[:, (j - 2 * u) * D:(j - 2 * u + 1) * D]
                            pe.matmul(o, st2[:, j * P:(j + 1) * P], sw3[:], start=True, stop=False)
                            pe.matmul(o, net.ones[0:1, :], sb3[:], start=False, stop=False)
                            mm = pe.matmul(o, wt[:, j * P:(j + 1) * P], eb3[:], start=False, stop=True)
                        mm.then_inc(outs.full, 1)
                    for e in range(ne):
                        for s in range(2):
                            columns(b, e1, [ew1[:, e, c, :] for c in range(2)],
                                    [xt[:, c, s * HB:(s + 1) * HB] for c in range(2)])
                        drained(b, n + 2)
                        for s in range(2):
                            columns(b, e2, [ew2[:, e, :]], [h1[:, s * HB:(s + 1) * HB]])
                        n += 4
                        drained(b, n)
                        for u in range(4):
                            bank = outs.fill(pe, b)
                            for j in range(2 * u, min(2 * u + 2, BT)):
                                mm = pe.matmul(bank[:, (j - 2 * u) * D:(j - 2 * u + 1) * D],
                                               h2[:, j * P:(j + 1) * P], ew3[:, e, :], start=True, stop=True)
                            mm.then_inc(outs.full, 1)


def segment_max(nc, net, name, table):
    half = KT + 2 - KT % 2
    turns = -(-half // (2 * HALF))
    with Stage(nc, name) as st:
        index = st.sb("index", [P, 2, HALF], I32)
        rows = st.sb("rows", [P, 2, HALF, HEADS])
        cols = st.sb("cols", [P, KP, HEADS])
        best, back = st.sb("best", [P, HEADS, KC, P]), st.sb("back", [P, 2, KC, P])
        item_of = st.sb("item_of", [P, KC, NIP])
        ends = st.sb("ends", [HEADS, 2, KP])
        step, carry = st.sb("step", [HEADS, 2, KP]), st.sb("carry", [HEADS, 2, KP])
        carried = st.sb("carried", [P, 2, KC, HEADS])
        gathered = [st.sem("gathered0"), st.sem("gathered1")]
        indexed, go, copied, cleared = (st.sem(x) for x in ("indexed", "go", "copied", "cleared"))
        turned, laid, scanned, chain, pe_done = (st.sem(x) for x in ("turned", "laid", "scanned", "chain", "pe_done"))
        taken, widened = st.sem("taken"), st.sem("widened")
        bank = st.banks(8)

        with nc.Block() as block:
            @block.gpsimd
            def _(pool):
                pool.memset(cols[:, turns * 2 * HALF:KP, :], 0.0).then_inc(cleared, 1)

                def turn(i, first):
                    for h in range(2):
                        if not first:
                            pool.wait_ge(gathered[h], P * i)
                            pool.wait_ge(copied, i * 2 + h - 1)
                        pool.tensor_copy(index[:, h, :], net.src_col[:, bass.ds(i * (2 * HALF) + h * HALF, HALF)])\
                            .then_inc(indexed, 1)
                        pool.wait_ge(indexed, i * 2 + h + 1)
                        pool.sem_inc(go, 1)
                        for j in range(HALF):
                            pool.indirect_dma_start(rows[:, h, j, :], None, table,
                                                    bass.IndirectOffsetOnAxis(ap=index[:, h, j:j + 1], axis=0))\
                                .then_inc(gathered[h], 16)

                turn(0, True)
                with pool.Fori(1, turns) as i:
                    turn(i, False)

            @block.vector
            def _(dve):
                ch = Chain(dve, chain)
                with dve.Fori(0, turns) as i:
                    for h in range(2):
                        dve.wait_ge(gathered[h], P * i + P)
                        dve.tensor_copy(cols[:, bass.ds(i * (2 * HALF) + h * HALF, HALF), :], rows[:, h])\
                            .then_inc(copied, 1)
                for h in range(HEADS):
                    dve.wait_ge(laid, 2 * h + 2)
                    b = best[:, h].rearrange("p c e -> p (c e)")
                    left, right = (back[:, s].rearrange("p c e -> p (c e)") for s in range(2))
                    start, end = (m[:].rearrange("p c e -> p (c e)") for m in (net.run_start, net.run_end))
                    ch.mark(dve.tensor_tensor_scan(left, start, b, -BIG, ALU.add, ALU.max))
                    ch.link(dve.tensor_tensor_scan(right[:, ::-1], end[:, ::-1], b[:, ::-1], -BIG, ALU.add, ALU.max))
                    ch.link(dve.tensor_tensor(b, left, right, ALU.max))
                dve.sem_inc(scanned, 1)
                dve.wait_ge(pe_done, 1)
                for s in range(2):
                    ch.mark(dve.tensor_copy(ends[:, s, 0:512], bank[2 * s][0:HEADS, :]))
                    ch.link(dve.tensor_copy(ends[:, s, 512:KP], bank[2 * s + 1][0:HEADS, 0:KP - 512]))
                ch.mark(dve.memset(step[:, 0, 0:1], -BIG))
                ch.mark(dve.memset(step[:, 1, KP - 1:KP], -BIG))
                ch.mark(dve.tensor_tensor(step[:, 0, 1:KP], ends[:, 1, 0:KP - 1], net.link_left[:, 1:KP], ALU.add))
                ch.link(dve.tensor_tensor(step[:, 1, 0:KP - 1], ends[:, 0, 1:KP], net.link_right[:, 0:KP - 1],
                                          ALU.add))
                ch.mark(dve.tensor_tensor_scan(carry[:, 0, :], net.pass_left[:], step[:, 0, :], -BIG,
                                               ALU.add, ALU.max))
                ch.link(dve.tensor_tensor_scan(carry[:, 1, ::-1], net.pass_right[:, ::-1], step[:, 1, ::-1], -BIG,
                                               ALU.add, ALU.max))
                dve.sem_inc(scanned, 1)
                dve.wait_ge(pe_done, 2)
                ch.link(dve.tensor_copy(carried[:].rearrange("p s c h -> p (s c h)"),
                                        bank[4][:, 0:2 * KC * HEADS]))
                for h in range(HEADS):
                    for s, mask in enumerate((net.not_first_run, net.not_last_run)):
                        ch.link(dve.tensor_tensor(back[:, s], mask[:], over(carried[:, s, :, h], P), ALU.add))
                        last = dve.tensor_tensor(best[:, h], best[:, h], back[:, s], ALU.max)
                        if s == 0:
                            ch.link(last)
                        else:
                            last.then_inc(scanned, 1)
                for n in range(2 * HEADS):
                    h, s = n // 2, n % 2
                    dve.wait_ge(pe_done, 3 + n)
                    dve.tensor_copy(net.peak[:, s * IC:(s + 1) * IC, h], bank[n][:, 0:IC]).then_inc(taken, 1)

            @block.scalar
            def _(act):
                act.activation(item_of[:], net.item_of[:], ACT.Copy).then_inc(widened, 1)
                for n in range(2 * HEADS):
                    h, s = n // 2, n % 2
                    act.wait_ge(turned, n + 1)
                    c0, c1 = (0, 4) if s == 0 else (4, KC)
                    act.activation(best[:, h, c0:c1, :].rearrange("p c e -> p (c e)"),
                                   bank[n][:, 0:(c1 - c0) * P], ACT.Copy).then_inc(laid, 1)

            @block.tensor
            def _(pe):
                pe.wait_ge(cleared, 1)
                pe.wait_ge(copied, turns * 2)
                for n in range(2 * HEADS):
                    h, s = n // 2, n % 2
                    for c in range(4 * s, min(4 * s + 4, KC)):
                        mm = pe.transpose(bank[n][:, (c - 4 * s) * P:(c - 4 * s + 1) * P],
                                          cols[:, c * P:(c + 1) * P, h], net.ident[:])
                    mm.then_inc(turned, 1)
                pe.wait_ge(scanned, 1)
                for s, at in enumerate((0, P - 1)):
                    for c in range(KC):
                        b = bank[2 * s + c // 4]
                        mm = pe.transpose(b[0:HEADS, c % 4 * P:(c % 4 + 1) * P], best[:, :, c, at], net.ident[:])
                mm.then_inc(pe_done, 1)
                pe.wait_ge(scanned, 2)
                for s in range(2):
                    for c in range(KC):
                        at = (s * KC + c) * HEADS
                        mm = pe.transpose(bank[4][:, at:at + HEADS], carry[:, s, c * P:(c + 1) * P],
                                          net.ident[0:HEADS, 0:HEADS])
                mm.then_inc(pe_done, 1)
                pe.wait_ge(widened, 1)
                for n in range(2 * HEADS):
                    h, s = n // 2, n % 2
                    pe.wait_ge(scanned, 3 + h)
                    for c in range(KC):
                        mm = pe.matmul(bank[n][:, 0:IC], best[:, h, c, :], item_of[:, c, s * IC:(s + 1) * IC],
                                       start=c == 0, stop=c == KC - 1)
                    mm.then_inc(pe_done, 1)


def gat_pass(nc, net, name, table):
    with Stage(nc, name) as st:
        index = st.sb("index", [P, 2, HALF], I32)
        rows, msg = st.sb("rows", [P, 2, HALF, GW]), st.sb("msg", [P, 2, HALF, MW])
        onehot, turned_sb = st.sb("onehot", [P, 2, HALF, P]), st.sb("turned_sb", [P, 2, HALF, P])
        lg, mx, scaled = (st.sb(x, [P, HALF, HEADS]) for x in ("lg", "mx", "scaled"))
        sums = st.banks(4, "sum")
        flips = st.banks(2, "flip")
        node_lg = st.banks(2, "node")
        gathered = [st.sem("gathered0"), st.sem("gathered1")]
        indexed, go, made, turned, copied = (st.sem(x) for x in ("indexed", "go", "made", "turned", "copied"))
        looked, shifted, raised, ready, summed, added = (
            st.sem(x) for x in ("looked", "shifted", "raised", "ready", "summed", "added"))
        chain = st.sem("chain")

        with nc.Block() as block:
            @block.gpsimd
            def _(pool):
                gather_items(pool, net, table, rows, GW, index, gathered, indexed, go, ready, lambda q: q - 1)

            @block.vector
            def _(dve):
                ch = Chain(dve, chain)
                tile = [dve.alloc_register(f"{name}_t{j}") for j in range(HALF)]

                def one_hot(col, h):
                    dve.tensor_tensor(onehot[:, h], over(net.dloc[:, col], P), mid(net.iota[:], HALF),
                                      ALU.is_equal).then_inc(made, 1)

                def leaky(x):
                    ch.link(dve.tensor_scalar(scaled[:], x[:], 0.2, None, ALU.mult))
                    ch.link(dve.tensor_tensor(x[:], x[:], scaled[:], ALU.max))

                def weigh(q, h):
                    at = node_lg[h][:, 0:HALF * 2 * HEADS].rearrange("p (j a) -> p j a", a=2 * HEADS)
                    dve.wait_ge(gathered[h], (q - h) * (P // 2) + P)
                    dve.wait_ge(looked, q + 1)
                    ch.mark(dve.tensor_tensor(lg[:], rows[:, h, :, D:GW], at[:, :, HEADS:2 * HEADS], ALU.add))
                    ch.link(dve.tensor_tensor(mx[:], net.peak[:, bass.ds(q * HALF, HALF), :], at[:, :, 0:HEADS],
                                              ALU.max))
                    ch.link(dve.tensor_tensor(mx[:], mx[:], at[:, :, HEADS:2 * HEADS], ALU.add))
                    leaky(mx)
                    leaky(lg)
                    ch.link(dve.tensor_tensor(lg[:], lg[:], mx[:], ALU.subtract))
                    dve.tensor_scalar(lg[:], lg[:], 0.0, None, ALU.min).then_inc(shifted, 1)

                def accumulate(q, first):
                    dve.load(tile, net.t_of[0:1, bass.ds(q * HALF, HALF)])
                    for j in range(HALF):
                        dve.wait_ge(summed, q * HALF + j + 1)
                        if not (first and j == 0):
                            dve.wait_ge(added, q * HALF + j)
                        acc = net.acc[:, bass.ds(dve.snap(tile[j], min_val=0, max_val=NT - 1) * MW, MW)]
                        dve.tensor_tensor(acc, acc, sums[j % 4][:, 0:MW], ALU.add).then_inc(added, 1)

                def message(q, h):
                    ch.mark(dve.tensor_tensor(msg[:, h, :, GW:MW], net.peak[:, bass.ds(q * HALF, HALF), :],
                                              over(net.first_of[:, bass.ds(q * HALF, HALF)], HEADS), ALU.mult))
                    dve.wait_ge(raised, q + 1)
                    heads = [x[:, h, :, 0:D].rearrange("p j (h f) -> p j h f", f=HID) for x in (msg, rows)]
                    dve.tensor_tensor(heads[0], heads[1], over(msg[:, h, :, D:GW], HID), ALU.mult)\
                        .then_inc(ready, 1)

                def step(q, h, first):
                    weigh(q, h)
                    if not first:
                        accumulate(q - 1, first=False)
                    one_hot(bass.ds((q + 1) * HALF, HALF), 1 - h)
                    message(q, h)

                marks = 9
                one_hot(slice(0, HALF), 0)
                weigh(0, 0)
                one_hot(slice(HALF, 2 * HALF), 1)
                message(0, 0)
                weigh(1, 1)
                accumulate(0, True)
                one_hot(slice(2 * HALF, 3 * HALF), 0)
                message(1, 1)
                with dve.Fori(1, STEPS // 2) as i:
                    ch.enter(i - 1, 2 * marks)
                    for h in range(2):
                        step(i * 2 + h, h, False)
                    ch.leave(STEPS // 2 - 1)
                accumulate(STEPS - 1, False)

            @block.scalar
            def _(act):
                def copy_turned(q, h):
                    act.wait_ge(turned, q + 1)
                    for s in range(2):
                        last = act.activation(
                            turned_sb[:, h, 4 * s:4 * s + 4, :].rearrange("p j n -> p (j n)"), flips[s][:], ACT.Copy)
                    last.then_inc(copied, 1)

                copy_turned(0, 0)
                with act.Fori(0, STEPS // 2) as i:
                    for h in range(2):
                        copy_turned(i * 2 + h + 1, 1 - h)
                        act.wait_ge(shifted, i * 2 + h + 1)
                        act.activation(msg[:, h, :, D:GW], lg[:], ACT.Exp).then_inc(raised, 1)

            @block.tensor
            def _(pe):
                tile = [pe.alloc_register(f"{name}_u{j}") for j in range(HALF)]

                def look_up(q, h, first):
                    pe.wait_ge(made, q + 1)
                    if not first:
                        pe.wait_ge(copied, q)
                    for j in range(HALF):
                        mm = pe.transpose(flips[j // 4][:, j % 4 * P:(j % 4 + 1) * P], onehot[:, h, j, :],
                                          net.ident[:])
                    mm.then_inc(turned, 1)
                    pe.load(tile, net.t_of[0:1, bass.ds(q * HALF, HALF)])
                    pe.wait_ge(copied, q + 1)
                    for j in range(HALF):
                        t = pe.snap(tile[j], min_val=0, max_val=NT - 1)
                        mm = pe.matmul(node_lg[h][:, j * 2 * HEADS:(j + 1) * 2 * HEADS], turned_sb[:, h, j, :],
                                       net.logit[:, bass.ds(t * (2 * HEADS), 2 * HEADS)], start=True, stop=True)
                    mm.then_inc(looked, 1)

                def sum_up(q, h, first):
                    pe.wait_ge(ready, q + 1)
                    for j in range(HALF):
                        if not first or j >= 4:
                            pe.wait_ge(added, q * HALF + j - 3)
                        pe.matmul(sums[j % 4][:, 0:MW], onehot[:, h, j, :], msg[:, h, j, :], start=True, stop=True)\
                            .then_inc(summed, 1)

                look_up(0, 0, True)
                look_up(1, 1, False)
                sum_up(0, 0, True)
                with pe.Fori(0, STEPS // 2 - 1) as i:
                    look_up(i * 2 + 2, 0, False)
                    sum_up(i * 2 + 1, 1, False)
                    look_up(i * 2 + 3, 1, False)
                    sum_up(i * 2 + 2, 0, False)
                look_up(STEPS, 0, False)
                sum_up(STEPS - 1, 1, False)


def gat_finish(nc, net, name, table, bias, add_to_x):
    with Stage(nc, name) as st:
        own, own_w, mx, scaled = (st.sb(x, [P, NT, HEADS]) for x in ("own", "own_w", "mx", "scaled"))
        den, b_sb = st.sb("den", [P, NT, HEADS]), st.sb("b", [P, D])
        rows, tmp = st.sb("rows", [P, BT, D]), st.sb("tmp", [P, BT, D])
        part = st.sb("part", [P, 2, BT, HEADS])
        loaded, row_in, row_free, chain, diff, raised = (
            st.sem(x) for x in ("loaded", "row_in", "row_free", "chain", "diff", "raised"))
        acc = net.acc[:].rearrange("p (t w) -> p t w", w=MW)
        lg = net.logit[:].rearrange("p (t a) -> p t a", a=2 * HEADS)

        with nc.Block() as block:
            @block.sync
            def _(sp):
                sp.dma_start(b_sb[:], bias.partition_broadcast(P)).then_inc(loaded, 16)
                view = table.rearrange("(t p) w -> p t w", p=P)
                with sp.Fori(0, NB) as b:
                    sp.wait_ge(row_free, b + 1)
                    sp.dma_start(rows[:], view[:, bass.ds(b * BT, BT), 0:D]).then_inc(row_in, 16)

            @block.vector
            def _(dve):
                ch = Chain(dve, chain)
                dve.sem_inc(row_free, 1)

                def leaky(x):
                    ch.link(dve.tensor_scalar(scaled[:], x[:], 0.2, None, ALU.mult))
                    ch.link(dve.tensor_tensor(x[:], x[:], scaled[:], ALU.max))

                ch.link(dve.tensor_scalar(scaled[:, :, 0], net.has_edge[:], -1.0, BIG, ALU.add, ALU.mult))
                ch.link(dve.tensor_tensor(mx[:], acc[:, :, GW:MW], over(scaled[:, :, 0], HEADS), ALU.add))
                ch.link(dve.tensor_tensor(mx[:], mx[:], lg[:, :, 0:HEADS], ALU.max))
                ch.link(dve.tensor_tensor(mx[:], mx[:], lg[:, :, HEADS:2 * HEADS], ALU.add))
                leaky(mx)
                ch.link(dve.tensor_tensor(own[:], lg[:, :, 0:HEADS], lg[:, :, HEADS:2 * HEADS], ALU.add))
                leaky(own)
                dve.tensor_tensor(own[:], own[:], mx[:], ALU.subtract).then_inc(diff, 1)
                dve.wait_ge(raised, 1)
                ch.link(dve.tensor_tensor(den[:], acc[:, :, D:GW], own_w[:], ALU.add))
                ch.link(dve.tensor_scalar(den[:], den[:], 1e-16, None, ALU.add))
                ch.link(dve.reciprocal(den[:], den[:]))
                dve.wait_ge(loaded, 16)
                with dve.Fori(0, NB) as b:
                    ch.enter(b, 4 + (3 if add_to_x else 2) * BT)
                    ch.mark(dve.tensor_copy(part[:, 0], own_w[:, bass.ds(b * BT, BT), :]))
                    ch.link(dve.tensor_copy(part[:, 1], den[:, bass.ds(b * BT, BT), :]))
                    dve.wait_ge(row_in, b * 16 + 16)
                    heads = [x[:].rearrange("p j (h f) -> p (j h) f", f=HID) for x in (rows, tmp)]
                    ch.link(dve.tensor_tensor(heads[1], heads[0],
                                              over(part[:, 0].rearrange("p j h -> p (j h)"), HID), ALU.mult))
                    dve.sem_inc(row_free, 1)
                    for j in range(BT):
                        ch.mark(dve.tensor_tensor(tmp[:, j, :], tmp[:, j, :],
                                                  net.acc[:, bass.ds(b * (BT * MW) + j * MW, D)], ALU.add))
                    ch.wait()
                    ch.link(dve.tensor_tensor(heads[1], heads[1],
                                              over(part[:, 1].rearrange("p j h -> p (j h)"), HID), ALU.mult))
                    for j in range(BT):
                        if add_to_x:
                            ch.mark(dve.tensor_tensor(tmp[:, j, :], tmp[:, j, :], b_sb[:], ALU.add))
                        else:
                            ch.mark(dve.tensor_tensor(net.acc[:, bass.ds(b * (BT * MW) + j * MW, D)],
                                                      tmp[:, j, :], b_sb[:], ALU.add))
                    ch.wait()
                    for j in range(BT):
                        if add_to_x:
                            x = net.x[:, bass.ds(b * (BT * D) + j * D, D)]
                            ch.mark(dve.tensor_tensor(x, x, tmp[:, j, :], ALU.add))
                    ch.wait()
                    ch.leave(NB)

            @block.scalar
            def _(act):
                act.wait_ge(diff, 1)
                act.activation(own_w[:], own[:], ACT.Exp).then_inc(raised, 1)


def route_nodes(nc, net, w):
    ne = w["Wr"].shape[1]
    with Stage(nc, "route") as st:
        gate = Gate(st, ne, False)
        part = st.sb("part", [P, 2, BT])
        xn, xt = st.sb("xn", [P, BT, D]), st.sb("xt", [P, 2, BN])
        wr, b2, wt = st.sb("wr", [P, 2, ne]), st.sb("b2", [ne, D]), st.sb("wt", [ne, BN])
        loaded, ready, chain, weighed = st.sem("loaded"), st.sem("ready"), st.sem("chain"), st.sem("weighed")
        kept = st.sem("kept")
        n_cols = 4 + 2
        cols = Ring(st.sem("cols"), st.sem("cols_free"), st.banks(4, "c"), n_cols)
        outs = Ring(st.sem("outs"), st.sem("outs_free"), st.banks(4, "o"), 1 + 4)

        with nc.allow_non_contiguous_dma(reason="gate weights, once"), nc.Block() as block:
            @block.sync
            def _(sp):
                for o, i in ((wr[:], w["Wr"].rearrange("(c k) e -> k c e", k=P)),
                             (gate.bias[:], w["br"].partition_broadcast(P)), (b2[:], w["b2"])):
                    sp.dma_start(o, i).then_inc(loaded, 16)

            @block.gpsimd
            def _(pool):
                pool.sem_inc(kept, 1)
                with pool.Fori(0, NB) as b:
                    pool.wait_ge(cols.empty, (b + 1) * n_cols + 4)
                    pool.tensor_copy(net.xnt[:, :, bass.ds(b * BN, BN)], xt[:]).then_inc(kept, 1)

            @block.vector
            def _(dve):
                ch = Chain(dve, chain)
                outs.give_credit(dve)
                dve.wait_ge(loaded, 48)
                gate.order(ch, dve, net)

                def prepare(b):
                    ch.mark(dve.tensor_copy(part[:, 0, :], net.mean[:, bass.ds(b * BT, BT)]))
                    ch.link(dve.tensor_copy(part[:, 1, :], net.rstd[:, bass.ds(b * BT, BT)]))
                    for j in range(BT):
                        last = dve.tensor_scalar(xn[:, j, :], net.x[:, bass.ds(b * (BT * D) + j * D, D)],
                                                 part[:, 0, j:j + 1], part[:, 1, j:j + 1], ALU.subtract, ALU.mult)
                    last.then_inc(ready, 1)

                def finish(b):
                    gate.weights(ch, dve, b, outs.drain(dve, b)[:, 0:BT * ne], outs)
                    dve.sem_inc(weighed, 1)
                    ch.link(dve.tensor_copy(net.weight[:, :, bass.ds(b * BT, BT)],
                                            gate.q[:].rearrange("p j e -> p e j")))
                    for u in range(4):
                        bank = outs.drain(dve, b)
                        n = min(2, BT - 2 * u)
                        x = net.x[:, bass.ds(b * (BT * D) + 2 * u * D, n * D)]
                        dve.tensor_tensor(x, x, bank[:, 0:n * D], ALU.add).then_inc(outs.empty, 1)

                prepare(0)
                with dve.Fori(0, NB - 1) as b:
                    ch.enter(b, Gate.marks + 3)
                    dve.wait_ge(cols.full, b * n_cols + 4)
                    prepare(b + 1)
                    finish(b)
                    ch.leave(NB - 1)
                finish(NB - 1)

            @block.scalar
            def _(act):
                cols.give_credit(act)
                flat = xt[:].rearrange("p c n -> p (c n)")
                with act.Fori(0, NB) as b:
                    act.wait_ge(kept, b + 1)
                    for u in range(4):
                        n = min(4, 2 * BT - 4 * u) * P
                        act.activation(flat[:, u * 512:u * 512 + n], cols.drain(act, b)[:, 0:n], ACT.Copy)\
                            .then_inc(cols.empty, 1)
                    gate.raise_(act, b)
                    for u in range(2):
                        n = min(4, BT - 4 * u) * P
                        act.activation(wt[:, u * 512:u * 512 + n], cols.drain(act, b)[0:ne, 0:n], ACT.Copy)\
                            .then_inc(cols.empty, 1)

            @block.tensor
            def _(pe):
                pe.wait_ge(loaded, 48)
                with pe.Fori(0, NB) as b:
                    pe.wait_ge(ready, b + 1)
                    for u in range(4):
                        bank = cols.fill(pe, b)
                        for m in range(4 * u, min(4 * u + 4, 2 * BT)):
                            mm = pe.transpose(bank[:, m % 4 * P:(m % 4 + 1) * P],
                                              xn[:, m % BT, m // BT * P:(m // BT + 1) * P], net.ident[:])
                        mm.then_inc(cols.full, 1)
                    pe.wait_ge(cols.empty, (b + 1) * n_cols + 4)
                    bank = outs.fill(pe, b)
                    for j in range(BT):
                        for c in range(2):
                            mm = pe.matmul(bank[:, j * ne:(j + 1) * ne], xt[:, c, j * P:(j + 1) * P], wr[:, c, :],
                                           start=c == 0, stop=c == 1)
                    mm.then_inc(outs.full, 1)
                    pe.wait_ge(weighed, b + 1)
                    for u in range(2):
                        bank = cols.fill(pe, b)
                        for j in range(4 * u, min(4 * u + 4, BT)):
                            mm = pe.transpose(bank[0:ne, j % 4 * P:(j % 4 + 1) * P], gate.q[:, j, :], net.ident[:])
                        mm.then_inc(cols.full, 1)
                    pe.wait_ge(cols.empty, (b + 1) * n_cols + 6)
                    for u in range(4):
                        bank = outs.fill(pe, b)
                        for j in range(2 * u, min(2 * u + 2, BT)):
                            mm = pe.matmul(bank[:, (j - 2 * u) * D:(j - 2 * u + 1) * D], wt[:, j * P:(j + 1) * P],
                                           b2[:], start=True, stop=True)
                        mm.then_inc(outs.full, 1)


def large_mixture(nc, net, w):
    ne, _, hid = w["W1"].shape
    hc = hid // P
    with Stage(nc, "moe") as st:
        w1, w2 = st.sb("w1", [P, 2, 2, hid]), st.sb("w2", [P, 2, hc, D])
        b1, scale, shift = st.sb("b1", [P, 2, hc]), st.sb("scale", [P, 2, 2]), st.sb("shift", [P, 2, 2])
        xe, ht = st.sb("xe", [P, 2, BN]), st.sb("ht", [P, hc, BN])
        part = st.sb("part", [P, BT])
        loaded = [st.sem("loaded0"), st.sem("loaded1")]
        ready, chain = st.sem("ready"), st.sem("chain")
        begun_dve, begun_pe = st.sem("begun_dve"), st.sem("begun_pe")
        hidden = Ring(st.sem("hidden"), st.sem("hidden_free"), st.banks(4, "h"), 2 * hc)
        outs = Ring(st.sem("outs"), st.sem("outs_free"), st.banks(4, "o"), 4)
        n_loads = 5

        with nc.allow_non_contiguous_dma(reason="biases and scales"), nc.Block() as block:
            @block.sync
            def _(sp):
                def load(e, h):
                    one = lambda a: a[bass.ds(e, 1)]
                    for o, i in ((w1[:, h], one(w["W1"]).rearrange("o (c k) m -> k (o c) m", k=P)),
                                 (scale[:, h, :], one(w["ln_g"]).rearrange("o (c k) -> k (o c)", k=P)),
                                 (shift[:, h, :], one(w["ln_b"]).rearrange("o (c k) -> k (o c)", k=P)),
                                 (b1[:, h, :], one(w["b1"]).rearrange("o (c k) -> k (o c)", k=P)),
                                 (w2[:, h], one(w["W2"]).rearrange("o (c k) m -> k (o c) m", k=P))):
                        sp.dma_start(o, i).then_inc(loaded[h], 16)

                for h in range(2):
                    load(h, h)
                with sp.Fori(1, ne // 2) as i:
                    for h in range(2):
                        sp.wait_ge(outs.full, (i * 2 + h - 1) * (NB * 4))
                        load(i * 2 + h, h)

            @block.vector
            def _(dve):
                ch = Chain(dve, chain)
                outs.give_credit(dve)
                with dve.Fori(0, ne // 2) as i:
                    for h in range(2):
                        e = i * 2 + h
                        dve.wait_ge(loaded[h], i * (16 * n_loads) + 16 * n_loads)
                        dve.sem_inc(begun_dve, 1)
                        with dve.Fori(0, NB) as b:
                            turn = e * NB + b
                            for c in range(2):
                                last = dve.tensor_scalar(xe[:, c, :], net.xnt[:, c, bass.ds(b * BN, BN)],
                                                         scale[:, h, c:c + 1], shift[:, h, c:c + 1],
                                                         ALU.mult, ALU.add)
                            last.then_inc(ready, 1)
                            dve.tensor_copy(part[:], net.weight[:, bass.ds(e, 1), bass.ds(b * BT, BT)])\
                                .then_inc(chain, 1)
                            dve.wait_ge(chain, turn + 1)
                            for u in range(4):
                                bank = outs.drain(dve, turn)
                                for j in range(2 * u, min(2 * u + 2, BT)):
                                    x = net.x[:, bass.ds(b * (BT * D) + j * D, D)]
                                    last = dve.scalar_tensor_tensor(
                                        out=x, in0=bank[:, (j - 2 * u) * D:(j - 2 * u + 1) * D],
                                        scalar=part[:, j:j + 1], in1=x, op0=ALU.mult, op1=ALU.add)
                                last.then_inc(outs.empty, 1)
                            outs.settle(dve, turn)

            @block.scalar
            def _(act):
                hidden.give_credit(act)
                with act.Fori(0, ne // 2) as i:
                    for h in range(2):
                        act.wait_ge(loaded[h], i * (16 * n_loads) + 16 * n_loads)
                        with act.Fori(0, NB) as b:
                            turn = (i * 2 + h) * NB + b
                            for s in range(2):
                                for m in range(hc):
                                    act.activation(ht[:, m, s * HB:(s + 1) * HB], hidden.drain(act, turn)[:, 0:HB],
                                                   ACT.Gelu, bias=b1[:, h, m:m + 1]).then_inc(hidden.empty, 1)

            @block.tensor
            def _(pe):
                with pe.Fori(0, ne // 2) as i:
                    for h in range(2):
                        pe.wait_ge(loaded[h], i * (16 * n_loads) + 16 * n_loads)
                        pe.sem_inc(begun_pe, 1)
                        with pe.Fori(0, NB) as b:
                            turn = (i * 2 + h) * NB + b
                            pe.wait_ge(ready, turn + 1)
                            for s in range(2):
                                for m in range(hc):
                                    bank = hidden.fill(pe, turn)
                                    for c in range(2):
                                        mm = pe.matmul(bank[:, 0:HB], w1[:, h, c, m * P:(m + 1) * P],
                                                       xe[:, c, s * HB:(s + 1) * HB], start=c == 0, stop=c == 1)
                                    mm.then_inc(hidden.full, 1)
                            pe.wait_ge(hidden.empty, (turn + 2) * (2 * hc))
                            for u in range(4):
                                bank = outs.fill(pe, turn)
                                for j in range(2 * u, min(2 * u + 2, BT)):
                                    for m in range(hc):
                                        mm = pe.matmul(bank[:, (j - 2 * u) * D:(j - 2 * u + 1) * D],
                                                       ht[:, m, j * P:(j + 1) * P], w2[:, h, m, :],
                                                       start=m == 0, stop=m == hc - 1)
                                mm.then_inc(outs.full, 1)


def program(nc, a, out):
    part = lambda prefix: {k[len(prefix):]: v for k, v in a.items() if k.startswith(prefix)}
    g0, g1, f0, f1 = (part(p) for p in ("L0_gnn_", "L1_gnn_", "L0_ffn_", "L1_ffn_"))
    net = Net()
    tab1 = nc.dram_tensor("gcn_rows1", (NP, g0["W1"].shape[1]), F32).ap()
    tab2 = nc.dram_tensor("gcn_rows2", (NP, g0["W2"].shape[1]), F32).ap()
    gat_rows = nc.dram_tensor("gat_rows", (NP, GW), F32).ap()
    gat_logits = nc.dram_tensor("gat_logits", (NP, HEADS), F32).ap()
    x_mid = nc.dram_tensor("x_mid", (N, D), F32).ap()

    with ExitStack() as consts:
        alloc_constants(nc, net, consts)
        make_constants(nc, net)
        with ExitStack() as graph:
            alloc_edges(nc, net, graph)
            prepare_edges(nc, net, a["src"], a["dst"])
            alloc_nodes(nc, net, graph)
            with nc.sbuf_tensor("x0", [P, NT * D], F32) as net.x:
                load_nodes(nc, net, "load_x", a["x"], N)
                layer_stats(nc, net, "stats0")
                project(nc, net, "gcn1", "norm", D, g0["W1"], tab1.shape[1], tab1)
                gcn_pass(nc, net, "gcn1_pass", tab1, tab1.shape[1])
                project(nc, net, "gcn2", "relu", tab1.shape[1], g0["W2"], tab2.shape[1], tab2, bias=g0["b1"])
                gcn_pass(nc, net, "gcn2_pass", tab2, tab2.shape[1])
                fc_layers(nc, net, g0["b2"], g0["fc1_w"], g0["fc1_b"], g0["fc2_w"], g0["fc2_b"])
                layer_stats(nc, net, "stats1")
                small_mixture(nc, net, f0)
                layer_stats(nc, net, "stats2")
                project(nc, net, "gat0", "norm", D, g1["W0"], D, gat_rows,
                        logits=(g1["as0"], g1["ad0"], gat_logits))
                save_nodes(nc, net, "save_x", x_mid, N)
            for layer in range(3):
                if layer:
                    project(nc, net, f"gat{layer}", "copy", D, g1[f"W{layer}"], D, gat_rows,
                            logits=(g1[f"as{layer}"], g1[f"ad{layer}"], gat_logits))
                segment_max(nc, net, f"gat{layer}_max", gat_logits)
                gat_pass(nc, net, f"gat{layer}_pass", gat_rows)
                if layer < 2:
                    gat_finish(nc, net, f"gat{layer}_end", gat_rows, g1[f"b{layer}"], False)
            with nc.sbuf_tensor("x1", [P, NT * D], F32) as net.x:
                load_nodes(nc, net, "load_mid", x_mid, N)
                gat_finish(nc, net, "gat2_end", gat_rows, g1["b2"], True)
                save_nodes(nc, net, "save_mid", x_mid, N)
        with ExitStack() as last:
            alloc_mixture(nc, net, last, f1["Wr"].shape[1])
            load_nodes(nc, net, "load_last", x_mid, N)
            layer_stats(nc, net, "stats3")
            route_nodes(nc, net, f1)
            large_mixture(nc, net, f1)
            save_nodes(nc, net, "save_out", out, N)


def alloc_constants(nc, net, ctx):
    def sb(name, cols):
        return ctx.enter_context(nc.sbuf_tensor(name, [P, cols], F32))

    net.ident = sb("ident", P)
    net.iota = sb("iota", P)
    net.ones = sb("ones", P)
    net.part = sb("part", KC)


def alloc_mixture(nc, net, ctx, ne):
    def sb(name, shape):
        return ctx.enter_context(nc.sbuf_tensor(f"last_{name}", shape, F32))

    net.x = sb("x", [P, NT * D])
    net.xnt = sb("xnt", [P, 2, NP])
    net.weight = sb("weight", [P, ne, NT])
    net.mean = sb("mean", [P, NT])
    net.rstd = sb("rstd", [P, NT])


_INS = ['x', 'src', 'dst', 'L0_gnn_W1', 'L0_gnn_b1', 'L0_gnn_W2', 'L0_gnn_b2', 'L0_gnn_fc1_w', 'L0_gnn_fc1_b',
        'L0_gnn_fc2_w', 'L0_gnn_fc2_b', 'L0_ffn_sW1', 'L0_ffn_sb1', 'L0_ffn_sW2', 'L0_ffn_sb2', 'L0_ffn_sW3',
        'L0_ffn_sb3', 'L0_ffn_eW1', 'L0_ffn_eb1', 'L0_ffn_eW2', 'L0_ffn_eb2', 'L0_ffn_eW3', 'L0_ffn_eb3',
        'L0_ffn_gW', 'L0_ffn_gb', 'L1_gnn_W0', 'L1_gnn_as0', 'L1_gnn_ad0', 'L1_gnn_b0', 'L1_gnn_W1',
        'L1_gnn_as1', 'L1_gnn_ad1', 'L1_gnn_b1', 'L1_gnn_W2', 'L1_gnn_as2', 'L1_gnn_ad2', 'L1_gnn_b2',
        'L1_ffn_Wr', 'L1_ffn_br', 'L1_ffn_ln_g', 'L1_ffn_ln_b', 'L1_ffn_W1', 'L1_ffn_b1', 'L1_ffn_W2',
        'L1_ffn_b2']


def kernel(**inputs):
    import numpy as _np
    import concourse.bacc as _bacc
    from concourse import mybir as _mybir
    from concourse.bass_utils import run_bass_kernel_spmd as _run

    nc = _bacc.Bacc("TRN2", target_bir_lowering=False, num_devices=1)
    arrays, args = {}, {}
    for name in _INS:
        arr = _np.ascontiguousarray(inputs[name])
        arrays[f"in_{name}_dram"] = arr
        args[name] = nc.dram_tensor(f"in_{name}_dram", arr.shape, _mybir.dt.from_np(arr.dtype),
                                    kind="ExternalInput").ap()
    out = nc.dram_tensor("out_0_dram", (N, D), _mybir.dt.float32, kind="ExternalOutput").ap()
    program(nc, args, out)
    r = _run(nc, [arrays], core_ids=[0])
    return r.results[0]["out_0_dram"]
```

```python
from contextlib import ExitStack

import numpy as np

import concourse.bass as bass
from concourse import mybir
from concourse.alu_op_type import AluOpType as ALU

P = 128
N = 6250
E = 100000
D = 256
NT = (N + P - 1) // P
NP = NT * P
KT = (E + P - 1) // P
KC = (KT + P - 1) // P
KP = KC * P
NI = KT + NT - 1
HALF = 8
DEPTH = 4
STEPS = -(-NI // (DEPTH * HALF)) * DEPTH
NIP = STEPS * HALF
IC = NIP // 2
PAD_DST = 8191
BIG = 1.0e30
BT = 7
NB = NT // BT
BN = BT * P
HB = BN // 2
HEADS, HID = 4, 64
GW = D + HEADS
MW = D + 2 * HEADS
LN_EPS = 1e-5
EXPERTS = 8
BLOCK = 512
BLOCKS = (2 * NP + EXPERTS * (BLOCK - 1)) // BLOCK
BLOCKS += BLOCKS % 2
SLOT_COLS = BLOCKS * BLOCK // P
FAR = 2.0 ** 20

F32 = mybir.dt.float32
BF16 = mybir.dt.bfloat16
I32 = mybir.dt.int32
ACT = mybir.ActivationFunctionType
AX = mybir.AxisListType.X
assert NT % BT == 0 and IC <= 512 and HB <= 512


class Chain:

    def __init__(self, eng, sem):
        self.eng, self.sem, self.base, self.n = eng, sem, 0, 0

    def mark(self, ins):
        self.n += 1
        ins.then_inc(self.sem, 1)
        return ins

    def wait(self):
        self.eng.wait_ge(self.sem, self.base + self.n)

    def link(self, ins):
        self.mark(ins)
        self.wait()

    def enter(self, i, per_turn):
        self.before, self.per_turn = self.base + self.n, per_turn
        self.base, self.n = self.before + i * per_turn, 0

    def leave(self, turns):
        assert self.n == self.per_turn, (self.n, self.per_turn)
        self.base, self.n = self.before + turns * self.per_turn, 0


class Ring:

    def __init__(self, full, empty, banks, per_turn):
        self.full, self.empty, self.banks, self.per_turn = full, empty, banks, per_turn
        self.fill_n = self.drain_n = 0

    def give_credit(self, eng):
        eng.sem_inc(self.empty, self.per_turn)

    def fill(self, pe, i):
        u, r = self.fill_n % self.per_turn, len(self.banks)
        last = u - r + self.per_turn if u >= r else max(
            (v for v in range(self.per_turn) if v % r == u % r), default=u)
        pe.wait_ge(self.empty, i * self.per_turn + last + 1)
        self.fill_n += 1
        return self.banks[u % r]

    def settle(self, eng, i):
        eng.wait_ge(self.empty, (i + 1) * self.per_turn + (self.drain_n - 1) % self.per_turn + 1)

    def drain(self, eng, i):
        u = self.drain_n % self.per_turn
        eng.wait_ge(self.full, i * self.per_turn + u + 1)
        self.drain_n += 1
        return self.banks[u % len(self.banks)]


def refine_rsqrt(ch, dve, y, v, tmp):
    ch.link(dve.tensor_tensor(tmp, y, y, ALU.mult))
    ch.link(dve.scalar_tensor_tensor(out=tmp, in0=tmp, scalar=-0.5, in1=v, op0=ALU.mult, op1=ALU.mult))
    ch.link(dve.scalar_tensor_tensor(out=y, in0=tmp, scalar=1.5, in1=y, op0=ALU.add, op1=ALU.mult))


class Net:
    pass


def over(ap, n):
    ap = ap.unsqueeze(len(ap.shape))
    return ap.broadcast_to(list(ap.shape[:-1]) + [n])


def mid(ap, n):
    ap = ap.unsqueeze(1)
    return ap.broadcast_to([ap.shape[0], n, ap.shape[2]])


class Stage:

    def __init__(self, nc, name):
        self.nc, self.name, self.ctx, self.sems = nc, name, ExitStack(), []

    def __enter__(self):
        return self

    def __exit__(self, *a):
        self.nc.clear_and_free_semaphores(self.sems)
        self.nc.all_engine_barrier()
        self.ctx.close()

    def sb(self, name, shape, dt=F32):
        return self.ctx.enter_context(self.nc.sbuf_tensor(f"{self.name}_{name}", shape, dt))

    def ps(self, name, shape, dt=F32):
        return self.ctx.enter_context(self.nc.psum_tensor(f"{self.name}_{name}", shape, dt))

    def banks(self, n, name="bank"):
        return [self.ps(f"{name}{i}", [P, 512]) for i in range(n)]

    def sem(self, name):
        self.sems.append(self.nc.alloc_semaphore(f"{self.name}_{name}"))
        return self.sems[-1]


def make_constants(nc, net):
    with Stage(nc, "const") as st:
        made = st.sem("made")
        with nc.Block() as block:
            @block.gpsimd
            def _(pool):
                pool.iota(net.iota[:], [[1, P]], base=0, channel_multiplier=0,
                          allow_small_or_imprecise_dtypes=True)
                pool.iota(net.part[:], [[P, KC]], base=0, channel_multiplier=1,
                          allow_small_or_imprecise_dtypes=True)
                pool.memset(net.ones[:], 1.0)
                pool.memset(net.ident[:], 0.0).then_inc(made, 1)
                pool.wait_ge(made, 1)
                pool.affine_select(out=net.ident[:], in_=net.ident[:], compare_op=ALU.not_equal, fill=1.0,
                                   base=0, pattern=[[-1, P]], channel_multiplier=1)


def load_edges(dst_of, src):
    whole = E // (P * P)
    yield dst_of[:, 0:whole, :], src[0:whole * P * P].rearrange("(c p e) -> p c e", p=P, e=P)
    rows = (E - whole * P * P) // P
    yield dst_of[0:rows, whole, :], src[whole * P * P:(whole * P + rows) * P].rearrange("(p e) -> p e", e=P)
    at, left = (whole * P + rows) * P, E % P
    yield dst_of[rows:rows + 1, whole, 0:left], src[at:at + left].rearrange("(p e) -> p e", p=1)


def prepare_edges(nc, net, src, dst):
    whole = E // (P * P)
    with Stage(nc, "edges") as st:
        src_i, dst_i = st.sb("src_i", [P, KC, P], I32), st.sb("dst_i", [P, KC, P], I32)
        prev_i, next_i = st.sb("prev_i", [P, KC, P], I32), st.sb("next_i", [P, KC, P], I32)
        low_i = st.sb("low_i", [P, KC, P], I32)
        src_f, dst_f = st.sb("src_f", [P, KC, P]), st.sb("dst_f", [P, KC, P])
        first_f = st.sb("first_f", [P, KC, P])
        hi_f, lo_f = st.sb("hi_f", [P, KC, P]), st.sb("lo_f", [P, KC, P])
        hi_t, lo_t = st.sb("hi_t", [P, KP]), st.sb("lo_t", [P, KP])
        d0, d127 = st.sb("d0", [HEADS, KP], I32), st.sb("d127", [HEADS, KP], I32)
        whole_run, link = st.sb("whole_run", [HEADS, KP]), st.sb("link", [HEADS, KP])
        one_hi, one_lo = st.sb("one_hi", [P, 2, HALF, NT], BF16), st.sb("one_lo", [P, 2, HALF, P], BF16)
        zero = st.sb("zero", [P, P], BF16)
        count, per_tile = st.sb("count", [P, NT]), st.sb("per_tile", [P, 1])
        degree, spare = st.sb("degree", [P, NT]), st.sb("spare", [P, NT])
        below = st.sb("below", [P, P])
        kf_i, kf, first_item = st.sb("kf_i", [P, 1], I32), st.sb("kf", [P, 1]), st.sb("first_item", [P, 1])
        iota_i, begun = st.sb("iota_i", [P, NIP]), st.sb("begun", [NT, NIP])
        item_f = st.sb("item_f", [P, KC, NIP])
        t_all, k_all = st.sb("t_all", [P, NIP]), st.sb("k_all", [P, NIP])
        bank = st.banks(8)
        padded, loaded, rows = st.sem("padded"), st.sem("loaded"), st.sem("rows")
        ready, turned, copied = st.sem("ready"), st.sem("turned"), st.sem("copied")
        onehot, counted, chain, root = st.sem("onehot"), st.sem("counted"), st.sem("chain"), st.sem("root")
        pe_done, rooted = st.sem("pe_done"), st.sem("rooted")

        with nc.allow_non_contiguous_dma(reason="a few columns, once"), nc.Block() as block:
            @block.gpsimd
            def _(pool):
                pool.iota(iota_i[:], [[1, NIP]], base=0, channel_multiplier=0,
                          allow_small_or_imprecise_dtypes=True).then_inc(padded, 1)
                for t, v in ((src_i, 0), (dst_i, PAD_DST), (prev_i, PAD_DST), (next_i, PAD_DST),
                             (d0, PAD_DST), (d127, PAD_DST)):
                    pool.memset(t[:], v).then_inc(padded, 1)
                pool.memset(zero[:], 0.0).then_inc(padded, 1)

            @block.sync
            def _(sp):
                sp.wait_ge(padded, 7)
                n = 0
                for t, a in ((src_i, src), (dst_i, dst)):
                    for o, i in load_edges(t, a):
                        sp.dma_start(o, i).then_inc(loaded, 16)
                        n += 1
                sp.dma_start(d0[:, 0:KT], dst_column(dst, 0, KT)).then_inc(loaded, 16)
                sp.dma_start(d127[:, 0:E // P], dst_column(dst, P - 1, E // P)).then_inc(loaded, 16)
                sp.wait_ge(loaded, 16 * (n + 2))
                sp.dma_start(next_i[:, :, 0:P - 1], dst_i[:, :, 1:P]).then_inc(rows, 16)
                sp.dma_start(prev_i[:, :, 1:P], dst_i[:, :, 0:P - 1]).then_inc(rows, 16)
                sp.dma_start(prev_i[1:P, 0, 0:1], dst[0:(P - 1) * P].rearrange("(p e) -> p e", e=P)[:, P - 1:P])\
                    .then_inc(rows, 16)
                for c in range(1, KC):
                    n = min(P, KT - c * P)
                    sp.dma_start(prev_i[0:n, c, 0:1], bass.AP(dst.tensor, c * P * P - 1, [[P, n], [1, 1]]))\
                        .then_inc(rows, 16)

            @block.vector
            def _(dve):
                ch = Chain(dve, chain)
                dve.wait_ge(loaded, 16 * 8)
                dve.wait_ge(padded, 8)
                ch.link(dve.tensor_scalar(low_i[:], dst_i[:], 7, None, ALU.arith_shift_right))
                ch.link(dve.tensor_copy(hi_f[:], low_i[:]))
                ch.link(dve.tensor_scalar(low_i[:], dst_i[:], 127, None, ALU.bitwise_and))
                ch.link(dve.tensor_copy(lo_f[:], low_i[:]))
                ch.mark(dve.tensor_copy(dst_f[:], dst_i[:]))
                dve.tensor_copy(src_f[:], src_i[:]).then_inc(ready, 1)
                dve.wait_ge(ready, 1)
                for c in range(3 * KC):
                    dve.wait_ge(turned, c + 1)
                    t = (hi_t, lo_t, net.src_col)[c // KC]
                    dve.tensor_copy(t[:, c % KC * P:(c % KC + 1) * P], bank[c % 8][:, 0:P]).then_inc(copied, 1)
                dve.wait_ge(copied, 3 * KC)
                def one_hots(i, h, col):
                    dve.tensor_tensor(one_hi[:, h], over(hi_t[:, col], NT), mid(net.iota[:, 0:NT], HALF),
                                      ALU.is_equal)
                    dve.tensor_tensor(one_lo[:, h], over(lo_t[:, col], P), mid(net.iota[:], HALF),
                                      ALU.is_equal).then_inc(onehot, 1)

                for h in range(2):
                    one_hots(0, h, slice(h * HALF, (h + 1) * HALF))
                with dve.Fori(1, KT // (2 * HALF) + 1) as i:
                    for h in range(2):
                        dve.wait_ge(counted, 2 * i - 1 + h)
                        one_hots(i, h, bass.ds(i * (2 * HALF) + h * HALF, HALF))
                dve.wait_ge(pe_done, 1)
                ch.link(dve.tensor_copy(count[:], bank[0][:, 0:NT]))
                ch.link(dve.tensor_scalar(net.has_edge[:], count[:], 0.0, None, ALU.is_gt))
                ch.link(dve.tensor_scalar(degree[:], count[:], 1.0, None, ALU.add))
                ch.link(dve.reciprocal(net.dinv[:], degree[:]))
                dve.tensor_scalar(below[:], net.iota[:], net.part[:, 0:1], None, ALU.is_gt).then_inc(root, 1)
                dve.wait_ge(rooted, 1)
                refine_rsqrt(ch, dve, net.dinv[:], degree[:], spare[:])
                dve.wait_ge(pe_done, 2)
                dve.tensor_copy(per_tile[0:NT, :], bank[1][0:NT, 0:1]).then_inc(root, 1)
                dve.wait_ge(pe_done, 3)
                ch.link(dve.tensor_copy(kf_i[:], bank[2][:, 0:1]))
                ch.link(dve.tensor_scalar(kf_i[:], kf_i[:], 7, None, ALU.arith_shift_right))
                ch.link(dve.tensor_copy(kf[:], kf_i[:]))
                ch.link(dve.tensor_scalar(first_item[:], kf[:], float(KT - 1), net.part[:, 0:1], ALU.min, ALU.add))
                dve.tensor_scalar(begun[:], iota_i[0:NT, :], first_item[0:NT, 0:1], None, ALU.is_ge)\
                    .then_inc(root, 1)
                dve.wait_ge(pe_done, 4)
                for s in range(2):
                    ch.link(dve.tensor_scalar(t_all[:, s * IC:(s + 1) * IC], bank[3 + s][:, 0:IC], -1.0, None,
                                              ALU.add))
                ch.mark(dve.tensor_copy(net.t_of[:, 0:NIP], t_all[0:1, :]))
                ch.mark(dve.memset(net.t_of[:, NIP:NIP + HALF], NT - 1))
                ch.mark(dve.memset(net.dloc[:, NIP:NIP + HALF], -1.0))
                ch.link(dve.tensor_tensor(k_all[:], iota_i[:], t_all[:], ALU.subtract))
                dve.wait_ge(rows, 16 * (3 + KC - 1))
                ch.link(dve.tensor_tensor(first_f[:], dst_i[:], prev_i[:], ALU.not_equal))
                for c in range(KC):
                    last = dve.tensor_scalar(item_f[:, c, :], k_all[:], net.part[:, c:c + 1], None,
                                             ALU.is_equal)
                last.then_inc(root, 1)
                dve.wait_ge(root, 4)
                ch.mark(dve.tensor_copy(net.item_of[:], item_f[:]))
                ch.link(dve.tensor_scalar(net.run_start[:], first_f[:], -BIG, None, ALU.mult))
                ch.mark(dve.memset(net.run_start[:, :, 0:1], -BIG))
                ch.link(dve.tensor_tensor(net.run_end[:], dst_i[:], next_i[:], ALU.not_equal))
                ch.link(dve.tensor_scalar(net.run_end[:], net.run_end[:], -BIG, None, ALU.mult))
                ch.mark(dve.memset(net.run_end[:, :, P - 1:P], -BIG))
                for m, at in ((net.not_first_run, 0), (net.not_last_run, P - 1)):
                    ch.link(dve.tensor_tensor(m[:], dst_f[:], dst_f[:, :, at:at + 1].broadcast_to([P, KC, P]),
                                              ALU.not_equal))
                    ch.mark(dve.tensor_scalar(m[:], m[:], -BIG, None, ALU.mult))
                ch.link(dve.tensor_tensor(whole_run[:], d0[:], d127[:], ALU.not_equal))
                ch.link(dve.tensor_scalar(whole_run[:], whole_run[:], -BIG, None, ALU.mult))
                ch.link(dve.tensor_tensor(link[:, 1:KP], d0[:, 1:KP], d127[:, 0:KP - 1], ALU.not_equal))
                ch.link(dve.tensor_scalar(net.link_left[:, 1:KP], link[:, 1:KP], -BIG, None, ALU.mult))
                ch.mark(dve.tensor_scalar(net.link_right[:, 0:KP - 1], link[:, 1:KP], -BIG, None, ALU.mult))
                ch.mark(dve.memset(net.link_left[:, 0:1], -BIG))
                ch.mark(dve.memset(net.link_right[:, KP - 1:KP], -BIG))
                ch.mark(dve.memset(net.pass_left[:, 0:1], -BIG))
                ch.link(dve.memset(net.pass_right[:, KP - 1:KP], -BIG))
                ch.link(dve.tensor_tensor(net.pass_left[:, 1:KP], whole_run[:, 0:KP - 1],
                                          net.link_left[:, 1:KP], ALU.min))
                ch.link(dve.tensor_tensor(net.pass_right[:, 0:KP - 1], whole_run[:, 1:KP],
                                          net.link_right[:, 0:KP - 1], ALU.min))
                for n in range(6):
                    what, s = n // 2, n % 2
                    cols = slice(s * IC, (s + 1) * IC)
                    dve.wait_ge(pe_done, 5 + n)
                    b = bank[n % 8][:, 0:IC]
                    if what == 0:
                        ch.mark(dve.tensor_copy(net.src_of[:, cols], b))
                    elif what == 1:
                        ch.mark(dve.scalar_tensor_tensor(out=net.dloc[:, cols], in0=t_all[:, cols],
                                                         scalar=-float(P), in1=b, op0=ALU.mult, op1=ALU.add))
                    else:
                        ch.mark(dve.tensor_copy(net.first_of[:, cols], b))
                ch.wait()

            @block.scalar
            def _(act):
                act.wait_ge(root, 1)
                act.activation(net.dinv[:], net.dinv[:], ACT.Sqrt).then_inc(rooted, 1)

            @block.tensor
            def _(pe):
                pe.wait_ge(ready, 1)
                for c in range(3 * KC):
                    if c >= 8:
                        pe.wait_ge(copied, c - 7)
                    pe.transpose(bank[c % 8][:, 0:P], (hi_f, lo_f, src_f)[c // KC][:, c % KC, :], net.ident[:])\
                        .then_inc(turned, 1)
                pe.wait_ge(padded, 8)
                pe.wait_ge(copied, 3 * KC)
                counts = bank[0][:, 0:NT]
                pe.matmul(counts, zero[:], zero[:, 0:NT], start=True, stop=False, skip_group_check=True)
                with pe.Fori(0, KT // (2 * HALF) + 1) as i:
                    for h in range(2):
                        pe.wait_ge(onehot, 2 * i + h + 1)
                        for j in range(HALF):
                            mm = pe.matmul(counts, one_lo[:, h, j, :], one_hi[:, h, j, :], start=False,
                                           stop=False, skip_group_check=True)
                        mm.then_inc(counted, 1)
                pe.matmul(counts, zero[:], zero[:, 0:NT], start=False, stop=True, skip_group_check=True)\
                    .then_inc(pe_done, 1)
                pe.wait_ge(root, 1)
                pe.matmul(bank[1][0:NT, 0:1], count[:], net.ones[:, 0:1], start=True, stop=True)\
                    .then_inc(pe_done, 1)
                pe.wait_ge(root, 2)
                pe.matmul(bank[2][:, 0:1], below[0:NT, :], per_tile[0:NT, :], start=True, stop=True)\
                    .then_inc(pe_done, 1)
                pe.wait_ge(root, 3)
                for s in range(2):
                    mm = pe.matmul(bank[3 + s][:, 0:IC], net.ones[0:NT, :], begun[:, s * IC:(s + 1) * IC],
                                   start=True, stop=True)
                mm.then_inc(pe_done, 1)
                pe.wait_ge(root, 4)
                for n in range(6):
                    rows_of, s = (src_f, dst_f, first_f)[n // 2], n % 2
                    for c in range(KC):
                        mm = pe.matmul(bank[n][:, 0:IC], rows_of[:, c, :],
                                       item_f[:, c, s * IC:(s + 1) * IC], start=c == 0, stop=c == KC - 1)
                    mm.then_inc(pe_done, 1)


def dst_column(dst, at, n):
    return bass.AP(dst.tensor, dst.offset + at, [[0, HEADS], [P, n], [1, 1]])


def alloc_edges(nc, net, ctx):
    def sb(name, shape, dt=F32):
        return ctx.enter_context(nc.sbuf_tensor(name, shape, dt))

    net.has_edge = sb("has_edge", [P, NT])
    net.dinv = sb("dinv", [P, NT])
    net.src_col = sb("src_col", [P, KP], I32)
    net.src_of = sb("src_of", [P, NIP], I32)
    net.dloc = sb("dloc", [P, NIP + HALF])
    net.first_of = sb("first_of", [P, NIP], BF16)
    net.t_of = sb("t_of", [1, NIP + HALF], I32)
    net.item_of = sb("item_of", [P, KC, NIP], BF16)
    net.run_start = sb("run_start", [P, KC, P], BF16)
    net.run_end = sb("run_end", [P, KC, P], BF16)
    net.not_first_run = sb("not_first_run", [P, KC, P], BF16)
    net.not_last_run = sb("not_last_run", [P, KC, P], BF16)
    net.link_left = sb("link_left", [HEADS, KP], BF16)
    net.link_right = sb("link_right", [HEADS, KP], BF16)
    net.pass_left = sb("pass_left", [HEADS, KP], BF16)
    net.pass_right = sb("pass_right", [HEADS, KP], BF16)


def gather_rows(pool, table, slots, columns, index, gathered, indexed, go, freed, least):
    depth, n, width = slots.shape[1:]
    steps = columns.shape[1] // n

    def turn(i, first):
        for h in range(depth):
            q = i * depth + h
            if not first:
                pool.wait_ge(gathered[h], 16 * n * i)
                pool.wait_ge(freed, least(q))
            pool.tensor_copy(index[:, h, :], columns[:, bass.ds(q * n, n)]).then_inc(indexed, 1)
            pool.wait_ge(indexed, q + 1)
            pool.sem_inc(go, 1)
            for j in range(n):
                pool.indirect_dma_start(slots[:, h, j, :], None, table,
                                        bass.IndirectOffsetOnAxis(ap=index[:, h, j:j + 1], axis=0))\
                    .then_inc(gathered[h], 16)

    turn(0, True)
    with pool.Fori(1, steps // depth) as i:
        turn(i, False)


def gcn_pass(nc, net, name, table, width):
    with Stage(nc, name) as st:
        index = st.sb("index", [P, 2, HALF], I32)
        rows, onehot = st.sb("rows", [P, 2, HALF, width]), st.sb("onehot", [P, 2, HALF, P])
        bank = st.banks(HALF)
        gathered = [st.sem("gathered0"), st.sem("gathered1")]
        indexed, go, made, summed, added = (st.sem(x) for x in ("indexed", "go", "made", "summed", "added"))

        with nc.Block() as block:
            @block.gpsimd
            def _(pool):
                gather_rows(pool, table, rows, net.src_of, index, gathered, indexed, go, summed,
                            lambda q: (q - 1) * HALF)

            @block.vector
            def _(dve):
                tile = [dve.alloc_register(f"{name}_t{j}") for j in range(HALF)]

                def one_hot(col, h):
                    dve.tensor_tensor(onehot[:, h], over(net.dloc[:, col], P), mid(net.iota[:], HALF),
                                      ALU.is_equal).then_inc(made, 1)

                def accumulate(q, first):
                    dve.load(tile, net.t_of[0:1, bass.ds(q * HALF, HALF)])
                    for j in range(HALF):
                        dve.wait_ge(summed, q * HALF + j + 1)
                        if not (first and j == 0):
                            dve.wait_ge(added, q * HALF + j)
                        acc = net.acc[:, bass.ds(dve.snap(tile[j], min_val=0, max_val=NT - 1) * MW, width)]
                        dve.tensor_tensor(acc, acc, bank[j][:, 0:width], ALU.add).then_inc(added, 1)

                one_hot(slice(0, HALF), 0)
                one_hot(slice(HALF, 2 * HALF), 1)
                accumulate(0, True)
                with dve.Fori(0, STEPS // 2 - 1) as i:
                    for h in range(2):
                        one_hot(bass.ds(i * (2 * HALF) + (2 + h) * HALF, HALF), h)
                        accumulate(i * 2 + h + 1, False)
                accumulate(STEPS - 1, False)

            @block.tensor
            def _(pe):
                def turn(i, first):
                    for h in range(2):
                        pe.wait_ge(made, i * 2 + h + 1)
                        pe.wait_ge(gathered[h], P * i + P)
                        for j in range(HALF):
                            if not first or h:
                                pe.wait_ge(added, (i * 2 + h - 1) * HALF + j + 1)
                            pe.matmul(bank[j][:, 0:width], onehot[:, h, j, :], rows[:, h, j, :],
                                      start=True, stop=True).then_inc(summed, 1)

                turn(0, True)
                with pe.Fori(1, STEPS // 2) as i:
                    turn(i, False)


def layer_stats(nc, net, name, twice=False):
    with Stage(nc, name) as st:
        stats, aggr = st.sb("stats", [P, NT, 6]), st.sb("aggr", [P, NT, 2])
        var, spare = st.sb("var", [P, NT]), st.sb("spare", [P, NT])
        chain, ready, rooted = st.sem("chain"), st.sem("ready"), st.sem("rooted")
        with nc.Block() as block:
            @block.vector
            def _(dve):
                ch = Chain(dve, chain)
                for t in range(NT):
                    ch.mark(dve.bn_stats(stats[:, t, :], net.x[:, t * D:(t + 1) * D]))
                ch.wait()
                for t in range(NT):
                    ch.mark(dve.bn_aggr(aggr[:, t, :], stats[:, t, :]))
                ch.wait()
                ch.mark(dve.tensor_copy(net.mean[:], aggr[:, :, 0]))
                ch.link(dve.tensor_scalar(var[:], aggr[:, :, 1], LN_EPS, None, ALU.add))
                dve.reciprocal(net.rstd[:], var[:]).then_inc(ready, 1)
                dve.wait_ge(rooted, 1)
                refine_rsqrt(ch, dve, net.rstd[:], var[:], spare[:])
                if twice:
                    ch.link(dve.tensor_tensor(var[:], net.rstd[:], net.rstd[:], ALU.mult))
                    ch.link(dve.tensor_tensor(var[:], var[:], aggr[:, :, 1], ALU.mult))
                    ch.link(dve.tensor_scalar(var[:], var[:], LN_EPS, None, ALU.add))
                    dve.reciprocal(net.rstd2[:], var[:]).then_inc(ready, 1)
                    dve.wait_ge(rooted, 2)
                    refine_rsqrt(ch, dve, net.rstd2[:], var[:], spare[:])

            @block.scalar
            def _(act):
                act.wait_ge(ready, 1)
                act.activation(net.rstd[:], net.rstd[:], ACT.Sqrt).then_inc(rooted, 1)
                if twice:
                    act.wait_ge(ready, 2)
                    act.activation(net.rstd2[:], net.rstd2[:], ACT.Sqrt).then_inc(rooted, 1)


def project(nc, net, name, prep, w_in, weight, w_out, table, bias=None, logits=None):
    kc = w_in // P
    per_in = -(-kc * BT // 4)
    per = 512 // w_out if w_out > P else 4
    per_out = -(-BT // per)
    tw = w_out + (HEADS if logits else 0)
    with Stage(nc, name) as st:
        xn, xt = st.sb("xn", [P, BT, w_in]), st.sb("xt", [P, kc, BN])
        w_sb = st.sb("w", [P, kc, w_out])
        b_sb = st.sb("b", [P, w_in]) if bias is not None else None
        outb = st.sb("out", [P, BT, tw])
        part = st.sb("part", [P, 3, BT])
        if logits:
            a_sb, prod = st.sb("a", [P, 2, w_out]), st.sb("prod", [P, BT, w_out])
            lg = st.sb("lg", [P, BT, 2 * HEADS])
        loaded, xn_ready, xt_ready = st.sem("loaded"), st.sem("xn_ready"), st.sem("xt_ready")
        chain, out_ready, stored, out_free = (st.sem(x) for x in ("chain", "out_ready", "stored", "out_free"))
        turned = Ring(st.sem("turned"), st.sem("turned_free"), st.banks(4, "t"), per_in)
        product = Ring(st.sem("product"), st.sem("product_free"), st.banks(4, "m"), per_out)
        n_loads = 1 + (bias is not None) + 2 * bool(logits)

        with nc.allow_non_contiguous_dma(reason="weights, once"), nc.Block() as block:
            @block.sync
            def _(sp):
                sp.dma_start(w_sb[:], weight.rearrange("(c k) m -> k c m", k=P)).then_inc(loaded, 16)
                if bias is not None:
                    sp.dma_start(b_sb[:], bias.partition_broadcast(P)).then_inc(loaded, 16)
                if logits:
                    for s in range(2):
                        sp.dma_start(a_sb[:, s, :], logits[s].rearrange("h f -> (h f)").partition_broadcast(P))\
                            .then_inc(loaded, 16)
                sp.sem_inc(out_free, 1)
                view = table.rearrange("(t p) w -> p t w", p=P)
                with sp.Fori(0, NB) as b:
                    sp.wait_ge(out_ready, b + 1)
                    sp.dma_start(view[:, bass.ds(b * BT, BT), :], outb[:]).then_inc(stored, 16)
                    if logits:
                        sp.dma_start(logits[2].rearrange("(t p) w -> p t w", p=P)[:, bass.ds(b * BT, BT), :],
                                     lg[:, :, 0:HEADS]).then_inc(stored, 16)
                    sp.wait_ge(stored, (b + 1) * (32 if logits else 16))
                    sp.sem_inc(out_free, 1)

            @block.vector
            def _(dve):
                ch = Chain(dve, chain)
                product.give_credit(dve)
                dve.wait_ge(loaded, 16 * n_loads)

                def prepare(b):
                    if prep == "norm":
                        ch.mark(dve.tensor_copy(part[:, 0, :], net.mean[:, bass.ds(b * BT, BT)]))
                        ch.link(dve.tensor_copy(part[:, 1, :], net.rstd[:, bass.ds(b * BT, BT)]))
                        for j in range(BT):
                            last = dve.tensor_scalar(xn[:, j, :], net.x[:, bass.ds(b * (BT * D) + j * D, D)],
                                                     part[:, 0, j:j + 1], part[:, 1, j:j + 1],
                                                     ALU.subtract, ALU.mult)
                    elif prep == "relu":
                        ch.link(dve.tensor_copy(part[:, 0, :], net.dinv[:, bass.ds(b * BT, BT)]))
                        for j in range(BT):
                            ch.mark(dve.scalar_tensor_tensor(
                                out=xn[:, j, :], in0=net.acc[:, bass.ds(b * (BT * MW) + j * MW, w_in)],
                                scalar=part[:, 0, j:j + 1], in1=b_sb[:], op0=ALU.mult, op1=ALU.add))
                        ch.wait()
                        last = dve.tensor_scalar(xn[:], xn[:], 0.0, None, ALU.max)
                    else:
                        for j in range(BT):
                            last = dve.tensor_copy(xn[:, j, :], net.acc[:, bass.ds(b * (BT * MW) + j * MW, w_in)])
                    last.then_inc(xn_ready, 1)

                marks_prep = {"norm": 2, "relu": 1 + BT, "copy": 0}[prep]

                def finish(b):
                    dve.wait_ge(out_free, b + 1)
                    if not logits:
                        ch.link(dve.tensor_copy(part[:, 2, :], net.dinv[:, bass.ds(b * BT, BT)]))
                    for u in range(per_out):
                        bank = product.drain(dve, b)
                        j0, n = u * per, min(per, BT - u * per)
                        src = bank[:, 0:n * w_out].rearrange("p (j w) -> p j w", w=w_out)
                        if logits:
                            dve.tensor_copy(outb[:, j0:j0 + n, 0:w_out], src).then_inc(product.empty, 1)
                        else:
                            dve.tensor_tensor(outb[:, j0:j0 + n, :], src, over(part[:, 2, j0:j0 + n], w_out),
                                              ALU.mult).then_inc(product.empty, 1)
                    dve.wait_ge(product.empty, (b + 2) * per_out)
                    if logits:
                        for s in range(2):
                            ch.link(dve.tensor_tensor(prod[:], outb[:, :, 0:w_out], mid(a_sb[:, s, :], BT),
                                                      ALU.mult))
                            ch.link(dve.tensor_reduce(lg[:, :, s * HEADS:(s + 1) * HEADS],
                                                      prod[:].rearrange("p j (h f) -> p j h f", f=HID), AX,
                                                      ALU.add))
                        ch.mark(dve.tensor_copy(net.logit[:, bass.ds(b * (BT * 2 * HEADS), BT * 2 * HEADS)],
                                                lg[:].rearrange("p j a -> p (j a)")))
                        dve.tensor_copy(outb[:, :, w_out:tw], lg[:, :, 0:HEADS]).then_inc(out_ready, 1)
                    else:
                        for j in range(BT):
                            last = dve.tensor_copy(net.acc[:, bass.ds(b * (BT * MW) + j * MW, w_out)],
                                                   outb[:, j, :])
                        last.then_inc(out_ready, 1)

                marks_finish = 5 if logits else 1
                prepare(0)
                with dve.Fori(0, NB - 1) as b:
                    ch.enter(b, marks_prep + marks_finish)
                    dve.wait_ge(turned.full, (b + 1) * per_in)
                    prepare(b + 1)
                    finish(b)
                    ch.leave(NB - 1)
                finish(NB - 1)
                if logits:
                    dve.wait_ge(turned.full, NB * per_in)
                    dve.memset(net.acc[:], 0.0)

            @block.scalar
            def _(act):
                turned.give_credit(act)
                flat = xt[:].rearrange("p c n -> p (c n)")
                with act.Fori(0, NB) as b:
                    for u in range(per_in):
                        n = min(4, kc * BT - 4 * u) * P
                        bank = turned.drain(act, b)
                        act.activation(flat[:, u * 512:u * 512 + n], bank[:, 0:n], ACT.Copy)\
                            .then_inc(turned.empty, 1)

            @block.tensor
            def _(pe):
                pe.wait_ge(loaded, 16 * n_loads)
                with pe.Fori(0, NB) as b:
                    pe.wait_ge(xn_ready, b + 1)
                    for u in range(per_in):
                        bank = turned.fill(pe, b)
                        for m in range(4 * u, min(4 * u + 4, kc * BT)):
                            mm = pe.transpose(bank[:, m % 4 * P:(m % 4 + 1) * P],
                                              xn[:, m % BT, m // BT * P:(m // BT + 1) * P], net.ident[:])
                        mm.then_inc(turned.full, 1)
                    pe.wait_ge(turned.empty, (b + 2) * per_in)
                    for u in range(per_out):
                        bank = product.fill(pe, b)
                        for j in range(u * per, min(u * per + per, BT)):
                            at = (j - u * per) * w_out
                            for c in range(kc):
                                mm = pe.matmul(bank[:, at:at + w_out], xt[:, c, j * P:(j + 1) * P],
                                               w_sb[:, c, :], start=c == 0, stop=c == kc - 1)
                        mm.then_inc(product.full, 1)


def alloc_nodes(nc, net, ctx):
    def sb(name, shape, dt=F32):
        return ctx.enter_context(nc.sbuf_tensor(name, shape, dt))

    net.acc = sb("acc", [P, NT * MW])
    net.logit = sb("logit", [P, NT * 2 * HEADS])
    net.mean = sb("mean", [P, NT])
    net.rstd = sb("rstd", [P, NT])
    net.peak = sb("peak", [P, NIP, HEADS])


def load_nodes(nc, net, name, x, n):
    with Stage(nc, name) as st:
        cleared, loaded = st.sem("cleared"), st.sem("loaded")
        full = n // P
        with nc.Block() as block:
            @block.gpsimd
            def _(pool):
                pool.memset(net.x[:, (NT - 1) * D:NT * D], 0.0).then_inc(cleared, 1)

            @block.sync
            def _(sp):
                sp.wait_ge(cleared, 1)
                for t0 in range(0, full, BT):
                    t1 = min(full, t0 + BT)
                    sp.dma_start(net.x[:, t0 * D:t1 * D].rearrange("p (t w) -> p t w", w=D),
                                 x[t0 * P:t1 * P, :].rearrange("(t p) w -> p t w", p=P)).then_inc(loaded, 16)
                if n % P:
                    sp.dma_start(net.x[0:n % P, full * D:(full + 1) * D], x[full * P:n, :]).then_inc(loaded, 16)
                sp.wait_ge(loaded, 16 * (-(-full // BT) + (n % P > 0)))


def save_nodes(nc, net, name, x, n):
    with Stage(nc, name) as st:
        saved = st.sem("saved")
        full = n // P
        with nc.Block() as block:
            @block.sync
            def _(sp):
                for t0 in range(0, full, BT):
                    t1 = min(full, t0 + BT)
                    sp.dma_start(x[t0 * P:t1 * P, :].rearrange("(t p) w -> p t w", p=P),
                                 net.x[:, t0 * D:t1 * D].rearrange("p (t w) -> p t w", w=D)).then_inc(saved, 16)
                if n % P:
                    sp.dma_start(x[full * P:n, :], net.x[0:n % P, full * D:(full + 1) * D]).then_inc(saved, 16)
                sp.wait_ge(saved, 16 * (-(-full // BT) + (n % P > 0)))


def fc_layers(nc, net, bias, w1, b1, w2, b2):
    h, m = w1.shape
    with Stage(nc, "fc") as st:
        bias_sb, part = st.sb("bias", [P, h]), st.sb("part", [P, BT])
        w1_sb, w2_sb = st.sb("w1", [h, m]), st.sb("w2", [m, D])
        b1_sb, b2_sb = st.sb("b1", [m, 1]), st.sb("b2", [1, D])
        rows, ht, ft = st.sb("rows", [P, BT, h]), st.sb("ht", [h, BN]), st.sb("ft", [m, BN])
        loaded, ready, chain, begun = st.sem("loaded"), st.sem("ready"), st.sem("chain"), st.sem("begun")
        cols = Ring(st.sem("cols"), st.sem("cols_free"), st.banks(4, "c"), 4)
        outs = Ring(st.sem("outs"), st.sem("outs_free"), st.banks(4, "o"), 4)

        with nc.allow_non_contiguous_dma(reason="a bias, once"), nc.Block() as block:
            @block.sync
            def _(sp):
                for o, i in ((bias_sb, bias.partition_broadcast(P)), (w1_sb, w1), (w2_sb, w2),
                             (b1_sb, b1.rearrange("(k o) -> k o", o=1)), (b2_sb, b2.rearrange("(o k) -> o k", o=1))):
                    sp.dma_start(o[:], i).then_inc(loaded, 16)

            @block.vector
            def _(dve):
                ch = Chain(dve, chain)
                outs.give_credit(dve)
                dve.wait_ge(loaded, 80)

                def prepare(b):
                    ch.link(dve.tensor_copy(part[:], net.dinv[:, bass.ds(b * BT, BT)]))
                    for j in range(BT):
                        ch.mark(dve.scalar_tensor_tensor(
                            out=rows[:, j, :], in0=net.acc[:, bass.ds(b * (BT * MW) + j * MW, h)],
                            scalar=part[:, j:j + 1], in1=bias_sb[:], op0=ALU.mult, op1=ALU.add))
                    ch.wait()
                    dve.tensor_scalar(rows[:], rows[:], 0.0, None, ALU.max).then_inc(ready, 1)

                def finish(b):
                    for u in range(4):
                        bank = outs.drain(dve, b)
                        n = min(2, BT - 2 * u)
                        x = net.x[:, bass.ds(b * (BT * D) + 2 * u * D, n * D)]
                        dve.tensor_tensor(x, x, bank[:, 0:n * D], ALU.add).then_inc(outs.empty, 1)

                prepare(0)
                with dve.Fori(0, NB - 1) as b:
                    ch.enter(b, 1 + BT)
                    dve.wait_ge(cols.full, b * 4 + 2)
                    prepare(b + 1)
                    finish(b)
                    ch.leave(NB - 1)
                finish(NB - 1)

            @block.scalar
            def _(act):
                cols.give_credit(act)
                act.wait_ge(loaded, 80)
                with act.Fori(0, NB) as b:
                    for u in range(2):
                        n = min(4, BT - 4 * u) * P
                        act.activation(ht[:, u * 512:u * 512 + n], cols.drain(act, b)[0:h, 0:n], ACT.Copy)\
                            .then_inc(cols.empty, 1)
                    for u in range(2):
                        act.activation(ft[:, u * HB:(u + 1) * HB], cols.drain(act, b)[0:m, 0:HB], ACT.Identity,
                                       bias=b1_sb[:]).then_inc(cols.empty, 1)

            @block.tensor
            def _(pe):
                pe.wait_ge(loaded, 80)
                with pe.Fori(0, NB) as b:
                    pe.wait_ge(ready, b + 1)
                    for u in range(2):
                        bank = cols.fill(pe, b)
                        pe.sem_inc(begun, 1)
                        for j in range(4 * u, min(4 * u + 4, BT)):
                            mm = pe.transpose(bank[0:h, j % 4 * P:(j % 4 + 1) * P], rows[:, j, :], net.ident[:])
                        mm.then_inc(cols.full, 1)
                    pe.wait_ge(cols.empty, b * 4 + 4 + 2)
                    for u in range(2):
                        pe.matmul(cols.fill(pe, b)[0:m, 0:HB], w1_sb[:], ht[:, u * HB:(u + 1) * HB],
                                  start=True, stop=True).then_inc(cols.full, 1)
                    pe.wait_ge(cols.empty, b * 4 + 4 + 4)
                    for u in range(4):
                        bank = outs.fill(pe, b)
                        for j in range(2 * u, min(2 * u + 2, BT)):
                            o = bank[:, (j - 2 * u) * D:(j - 2 * u + 1) * D]
                            pe.matmul(o, ft[:, j * P:(j + 1) * P], w2_sb[:], start=True, stop=False)
                            mm = pe.matmul(o, net.ones[0:1, :], b2_sb[:], start=False, stop=True)
                        mm.then_inc(outs.full, 1)


class Gate:
    marks = 15

    def __init__(self, st, ne, again):
        self.ne, self.again = ne, again
        self.p, self.q = st.sb("gate_p", [P, BT, ne]), st.sb("gate_q", [P, BT, ne])
        self.ex, self.ex2 = st.sb("gate_ex", [P, BT, ne]), st.sb("gate_ex2", [P, BT, ne])
        self.row, self.low = st.sb("gate_row", [P, BT]), st.sb("gate_low", [P, ne, ne])
        self.above, self.same = st.sb("gate_above", [P, BT, ne, ne]), st.sb("gate_same", [P, BT, ne, ne])
        self.bias = st.sb("gate_bias", [P, ne])
        self.shifted, self.raised = st.sem("gate_shifted"), st.sem("gate_raised")
        self.calls = 1 + again
        self.chosen = None if again else st.sb("gate_chosen", [P, BT, ne])

    def order(self, ch, dve, net):
        for e in range(self.ne):
            ch.mark(dve.tensor_scalar(self.low[:, e, :], net.iota[:, 0:self.ne], float(e), None, ALU.is_lt))
        ch.wait()

    def weights(self, ch, dve, i, logits, drained):
        p, q, row, ne = self.p, self.q, self.row, self.ne
        dve.tensor_tensor(p[:], logits.rearrange("p (j e) -> p j e", e=ne), mid(self.bias[:], BT), ALU.add)\
            .then_inc(drained.empty, 1)
        drained.settle(dve, i)
        ch.link(dve.tensor_reduce(row[:], p[:], AX, ALU.max))
        dve.tensor_tensor(p[:], p[:], over(row[:], ne), ALU.subtract).then_inc(self.shifted, 1)
        dve.wait_ge(self.raised, i * self.calls + 1)
        ch.link(dve.tensor_reduce(row[:], self.ex[:], AX, ALU.add))
        ch.link(dve.reciprocal(row[:], row[:]))
        ch.link(dve.tensor_tensor(p[:], self.ex[:], over(row[:], ne), ALU.mult))
        one, other = p[:].unsqueeze(3).broadcast_to([P, BT, ne, ne]), p[:].unsqueeze(2).broadcast_to([P, BT, ne, ne])
        ch.mark(dve.tensor_tensor(self.above[:], other, one, ALU.is_gt))
        ch.link(dve.tensor_tensor(self.same[:], other, one, ALU.is_equal))
        ch.link(dve.tensor_tensor(self.same[:], self.same[:],
                                  self.low[:].unsqueeze(1).broadcast_to([P, BT, ne, ne]), ALU.mult))
        ch.link(dve.tensor_tensor(self.above[:], self.above[:], self.same[:], ALU.add))
        ch.link(dve.tensor_reduce(q[:], self.above[:], AX, ALU.add))
        ch.link(dve.tensor_scalar(q[:], q[:], 1.5, None, ALU.is_lt))
        if self.again:
            ch.link(dve.tensor_reduce(row[:], p[:], AX, ALU.max))
            dve.tensor_tensor(p[:], p[:], over(row[:], ne), ALU.subtract).then_inc(self.shifted, 1)
            dve.wait_ge(self.raised, i * self.calls + 2)
            ch.link(dve.tensor_tensor(q[:], q[:], self.ex2[:], ALU.mult))
        else:
            ch.link(dve.tensor_copy(self.chosen[:], q[:]))
            ch.link(dve.tensor_tensor(q[:], q[:], p[:], ALU.mult))
        ch.link(dve.tensor_reduce(row[:], q[:], AX, ALU.add))
        ch.link(dve.reciprocal(row[:], row[:]))
        ch.link(dve.tensor_tensor(q[:], q[:], over(row[:], ne), ALU.mult))

    def raise_(self, act, i):
        act.wait_ge(self.shifted, i * self.calls + 1)
        act.activation(self.ex[:], self.p[:], ACT.Exp).then_inc(self.raised, 1)
        if self.again:
            act.wait_ge(self.shifted, i * self.calls + 2)
            act.activation(self.ex2[:], self.p[:], ACT.Exp).then_inc(self.raised, 1)


def small_mixture(nc, net, w):
    ne, e1, e2 = w["eW2"].shape
    s1, s2 = w["sW2"].shape
    sc = s1 // P
    with Stage(nc, "mix") as st:
        gate = Gate(st, ne, True)
        part = st.sb("part", [P, 2, BT])
        xn, xt = st.sb("xn", [P, BT, D]), st.sb("xt", [P, 2, BN])
        gw = st.sb("gw", [P, 2, ne])
        sw1, sw2, sw3 = st.sb("sw1", [P, 2, s1]), st.sb("sw2", [P, sc, s2]), st.sb("sw3", [s2, D])
        sb1, sb2, sb3 = st.sb("sb1", [P, sc]), st.sb("sb2", [s2, 1]), st.sb("sb3", [1, D])
        ew1, ew2, ew3 = st.sb("ew1", [P, ne, 2, e1]), st.sb("ew2", [e1, ne, e2]), st.sb("ew3", [e2, ne, D])
        eb1, eb2, eb3 = st.sb("eb1", [e1, ne]), st.sb("eb2", [e2, ne]), st.sb("eb3", [ne, D])
        st1, st2 = st.sb("st1", [P, sc, HB]), st.sb("st2", [s2, BN])
        h1, h2 = st.sb("h1", [e1, BN]), st.sb("h2", [e2, BN])
        wt = st.sb("wt", [ne, BN])
        loaded, ready, chain, weighed = st.sem("loaded"), st.sem("ready"), st.sem("chain"), st.sem("weighed")
        n_cols = 4 + 2 * (sc + 1) + 2 + 4 * ne
        cols = Ring(st.sem("cols"), st.sem("cols_free"), st.banks(4, "c"), n_cols)
        outs = Ring(st.sem("outs"), st.sem("outs_free"), st.banks(4, "o"), 1 + 4 + 4 * ne)
        loads = [
            (gw[:], w["gW"].rearrange("(c k) e -> k c e", k=P)), (gate.bias[:], w["gb"].partition_broadcast(P)),
            (sw1[:], w["sW1"].rearrange("(c k) m -> k c m", k=P)), (sw2[:], w["sW2"].rearrange("(c k) m -> k c m", k=P)),
            (sw3[:], w["sW3"]), (sb1[:], w["sb1"].rearrange("(c k) -> k c", k=P)),
            (sb2[:], w["sb2"].rearrange("(k o) -> k o", o=1)), (sb3[:], w["sb3"].rearrange("(o k) -> o k", o=1)),
            (ew2[:], w["eW2"].rearrange("e k m -> k e m")), (ew3[:], w["eW3"].rearrange("e k m -> k e m")),
            (eb1[:], w["eb1"].rearrange("e k -> k e")), (eb2[:], w["eb2"].rearrange("e k -> k e")),
            (eb3[:], w["eb3"]),
        ] + [(ew1[:, e], w["eW1"][e].rearrange("(c k) m -> k c m", k=P)) for e in range(ne)]

        with nc.allow_non_contiguous_dma(reason="biases, once"), nc.Block() as block:
            @block.sync
            def _(sp):
                for o, i in loads:
                    sp.dma_start(o, i).then_inc(loaded, 16)

            @block.vector
            def _(dve):
                ch = Chain(dve, chain)
                outs.give_credit(dve)
                dve.wait_ge(loaded, 16 * len(loads))
                gate.order(ch, dve, net)

                def prepare(b):
                    ch.mark(dve.tensor_copy(part[:, 0, :], net.mean[:, bass.ds(b * BT, BT)]))
                    ch.link(dve.tensor_copy(part[:, 1, :], net.rstd[:, bass.ds(b * BT, BT)]))
                    for j in range(BT):
                        last = dve.tensor_scalar(xn[:, j, :], net.x[:, bass.ds(b * (BT * D) + j * D, D)],
                                                 part[:, 0, j:j + 1], part[:, 1, j:j + 1], ALU.subtract, ALU.mult)
                    last.then_inc(ready, 1)

                def finish(b, before):
                    gate.weights(ch, dve, b, outs.drain(dve, b)[:, 0:BT * ne], outs)
                    dve.sem_inc(weighed, 1)
                    before()
                    for e in range(-1, ne):
                        for u in range(4):
                            bank = outs.drain(dve, b)
                            n = min(2, BT - 2 * u)
                            if e < 0:
                                x = net.x[:, bass.ds(b * (BT * D) + 2 * u * D, n * D)]
                                dve.tensor_tensor(x, x, bank[:, 0:n * D], ALU.add).then_inc(outs.empty, 1)
                                continue
                            for j in range(2 * u, 2 * u + n):
                                x = net.x[:, bass.ds(b * (BT * D) + j * D, D)]
                                last = dve.scalar_tensor_tensor(
                                    out=x, in0=bank[:, (j - 2 * u) * D:(j - 2 * u + 1) * D],
                                    scalar=gate.q[:, j, e:e + 1], in1=x, op0=ALU.mult, op1=ALU.add)
                            last.then_inc(outs.empty, 1)
                        outs.settle(dve, b)

                def ahead(b):
                    dve.wait_ge(cols.full, b * n_cols + 4)
                    prepare(b + 1)

                prepare(0)
                with dve.Fori(0, NB - 1) as b:
                    ch.enter(b, Gate.marks + 2)
                    finish(b, lambda: ahead(b))
                    ch.leave(NB - 1)
                finish(NB - 1, lambda: None)

            @block.scalar
            def _(act):
                cols.give_credit(act)
                act.wait_ge(loaded, 16 * len(loads))
                flat = xt[:].rearrange("p c n -> p (c n)")

                def relu(b, out, k, bias, n=HB):
                    act.activation(out, cols.drain(act, b)[0:k, 0:n], ACT.Relu, bias=bias).then_inc(cols.empty, 1)

                with act.Fori(0, NB) as b:
                    for u in range(4):
                        n = min(4, 2 * BT - 4 * u) * P
                        act.activation(flat[:, u * 512:u * 512 + n], cols.drain(act, b)[:, 0:n], ACT.Copy)\
                            .then_inc(cols.empty, 1)
                    for s in range(2):
                        for c in range(sc):
                            relu(b, st1[:, c, :], P, sb1[:, c:c + 1])
                        relu(b, st2[:, s * HB:(s + 1) * HB], s2, sb2[:])
                    gate.raise_(act, b)
                    for u in range(2):
                        n = min(4, BT - 4 * u) * P
                        act.activation(wt[:, u * 512:u * 512 + n], cols.drain(act, b)[0:ne, 0:n], ACT.Copy)\
                            .then_inc(cols.empty, 1)
                    for e in range(ne):
                        for s in range(2):
                            relu(b, h1[:, s * HB:(s + 1) * HB], e1, eb1[:, e:e + 1])
                        for s in range(2):
                            relu(b, h2[:, s * HB:(s + 1) * HB], e2, eb2[:, e:e + 1])

            @block.tensor
            def _(pe):
                pe.wait_ge(loaded, 16 * len(loads))

                def columns(b, out, lhs, rhs):
                    bank = cols.fill(pe, b)
                    for c, (l, r) in enumerate(zip(lhs, rhs)):
                        mm = pe.matmul(bank[0:out, 0:HB], l, r, start=c == 0, stop=c == len(lhs) - 1)
                    mm.then_inc(cols.full, 1)

                def drained(b, n):
                    pe.wait_ge(cols.empty, (b + 1) * n_cols + n)

                with pe.Fori(0, NB) as b:
                    pe.wait_ge(ready, b + 1)
                    for u in range(4):
                        bank = cols.fill(pe, b)
                        for m in range(4 * u, min(4 * u + 4, 2 * BT)):
                            mm = pe.transpose(bank[:, m % 4 * P:(m % 4 + 1) * P],
                                              xn[:, m % BT, m // BT * P:(m // BT + 1) * P], net.ident[:])
                        mm.then_inc(cols.full, 1)
                    drained(b, 4)
                    bank = outs.fill(pe, b)
                    for j in range(BT):
                        for c in range(2):
                            mm = pe.matmul(bank[:, j * ne:(j + 1) * ne], xt[:, c, j * P:(j + 1) * P], gw[:, c, :],
                                           start=c == 0, stop=c == 1)
                    mm.then_inc(outs.full, 1)
                    n = 4
                    for s in range(2):
                        xs = [xt[:, c, s * HB:(s + 1) * HB] for c in range(2)]
                        for m in range(sc):
                            columns(b, P, [sw1[:, c, m * P:(m + 1) * P] for c in range(2)], xs)
                        n += sc
                        drained(b, n)
                        columns(b, s2, [sw2[:, c, :] for c in range(sc)], [st1[:, c, :] for c in range(sc)])
                        n += 1
                    pe.wait_ge(weighed, b + 1)
                    for u in range(2):
                        bank = cols.fill(pe, b)
                        for j in range(4 * u, min(4 * u + 4, BT)):
                            mm = pe.transpose(bank[0:ne, j % 4 * P:(j % 4 + 1) * P], gate.q[:, j, :], net.ident[:])
                        mm.then_inc(cols.full, 1)
                    n += 2
                    drained(b, n)
                    for u in range(4):
                        bank = outs.fill(pe, b)
                        for j in range(2 * u, min(2 * u + 2, BT)):
                            o = bank[:, (j - 2 * u) * D:(j - 2 * u + 1) * D]
                            pe.matmul(o, st2[:, j * P:(j + 1) * P], sw3[:], start=True, stop=False)
                            pe.matmul(o, net.ones[0:1, :], sb3[:], start=False, stop=False)
                            mm = pe.matmul(o, wt[:, j * P:(j + 1) * P], eb3[:], start=False, stop=True)
                        mm.then_inc(outs.full, 1)
                    for e in range(ne):
                        for s in range(2):
                            columns(b, e1, [ew1[:, e, c, :] for c in range(2)],
                                    [xt[:, c, s * HB:(s + 1) * HB] for c in range(2)])
                        drained(b, n + 2)
                        for s in range(2):
                            columns(b, e2, [ew2[:, e, :]], [h1[:, s * HB:(s + 1) * HB]])
                        n += 4
                        drained(b, n)
                        for u in range(4):
                            bank = outs.fill(pe, b)
                            for j in range(2 * u, min(2 * u + 2, BT)):
                                mm = pe.matmul(bank[:, (j - 2 * u) * D:(j - 2 * u + 1) * D],
                                               h2[:, j * P:(j + 1) * P], ew3[:, e, :], start=True, stop=True)
                            mm.then_inc(outs.full, 1)


def segment_max(nc, net, name, table):
    half = KT + 2 - KT % 2
    turns = -(-half // (2 * HALF))
    with Stage(nc, name) as st:
        index = st.sb("index", [P, 2, HALF], I32)
        rows = st.sb("rows", [P, 2, HALF, HEADS])
        cols = st.sb("cols", [P, KP, HEADS])
        best, back = st.sb("best", [P, HEADS, KC, P]), st.sb("back", [P, 2, KC, P])
        item_of = st.sb("item_of", [P, KC, NIP])
        ends = st.sb("ends", [HEADS, 2, KP])
        step, carry = st.sb("step", [HEADS, 2, KP]), st.sb("carry", [HEADS, 2, KP])
        carried = st.sb("carried", [P, 2, KC, HEADS])
        gathered = [st.sem("gathered0"), st.sem("gathered1")]
        indexed, go, copied, cleared = (st.sem(x) for x in ("indexed", "go", "copied", "cleared"))
        turned, laid, scanned, chain, pe_done = (st.sem(x) for x in ("turned", "laid", "scanned", "chain", "pe_done"))
        taken, widened = st.sem("taken"), st.sem("widened")
        bank = st.banks(8)

        with nc.Block() as block:
            @block.gpsimd
            def _(pool):
                pool.memset(cols[:, turns * 2 * HALF:KP, :], 0.0).then_inc(cleared, 1)

                def turn(i, first):
                    for h in range(2):
                        if not first:
                            pool.wait_ge(gathered[h], P * i)
                            pool.wait_ge(copied, i * 2 + h - 1)
                        pool.tensor_copy(index[:, h, :], net.src_col[:, bass.ds(i * (2 * HALF) + h * HALF, HALF)])\
                            .then_inc(indexed, 1)
                        pool.wait_ge(indexed, i * 2 + h + 1)
                        pool.sem_inc(go, 1)
                        for j in range(HALF):
                            pool.indirect_dma_start(rows[:, h, j, :], None, table,
                                                    bass.IndirectOffsetOnAxis(ap=index[:, h, j:j + 1], axis=0))\
                                .then_inc(gathered[h], 16)

                turn(0, True)
                with pool.Fori(1, turns) as i:
                    turn(i, False)

            @block.vector
            def _(dve):
                ch = Chain(dve, chain)
                with dve.Fori(0, turns) as i:
                    for h in range(2):
                        dve.wait_ge(gathered[h], P * i + P)
                        dve.tensor_copy(cols[:, bass.ds(i * (2 * HALF) + h * HALF, HALF), :], rows[:, h])\
                            .then_inc(copied, 1)
                for h in range(HEADS):
                    dve.wait_ge(laid, 2 * h + 2)
                    b = best[:, h].rearrange("p c e -> p (c e)")
                    left, right = (back[:, s].rearrange("p c e -> p (c e)") for s in range(2))
                    start, end = (m[:].rearrange("p c e -> p (c e)") for m in (net.run_start, net.run_end))
                    ch.mark(dve.tensor_tensor_scan(left, start, b, -BIG, ALU.add, ALU.max))
                    ch.link(dve.tensor_tensor_scan(right[:, ::-1], end[:, ::-1], b[:, ::-1], -BIG, ALU.add, ALU.max))
                    ch.link(dve.tensor_tensor(b, left, right, ALU.max))
                dve.sem_inc(scanned, 1)
                dve.wait_ge(pe_done, 1)
                for s in range(2):
                    ch.mark(dve.tensor_copy(ends[:, s, 0:512], bank[2 * s][0:HEADS, :]))
                    ch.link(dve.tensor_copy(ends[:, s, 512:KP], bank[2 * s + 1][0:HEADS, 0:KP - 512]))
                ch.mark(dve.memset(step[:, 0, 0:1], -BIG))
                ch.mark(dve.memset(step[:, 1, KP - 1:KP], -BIG))
                ch.mark(dve.tensor_tensor(step[:, 0, 1:KP], ends[:, 1, 0:KP - 1], net.link_left[:, 1:KP], ALU.add))
                ch.link(dve.tensor_tensor(step[:, 1, 0:KP - 1], ends[:, 0, 1:KP], net.link_right[:, 0:KP - 1],
                                          ALU.add))
                ch.mark(dve.tensor_tensor_scan(carry[:, 0, :], net.pass_left[:], step[:, 0, :], -BIG,
                                               ALU.add, ALU.max))
                ch.link(dve.tensor_tensor_scan(carry[:, 1, ::-1], net.pass_right[:, ::-1], step[:, 1, ::-1], -BIG,
                                               ALU.add, ALU.max))
                dve.sem_inc(scanned, 1)
                dve.wait_ge(pe_done, 2)
                ch.link(dve.tensor_copy(carried[:].rearrange("p s c h -> p (s c h)"),
                                        bank[4][:, 0:2 * KC * HEADS]))
                for h in range(HEADS):
                    for s, mask in enumerate((net.not_first_run, net.not_last_run)):
                        ch.link(dve.tensor_tensor(back[:, s], mask[:], over(carried[:, s, :, h], P), ALU.add))
                        last = dve.tensor_tensor(best[:, h], best[:, h], back[:, s], ALU.max)
                        if s == 0:
                            ch.link(last)
                        else:
                            last.then_inc(scanned, 1)
                for n in range(2 * HEADS):
                    h, s = n // 2, n % 2
                    dve.wait_ge(pe_done, 3 + n)
                    dve.tensor_copy(net.peak[:, s * IC:(s + 1) * IC, h], bank[n][:, 0:IC]).then_inc(taken, 1)

            @block.scalar
            def _(act):
                act.activation(item_of[:], net.item_of[:], ACT.Copy).then_inc(widened, 1)
                for n in range(2 * HEADS):
                    h, s = n // 2, n % 2
                    act.wait_ge(turned, n + 1)
                    c0, c1 = (0, 4) if s == 0 else (4, KC)
                    act.activation(best[:, h, c0:c1, :].rearrange("p c e -> p (c e)"),
                                   bank[n][:, 0:(c1 - c0) * P], ACT.Copy).then_inc(laid, 1)

            @block.tensor
            def _(pe):
                pe.wait_ge(cleared, 1)
                pe.wait_ge(copied, turns * 2)
                for n in range(2 * HEADS):
                    h, s = n // 2, n % 2
                    for c in range(4 * s, min(4 * s + 4, KC)):
                        mm = pe.transpose(bank[n][:, (c - 4 * s) * P:(c - 4 * s + 1) * P],
                                          cols[:, c * P:(c + 1) * P, h], net.ident[:])
                    mm.then_inc(turned, 1)
                pe.wait_ge(scanned, 1)
                for s, at in enumerate((0, P - 1)):
                    for c in range(KC):
                        b = bank[2 * s + c // 4]
                        mm = pe.transpose(b[0:HEADS, c % 4 * P:(c % 4 + 1) * P], best[:, :, c, at], net.ident[:])
                mm.then_inc(pe_done, 1)
                pe.wait_ge(scanned, 2)
                for s in range(2):
                    for c in range(KC):
                        at = (s * KC + c) * HEADS
                        mm = pe.transpose(bank[4][:, at:at + HEADS], carry[:, s, c * P:(c + 1) * P],
                                          net.ident[0:HEADS, 0:HEADS])
                mm.then_inc(pe_done, 1)
                pe.wait_ge(widened, 1)
                for n in range(2 * HEADS):
                    h, s = n // 2, n % 2
                    pe.wait_ge(scanned, 3 + h)
                    for c in range(KC):
                        mm = pe.matmul(bank[n][:, 0:IC], best[:, h, c, :], item_of[:, c, s * IC:(s + 1) * IC],
                                       start=c == 0, stop=c == KC - 1)
                    mm.then_inc(pe_done, 1)


def gat_pass(nc, net, name, table):
    with Stage(nc, name) as st:
        index = st.sb("index", [P, DEPTH, HALF], I32)
        rows, msg = st.sb("rows", [P, DEPTH, HALF, GW]), st.sb("msg", [P, 2, HALF, MW])
        onehot, turned_sb = st.sb("onehot", [P, DEPTH, HALF, P]), st.sb("turned_sb", [P, 2, HALF, P])
        lg, diff = (st.sb(x, [P, 2, HALF, HEADS]) for x in ("lg", "diff"))
        sums = st.banks(4, "sum")
        flips = st.banks(2, "flip")
        node_lg = st.banks(2, "node")
        gathered = [st.sem(f"gathered{h}") for h in range(DEPTH)]
        indexed, go, made, turned, copied = (st.sem(x) for x in ("indexed", "go", "made", "turned", "copied"))
        looked, shifted, raised, ready, summed, added = (
            st.sem(x) for x in ("looked", "shifted", "raised", "ready", "summed", "added"))
        peaked, chain = st.sem("peaked"), st.sem("chain")
        turns = STEPS // DEPTH

        with nc.Block() as block:
            @block.gpsimd
            def _(pool):
                gather_rows(pool, table, rows, net.src_of, index, gathered, indexed, go, ready,
                            lambda q: (q - DEPTH + 1) * 4)

            @block.vector
            def _(dve):
                ch = Chain(dve, chain)
                tile = [dve.alloc_register(f"{name}_t{j}") for j in range(HALF)]
                marks = 5

                def items(q):
                    return bass.ds(q * HALF, HALF)

                def one_hot(q, s, p):
                    dve.tensor_tensor(onehot[:, s, 2 * p:2 * p + 2],
                                      over(net.dloc[:, bass.ds(q * HALF + 2 * p, 2)], P), mid(net.iota[:], 2),
                                      ALU.is_equal).then_inc(made, 1)

                def bring_peaks(q, h):
                    dve.tensor_tensor(msg[:, h, :, GW:MW], net.peak[:, items(q), :],
                                      over(net.first_of[:, items(q)], HEADS), ALU.mult).then_inc(peaked, 1)

                def multiply(q, s, p):
                    dve.tensor_tensor(msg[:, s % 2, 2 * p:2 * p + 2, 0:D].rearrange("p j (h f) -> p j h f", f=HID),
                                      rows[:, s, 2 * p:2 * p + 2, 0:D].rearrange("p j (h f) -> p j h f", f=HID),
                                      over(msg[:, s % 2, 2 * p:2 * p + 2, D:GW], HID), ALU.mult)\
                        .then_inc(ready, 1)

                def add(q, j, first=False):
                    dve.wait_ge(summed, q * HALF + j + 1)
                    if not first:
                        dve.wait_ge(added, q * HALF + j)
                    acc = net.acc[:, bass.ds(dve.snap(tile[j], min_val=0, max_val=NT - 1) * MW, MW)]
                    dve.tensor_tensor(acc, acc, sums[j % 4][:, 0:MW], ALU.add).then_inc(added, 1)

                def from_nodes(s, what):
                    at = node_lg[s % 2][:, 0:HALF * 2 * HEADS].rearrange("p (j a) -> p j a", a=2 * HEADS)
                    return at[:, :, what * HEADS:(what + 1) * HEADS]

                def begin_logits(q, s, turn):
                    dve.wait_ge(gathered[s], turn * P + P)
                    dve.wait_ge(looked, q + 1)
                    ch.mark(dve.tensor_tensor(lg[:, 0], rows[:, s, :, D:GW], from_nodes(s, 1), ALU.add))
                    ch.mark(dve.tensor_tensor(lg[:, 1], net.peak[:, items(q), :], from_nodes(s, 0), ALU.max))

                def join_logits(s):
                    ch.wait()
                    ch.mark(dve.tensor_tensor(lg[:, 1], lg[:, 1], from_nodes(s, 1), ALU.add))

                def leak_logits():
                    ch.wait()
                    ch.mark(dve.scalar_tensor_tensor(out=lg[:], in0=lg[:], scalar=0.2, in1=lg[:],
                                                     op0=ALU.mult, op1=ALU.max))

                def shift_logits(s):
                    ch.wait()
                    ch.mark(dve.tensor_tensor(diff[:, s % 2], lg[:, 0], lg[:, 1], ALU.subtract))

                def bound_logits(s):
                    ch.wait()
                    dve.tensor_scalar(diff[:, s % 2], diff[:, s % 2], 0.0, None, ALU.min).then_inc(shifted, 1)

                def step(i, s, first=False, last=False):
                    q = i * DEPTH + s
                    logits = not (last and s == DEPTH - 1)
                    hots = not (last and s >= 1)
                    n, turn = (s + 1) % DEPTH, i + (s + 1) // DEPTH
                    dve.wait_ge(raised, q + 1)
                    multiply(q, s, 0)
                    for p in range(4):
                        if not (first and s == 0):
                            add(q - 1, p + 4)
                        if p < 3:
                            multiply(q, s, p + 1)
                    dve.load(tile[0:4], net.t_of[0:1, bass.ds(q * HALF, 4)])
                    if hots:
                        one_hot(q + 3, (s + 3) % DEPTH, 0)
                    add(q, 0, first and s == 0)
                    dve.load(tile[4:8], net.t_of[0:1, bass.ds(q * HALF + 4, 4)])
                    if logits:
                        begin_logits(q + 1, n, turn)
                    if hots:
                        one_hot(q + 3, (s + 3) % DEPTH, 1)
                    if logits:
                        join_logits(n)
                    add(q, 1)
                    if logits:
                        leak_logits()
                    if hots:
                        one_hot(q + 3, (s + 3) % DEPTH, 2)
                    if logits:
                        shift_logits(n)
                    add(q, 2)
                    if logits:
                        bound_logits(n)
                    if hots:
                        one_hot(q + 3, (s + 3) % DEPTH, 3)
                    add(q, 3)
                    if logits:
                        bring_peaks(q + 1, n % 2)

                for q in range(3):
                    for p in range(4):
                        one_hot(q, q, p)
                bring_peaks(0, 0)
                begin_logits(0, 0, 0)
                join_logits(0)
                leak_logits()
                shift_logits(0)
                bound_logits(0)
                for s in range(DEPTH):
                    step(0, s, first=True)
                with dve.Fori(1, turns - 1) as i:
                    ch.enter(i - 1, DEPTH * marks)
                    for s in range(DEPTH):
                        step(i, s)
                    ch.leave(turns - 2)
                for s in range(DEPTH):
                    step(turns - 1, s, last=True)
                for j in range(4, HALF):
                    add(STEPS - 1, j)

            @block.scalar
            def _(act):
                def copy_turned(q, h):
                    act.wait_ge(turned, q + 1)
                    for s in range(2):
                        last = act.activation(
                            turned_sb[:, h, 4 * s:4 * s + 4, :].rearrange("p j n -> p (j n)"), flips[s][:], ACT.Copy)
                    last.then_inc(copied, 1)

                def raise_(q, h, fresh=False):
                    act.wait_ge(shifted, q + 1)
                    if not fresh:
                        act.wait_ge(summed, (q - 1) * HALF)
                    act.activation(msg[:, h, :, D:GW], diff[:, h], ACT.Exp).then_inc(raised, 1)

                copy_turned(0, 0)
                copy_turned(1, 1)
                raise_(0, 0, True)
                copy_turned(2, 0)
                raise_(1, 1, True)
                copy_turned(3, 1)
                raise_(2, 0)
                with act.Fori(1, STEPS // 2 - 1) as i:
                    copy_turned(i * 2 + 2, 0)
                    raise_(i * 2 + 1, 1)
                    copy_turned(i * 2 + 3, 1)
                    raise_(i * 2 + 2, 0)
                raise_(STEPS - 1, 1)

            @block.tensor
            def _(pe):
                tile = [pe.alloc_register(f"{name}_u{j}") for j in range(HALF)]

                def turn_over(q, s):
                    pe.wait_ge(made, (q + 1) * 4)
                    if not (isinstance(q, int) and q == 0):
                        pe.wait_ge(copied, q)
                    for j in range(HALF):
                        mm = pe.transpose(flips[j // 4][:, j % 4 * P:(j % 4 + 1) * P], onehot[:, s, j, :],
                                          net.ident[:])
                    mm.then_inc(turned, 1)

                def look_up(q, h):
                    pe.load(tile, net.t_of[0:1, bass.ds(q * HALF, HALF)])
                    pe.wait_ge(copied, q + 1)
                    for j in range(HALF):
                        t = pe.snap(tile[j], min_val=0, max_val=NT - 1)
                        mm = pe.matmul(node_lg[h][:, j * 2 * HEADS:(j + 1) * 2 * HEADS], turned_sb[:, h, j, :],
                                       net.logit[:, bass.ds(t * (2 * HEADS), 2 * HEADS)], start=True, stop=True)
                    mm.then_inc(looked, 1)

                def sum_up(q, s, p, fresh):
                    pe.wait_ge(ready, q * 4 + p + 1)
                    if p == 0:
                        pe.wait_ge(peaked, q + 1)
                    for j in range(2 * p, 2 * p + 2):
                        if not (fresh and j < 4):
                            pe.wait_ge(added, q * HALF + j - 3)
                        pe.matmul(sums[j % 4][:, 0:MW], onehot[:, s, j, :], msg[:, s % 2, j, :],
                                  start=True, stop=True).then_inc(summed, 1)

                def turn(i, first=False, last=False):
                    for s in range(DEPTH):
                        q = i * DEPTH + s
                        ahead = not (last and s >= DEPTH - 2)
                        for p in range(2):
                            sum_up(q, s, p, first and s == 0)
                        if ahead:
                            turn_over(q + 2, (s + 2) % DEPTH)
                        sum_up(q, s, 2, False)
                        if ahead:
                            look_up(q + 2, s % 2)
                        sum_up(q, s, 3, False)

                for q in range(2):
                    turn_over(q, q)
                    look_up(q, q)
                turn(0, first=True)
                with pe.Fori(1, turns - 1) as i:
                    turn(i)
                turn(turns - 1, last=True)


def gat_finish(nc, net, name, table, bias, add_to_x):
    with Stage(nc, name) as st:
        own, own_w, mx, scaled = (st.sb(x, [P, NT, HEADS]) for x in ("own", "own_w", "mx", "scaled"))
        den, b_sb = st.sb("den", [P, NT, HEADS]), st.sb("b", [P, D])
        rows, tmp = st.sb("rows", [P, BT, D]), st.sb("tmp", [P, BT, D])
        part = st.sb("part", [P, 2, BT, HEADS])
        loaded, row_in, row_free, chain, diff, raised = (
            st.sem(x) for x in ("loaded", "row_in", "row_free", "chain", "diff", "raised"))
        acc = net.acc[:].rearrange("p (t w) -> p t w", w=MW)
        lg = net.logit[:].rearrange("p (t a) -> p t a", a=2 * HEADS)

        with nc.Block() as block:
            @block.sync
            def _(sp):
                sp.dma_start(b_sb[:], bias.partition_broadcast(P)).then_inc(loaded, 16)
                view = table.rearrange("(t p) w -> p t w", p=P)
                with sp.Fori(0, NB) as b:
                    sp.wait_ge(row_free, b + 1)
                    sp.dma_start(rows[:], view[:, bass.ds(b * BT, BT), 0:D]).then_inc(row_in, 16)

            @block.vector
            def _(dve):
                ch = Chain(dve, chain)
                dve.sem_inc(row_free, 1)

                def leaky(x):
                    ch.link(dve.tensor_scalar(scaled[:], x[:], 0.2, None, ALU.mult))
                    ch.link(dve.tensor_tensor(x[:], x[:], scaled[:], ALU.max))

                ch.link(dve.tensor_scalar(scaled[:, :, 0], net.has_edge[:], -1.0, BIG, ALU.add, ALU.mult))
                ch.link(dve.tensor_tensor(mx[:], acc[:, :, GW:MW], over(scaled[:, :, 0], HEADS), ALU.add))
                ch.link(dve.tensor_tensor(mx[:], mx[:], lg[:, :, 0:HEADS], ALU.max))
                ch.link(dve.tensor_tensor(mx[:], mx[:], lg[:, :, HEADS:2 * HEADS], ALU.add))
                leaky(mx)
                ch.link(dve.tensor_tensor(own[:], lg[:, :, 0:HEADS], lg[:, :, HEADS:2 * HEADS], ALU.add))
                leaky(own)
                dve.tensor_tensor(own[:], own[:], mx[:], ALU.subtract).then_inc(diff, 1)
                dve.wait_ge(raised, 1)
                ch.link(dve.tensor_tensor(den[:], acc[:, :, D:GW], own_w[:], ALU.add))
                ch.link(dve.tensor_scalar(den[:], den[:], 1e-16, None, ALU.add))
                ch.link(dve.reciprocal(den[:], den[:]))
                dve.wait_ge(loaded, 16)
                with dve.Fori(0, NB) as b:
                    ch.enter(b, 4 + (3 if add_to_x else 2) * BT)
                    ch.mark(dve.tensor_copy(part[:, 0], own_w[:, bass.ds(b * BT, BT), :]))
                    ch.link(dve.tensor_copy(part[:, 1], den[:, bass.ds(b * BT, BT), :]))
                    dve.wait_ge(row_in, b * 16 + 16)
                    heads = [x[:].rearrange("p j (h f) -> p (j h) f", f=HID) for x in (rows, tmp)]
                    ch.link(dve.tensor_tensor(heads[1], heads[0],
                                              over(part[:, 0].rearrange("p j h -> p (j h)"), HID), ALU.mult))
                    dve.sem_inc(row_free, 1)
                    for j in range(BT):
                        ch.mark(dve.tensor_tensor(tmp[:, j, :], tmp[:, j, :],
                                                  net.acc[:, bass.ds(b * (BT * MW) + j * MW, D)], ALU.add))
                    ch.wait()
                    ch.link(dve.tensor_tensor(heads[1], heads[1],
                                              over(part[:, 1].rearrange("p j h -> p (j h)"), HID), ALU.mult))
                    for j in range(BT):
                        if add_to_x:
                            ch.mark(dve.tensor_tensor(tmp[:, j, :], tmp[:, j, :], b_sb[:], ALU.add))
                        else:
                            ch.mark(dve.tensor_tensor(net.acc[:, bass.ds(b * (BT * MW) + j * MW, D)],
                                                      tmp[:, j, :], b_sb[:], ALU.add))
                    ch.wait()
                    for j in range(BT):
                        if add_to_x:
                            x = net.x[:, bass.ds(b * (BT * D) + j * D, D)]
                            ch.mark(dve.tensor_tensor(x, x, tmp[:, j, :], ALU.add))
                    ch.wait()
                    ch.leave(NB)

            @block.scalar
            def _(act):
                act.wait_ge(diff, 1)
                act.activation(own_w[:], own[:], ACT.Exp).then_inc(raised, 1)


def route_nodes(nc, net, w, table):
    ne = w["Wr"].shape[1]
    with Stage(nc, "route") as st:
        gate = Gate(st, ne, False)
        part = st.sb("part", [P, 3, BT])
        again = st.sb("again", [P, BT, D])
        xn, xt = st.sb("xn", [P, BT, D]), st.sb("xt", [P, 2, BN])
        wr, b2, wt = st.sb("wr", [P, 2, ne]), st.sb("b2", [ne, D]), st.sb("wt", [ne, BN])
        loaded, ready, chain, weighed = st.sem("loaded"), st.sem("ready"), st.sem("chain"), st.sem("weighed")
        written, begun = st.sem("written"), st.sem("begun")
        n_cols = 4 + 2
        cols = Ring(st.sem("cols"), st.sem("cols_free"), st.banks(4, "c"), n_cols)
        outs = Ring(st.sem("outs"), st.sem("outs_free"), st.banks(4, "o"), 1 + 4)

        with nc.allow_non_contiguous_dma(reason="gate weights, once"), nc.Block() as block:
            @block.sync
            def _(sp):
                for o, i in ((wr[:], w["Wr"].rearrange("(c k) e -> k c e", k=P)),
                             (gate.bias[:], w["br"].partition_broadcast(P)), (b2[:], w["b2"])):
                    sp.dma_start(o, i).then_inc(loaded, 16)
                rows = table.rearrange("(t p) w -> p t w", p=P)
                with sp.Fori(0, NB) as b:
                    sp.wait_ge(ready, b + 1)
                    sp.dma_start(rows[:, bass.ds(b * BT, BT), :], again[:]).then_inc(written, 16)
                sp.wait_ge(written, 16 * NB)

            @block.vector
            def _(dve):
                ch = Chain(dve, chain)
                outs.give_credit(dve)
                dve.wait_ge(loaded, 48)
                gate.order(ch, dve, net)

                def prepare(b):
                    ch.mark(dve.tensor_copy(part[:, 0, :], net.mean[:, bass.ds(b * BT, BT)]))
                    ch.mark(dve.tensor_copy(part[:, 1, :], net.rstd[:, bass.ds(b * BT, BT)]))
                    ch.link(dve.tensor_tensor(part[:, 2, :], net.rstd[:, bass.ds(b * BT, BT)],
                                              net.rstd2[:, bass.ds(b * BT, BT)], ALU.mult))
                    for j in range(BT):
                        ch.mark(dve.tensor_scalar(again[:, j, :], net.x[:, bass.ds(b * (BT * D) + j * D, D)],
                                                  part[:, 0, j:j + 1], part[:, 2, j:j + 1],
                                                  ALU.subtract, ALU.mult))
                    ch.wait()
                    for j in range(BT):
                        last = dve.tensor_scalar(xn[:, j, :], net.x[:, bass.ds(b * (BT * D) + j * D, D)],
                                                 part[:, 0, j:j + 1], part[:, 1, j:j + 1], ALU.subtract, ALU.mult)
                    last.then_inc(ready, 1)

                def finish(b):
                    gate.weights(ch, dve, b, outs.drain(dve, b)[:, 0:BT * ne], outs)
                    dve.sem_inc(weighed, 1)
                    ch.mark(dve.tensor_copy(net.chosen[:, :, bass.ds(b * BT, BT)],
                                            gate.chosen[:].rearrange("p j e -> p e j")))
                    ch.link(dve.tensor_copy(net.weight[:, :, bass.ds(b * BT, BT)],
                                            gate.q[:].rearrange("p j e -> p e j")))
                    for u in range(4):
                        bank = outs.drain(dve, b)
                        n = min(2, BT - 2 * u)
                        x = net.x[:, bass.ds(b * (BT * D) + 2 * u * D, n * D)]
                        dve.tensor_tensor(x, x, bank[:, 0:n * D], ALU.add).then_inc(outs.empty, 1)

                prepare(0)
                with dve.Fori(0, NB - 1) as b:
                    ch.enter(b, Gate.marks + 5 + BT)
                    dve.wait_ge(cols.full, b * n_cols + 4)
                    dve.wait_ge(written, b * 16 + 16)
                    dve.sem_inc(begun, 1)
                    prepare(b + 1)
                    finish(b)
                    ch.leave(NB - 1)
                finish(NB - 1)

            @block.scalar
            def _(act):
                cols.give_credit(act)
                flat = xt[:].rearrange("p c n -> p (c n)")
                with act.Fori(0, NB) as b:
                    for u in range(4):
                        n = min(4, 2 * BT - 4 * u) * P
                        act.activation(flat[:, u * 512:u * 512 + n], cols.drain(act, b)[:, 0:n], ACT.Copy)\
                            .then_inc(cols.empty, 1)
                    gate.raise_(act, b)
                    for u in range(2):
                        n = min(4, BT - 4 * u) * P
                        act.activation(wt[:, u * 512:u * 512 + n], cols.drain(act, b)[0:ne, 0:n], ACT.Copy)\
                            .then_inc(cols.empty, 1)

            @block.tensor
            def _(pe):
                pe.wait_ge(loaded, 48)
                with pe.Fori(0, NB) as b:
                    pe.wait_ge(ready, b + 1)
                    for u in range(4):
                        bank = cols.fill(pe, b)
                        for m in range(4 * u, min(4 * u + 4, 2 * BT)):
                            mm = pe.transpose(bank[:, m % 4 * P:(m % 4 + 1) * P],
                                              xn[:, m % BT, m // BT * P:(m // BT + 1) * P], net.ident[:])
                        mm.then_inc(cols.full, 1)
                    pe.wait_ge(cols.empty, (b + 1) * n_cols + 4)
                    bank = outs.fill(pe, b)
                    for j in range(BT):
                        for c in range(2):
                            mm = pe.matmul(bank[:, j * ne:(j + 1) * ne], xt[:, c, j * P:(j + 1) * P], wr[:, c, :],
                                           start=c == 0, stop=c == 1)
                    mm.then_inc(outs.full, 1)
                    pe.wait_ge(weighed, b + 1)
                    for u in range(2):
                        bank = cols.fill(pe, b)
                        for j in range(4 * u, min(4 * u + 4, BT)):
                            mm = pe.transpose(bank[0:ne, j % 4 * P:(j % 4 + 1) * P], gate.q[:, j, :], net.ident[:])
                        mm.then_inc(cols.full, 1)
                    pe.wait_ge(cols.empty, (b + 1) * n_cols + 6)
                    for u in range(4):
                        bank = outs.fill(pe, b)
                        for j in range(2 * u, min(2 * u + 2, BT)):
                            mm = pe.matmul(bank[:, (j - 2 * u) * D:(j - 2 * u + 1) * D], wt[:, j * P:(j + 1) * P],
                                           b2[:], start=True, stop=True)
                        mm.then_inc(outs.full, 1)


def assign_slots(nc, net, ne):
    m = ne * NT
    with Stage(nc, "assign") as st:
        before = st.sb("before", [P, P])
        ones = st.sb("ones", [P, m])
        total, upto, slot = (st.sb(x, [P, m]) for x in ("total", "upto", "slot"))
        work = st.sb("work", [P, m])
        count, blocks, cum_n, cum_b = (st.sb(x, [P, ne]) for x in ("count", "blocks", "cum_n", "cum_b"))
        blocks_i, offset = st.sb("blocks_i", [P, ne], I32), st.sb("offset", [P, ne])
        past = st.sb("past", [1, BLOCKS, ne])
        block_f = st.sb("block_f", [1, BLOCKS])
        ends, ends_i = st.sb("ends", [P, 2, NT]), st.sb("ends_i", [P, 2, NT], I32)
        cut_i = st.sb("cut_i", [P, 2, NT], I32)
        hi, lo = st.sb("hi", [P, 2, NT]), st.sb("lo", [P, 2, NT])
        node = st.sb("node", [P, NT])
        one_lo, one_hi = st.sb("one_lo", [P, 2, BT, P]), st.sb("one_hi", [P, 2, BT, P])
        counts, sums, inverse = st.banks(3)
        ready, chain, pe_done = st.sem("ready"), st.sem("chain"), st.sem("pe_done")
        onehot, placed, numbered = st.sem("onehot"), st.sem("placed"), st.sem("numbered")
        by_node = lambda t: t[:].rearrange("p (e t) -> p t e", e=ne)
        by_expert = lambda t: t[:].rearrange("p (e t) -> p e t", e=ne)

        with nc.Block() as block:
            @block.gpsimd
            def _(pool):
                pool.iota(node[:], [[P, NT]], base=0, channel_multiplier=1, allow_small_or_imprecise_dtypes=True)\
                    .then_inc(numbered, 1)

            @block.vector
            def _(dve):
                ch = Chain(dve, chain)
                dve.tensor_scalar(before[:], net.iota[:], net.part[:, 0:1], None, ALU.is_gt).then_inc(ready, 1)
                ch.link(dve.memset(ones[:], 1.0))
                dve.wait_ge(pe_done, 2)
                ch.link(dve.tensor_copy(total[:], sums[:, 0:m]))
                ch.mark(dve.tensor_tensor_scan(upto[:], ones[:], total[:], 0.0, ALU.mult, ALU.add))
                ch.link(dve.tensor_reduce(count[:], by_expert(total), AX, ALU.add))
                ch.link(dve.tensor_scalar(blocks[:], count[:], float(BLOCK - 1), None, ALU.add))
                ch.link(dve.tensor_copy(blocks_i[:], blocks[:]))
                ch.link(dve.tensor_scalar(blocks_i[:], blocks_i[:], BLOCK.bit_length() - 1, None,
                                          ALU.arith_shift_right))
                ch.link(dve.tensor_copy(blocks[:], blocks_i[:]))
                ch.mark(dve.tensor_tensor_scan(cum_n[:], ones[:, 0:ne], count[:], 0.0, ALU.mult, ALU.add))
                ch.link(dve.tensor_tensor_scan(cum_b[:], ones[:, 0:ne], blocks[:], 0.0, ALU.mult, ALU.add))
                ch.link(dve.tensor_tensor(offset[:], cum_b[:], blocks[:], ALU.subtract))
                ch.link(dve.scalar_tensor_tensor(out=offset[:], in0=offset[:], scalar=float(BLOCK), in1=cum_n[:],
                                                 op0=ALU.mult, op1=ALU.subtract))
                ch.link(dve.tensor_tensor(offset[:], offset[:], count[:], ALU.add))
                ch.link(dve.tensor_tensor(slot[:], upto[:], total[:], ALU.subtract))
                ch.link(dve.tensor_tensor(by_expert(slot), by_expert(slot), over(offset[:], NT), ALU.add))
                ch.link(dve.tensor_tensor(slot[:], slot[:], counts[:, 0:m], ALU.add))
                chosen = net.chosen[:].rearrange("p e t -> p (e t)")
                ch.link(dve.tensor_scalar(work[:], chosen, -FAR, FAR, ALU.mult, ALU.add))
                ch.link(dve.tensor_tensor(work[:], work[:], slot[:], ALU.add))
                ch.link(dve.tensor_reduce(ends[:, 0, :], by_node(work), AX, ALU.min))
                ch.link(dve.tensor_tensor(work[:], chosen, slot[:], ALU.mult))
                ch.link(dve.tensor_reduce(ends[:, 1, :], by_node(work), AX, ALU.max))
                weight = net.weight[:].rearrange("p e t -> p (e t)")
                for s in range(2):
                    ch.link(dve.tensor_tensor(by_expert(work), by_expert(slot), mid(ends[:, s, :], ne),
                                              ALU.is_equal))
                    ch.link(dve.tensor_tensor(work[:], work[:], weight, ALU.mult))
                    ch.link(dve.tensor_reduce(net.share[:, s, :], by_node(work), AX, ALU.add))
                ch.link(dve.tensor_copy(ends_i[:], ends[:]))
                ch.mark(dve.tensor_copy(net.slots[:].rearrange("p (b s j) -> p b s j", s=2, j=BT),
                                        ends_i[:].rearrange("p s (b j) -> p b s j", j=BT)))
                ch.link(dve.tensor_tensor(past[:], over(net.iota[0:1, 0:BLOCKS], ne), mid(cum_b[0:1, :], BLOCKS),
                                          ALU.is_ge))
                ch.link(dve.tensor_reduce(block_f[:], past[:], AX, ALU.add))
                ch.link(dve.tensor_scalar(block_f[:], block_f[:], float(ne - 1), None, ALU.min))
                ch.mark(dve.tensor_copy(net.block_expert[:], block_f[:]))
                ch.link(dve.tensor_scalar(cut_i[:], ends_i[:], 7, None, ALU.arith_shift_right))
                ch.link(dve.tensor_copy(hi[:], cut_i[:]))
                ch.link(dve.tensor_scalar(cut_i[:], ends_i[:], 127, None, ALU.bitwise_and))
                ch.link(dve.tensor_copy(lo[:], cut_i[:]))
                dve.wait_ge(numbered, 1)
                for q in range(2 * NB):
                    s, cols, h = q // NB, slice(q % NB * BT, (q % NB + 1) * BT), q % 2
                    if q >= 2:
                        dve.wait_ge(placed, q - 1)
                    ch.mark(dve.tensor_tensor(one_lo[:, h], over(lo[:, s, cols], P), mid(net.iota[:], BT),
                                              ALU.is_equal))
                    ch.link(dve.tensor_tensor(one_hi[:, h], over(hi[:, s, cols], P), mid(net.iota[:], BT),
                                              ALU.is_equal))
                    dve.tensor_tensor(one_hi[:, h], one_hi[:, h], over(node[:, cols], P), ALU.mult)\
                        .then_inc(onehot, 1)
                dve.wait_ge(placed, 2 * NB)
                ch.link(dve.tensor_copy(net.node_of[:], inverse[:, 0:SLOT_COLS]))

            @block.tensor
            def _(pe):
                chosen = net.chosen[:].rearrange("p e t -> p (e t)")
                pe.matmul(sums[:, 0:m], net.ones[:], chosen, start=True, stop=True).then_inc(pe_done, 1)
                pe.wait_ge(ready, 1)
                pe.matmul(counts[:, 0:m], before[:], chosen, start=True, stop=True).then_inc(pe_done, 1)
                for q in range(2 * NB):
                    pe.wait_ge(onehot, q + 1)
                    for j in range(BT):
                        mm = pe.matmul(inverse[:, 0:P], one_lo[:, q % 2, j, :], one_hi[:, q % 2, j, :],
                                       start=q == 0 and j == 0, stop=q == 2 * NB - 1 and j == BT - 1)
                    mm.then_inc(placed, 1)


def large_mixture(nc, net, w, table, result):
    ne, _, hid = w["W1"].shape
    hc = hid // P
    g = BLOCK // P
    with Stage(nc, "moe") as st:
        index = st.sb("index", [P, 2, g], I32)
        rows = st.sb("rows", [P, 2, g, D])
        w1, w2 = st.sb("w1", [P, 2, 2, hid]), st.sb("w2", [P, 2, hc, D])
        b1, scale, shift = st.sb("b1", [P, 2, hc]), st.sb("scale", [P, 2, 2]), st.sb("shift", [P, 2, 2])
        xe, ht, y = st.sb("xe", [P, 2, 2, BLOCK]), st.sb("ht", [P, hc, BLOCK]), st.sb("y", [P, 2, g, D])
        gathered = [st.sem("gathered0"), st.sem("gathered1")]
        loaded = [st.sem("loaded0"), st.sem("loaded1")]
        stored = [st.sem("stored0"), st.sem("stored1")]
        indexed, go, begun, y_ready = st.sem("indexed"), st.sem("go"), st.sem("begun"), st.sem("y_ready")
        flipped = Ring(st.sem("flipped"), st.sem("flipped_free"), st.banks(2, "x"), 2)
        hidden = Ring(st.sem("hidden"), st.sem("hidden_free"), st.banks(4, "h"), hc)
        outs = Ring(st.sem("outs"), st.sem("outs_free"), st.banks(2, "o"), g // 2)
        n_loads = 5

        with nc.allow_non_contiguous_dma(reason="biases and scales"), nc.Block() as block:
            @block.gpsimd
            def _(pool):
                gather_rows(pool, table, rows, net.node_of, index, gathered, indexed, go, flipped.full,
                            lambda q: (q - 1) * 2)

            @block.sync
            def _(sp):
                expert = sp.alloc_register("moe_expert")
                out_rows = result.rearrange("(b j p) w -> b p j w", j=g, p=P)

                def load(b, h):
                    sp.load(expert, net.block_expert[0:1, bass.ds(b, 1)])
                    e = sp.snap(expert, min_val=0, max_val=ne - 1)
                    one = lambda a: a[bass.ds(e, 1)]
                    for o, i in ((scale[:, h, :], one(w["ln_g"]).rearrange("o (c k) -> k (o c)", k=P)),
                                 (shift[:, h, :], one(w["ln_b"]).rearrange("o (c k) -> k (o c)", k=P)),
                                 (b1[:, h, :], one(w["b1"]).rearrange("o (c k) -> k (o c)", k=P)),
                                 (w1[:, h], one(w["W1"]).rearrange("o (c k) m -> k (o c) m", k=P)),
                                 (w2[:, h], one(w["W2"]).rearrange("o (c k) m -> k (o c) m", k=P))):
                        sp.dma_start(o, i).then_inc(loaded[h], 16)

                def store(b, h):
                    sp.wait_ge(y_ready, b + 1)
                    sp.dma_start(out_rows[bass.ds(b, 1)].rearrange("o p j w -> p (o j) w"), y[:, h])\
                        .then_inc(stored[h], 16)

                for h in range(2):
                    load(h, h)
                with sp.Fori(0, BLOCKS // 2 - 1) as i:
                    for h in range(2):
                        store(i * 2 + h, h)
                        load(i * 2 + h + 2, h)
                for h in range(2):
                    store(BLOCKS - 2 + h, h)
                for h in range(2):
                    sp.wait_ge(stored[h], 16 * (BLOCKS // 2))

            @block.vector
            def _(dve):
                flipped.give_credit(dve)
                outs.give_credit(dve)

                def scale_rows(b, h, turn):
                    dve.wait_ge(loaded[h], turn * (16 * n_loads) + 16 * n_loads)
                    dve.sem_inc(begun, 1)
                    for c in range(2):
                        dve.tensor_scalar(xe[:, h, c, :], flipped.drain(dve, b)[:, 0:BLOCK],
                                          scale[:, h, c:c + 1], shift[:, h, c:c + 1], ALU.mult, ALU.add)\
                            .then_inc(flipped.empty, 1)

                def take(b, h):
                    for u in range(g // 2):
                        last = dve.tensor_copy(y[:, h, 2 * u:2 * u + 2, :].rearrange("p j w -> p (j w)"),
                                               outs.drain(dve, b)[:])
                        last.then_inc(outs.empty, 1)
                    outs.settle(dve, b)
                    dve.sem_inc(y_ready, 1)

                def turn(i, first=False, last=False):
                    for h in range(2):
                        b = i * 2 + h
                        if not (last and h == 1):
                            scale_rows(b + 1, 1 - h, i + h)
                        if not first:
                            dve.wait_ge(stored[h], i * 16)
                            dve.sem_inc(begun, 1)
                        take(b, h)

                scale_rows(0, 0, 0)
                turn(0, first=True)
                with dve.Fori(1, BLOCKS // 2 - 1) as i:
                    turn(i)
                turn(BLOCKS // 2 - 1, last=True)

            @block.scalar
            def _(act):
                hidden.give_credit(act)
                with act.Fori(0, BLOCKS // 2) as i:
                    for h in range(2):
                        act.wait_ge(loaded[h], i * (16 * n_loads) + 16 * n_loads)
                        for m in range(hc):
                            act.activation(ht[:, m, :], hidden.drain(act, i * 2 + h)[:, 0:BLOCK], ACT.Gelu,
                                           bias=b1[:, h, m:m + 1]).then_inc(hidden.empty, 1)

            @block.tensor
            def _(pe):
                def turn_over(b, h, turn):
                    pe.wait_ge(gathered[h], turn * (16 * g) + 16 * g)
                    for c in range(2):
                        bank = flipped.fill(pe, b)
                        for j in range(g):
                            mm = pe.transpose(bank[:, j * P:(j + 1) * P], rows[:, h, j, c * P:(c + 1) * P],
                                              net.ident[:])
                        mm.then_inc(flipped.full, 1)

                def turn(i, last=False):
                    for h in range(2):
                        b = i * 2 + h
                        pe.wait_ge(loaded[h], i * (16 * n_loads) + 16 * n_loads)
                        pe.wait_ge(flipped.empty, (b + 1) * 2 + 2)
                        for m in range(hc):
                            bank = hidden.fill(pe, b)
                            for c in range(2):
                                mm = pe.matmul(bank[:, 0:BLOCK], w1[:, h, c, m * P:(m + 1) * P], xe[:, h, c, :],
                                               start=c == 0, stop=c == 1)
                            mm.then_inc(hidden.full, 1)
                        if not (last and h == 1):
                            turn_over(b + 1, 1 - h, i + h)
                        pe.wait_ge(hidden.empty, (b + 2) * hc)
                        for u in range(g // 2):
                            bank = outs.fill(pe, b)
                            for j in range(2 * u, 2 * u + 2):
                                for m in range(hc):
                                    mm = pe.matmul(bank[:, (j - 2 * u) * D:(j - 2 * u + 1) * D],
                                                   ht[:, m, j * P:(j + 1) * P], w2[:, h, m, :],
                                                   start=m == 0, stop=m == hc - 1)
                            mm.then_inc(outs.full, 1)

                turn_over(0, 0, 0)
                with pe.Fori(0, BLOCKS // 2 - 1) as i:
                    turn(i)
                turn(BLOCKS // 2 - 1, last=True)


def collect_slots(nc, net, result):
    with Stage(nc, "collect") as st:
        index, rows = st.sb("index", [P, 2, BT], I32), st.sb("rows", [P, 2, BT, D])
        gathered = [st.sem("gathered0"), st.sem("gathered1")]
        part = st.sb("part", [P, 2, BT])
        indexed, go, added, begun, chain = (st.sem(x) for x in ("indexed", "go", "added", "begun", "chain"))

        with nc.Block() as block:
            @block.gpsimd
            def _(pool):
                gather_rows(pool, result, rows, net.slots, index, gathered, indexed, go, added,
                            lambda q: (q - 1) * BT)

            @block.vector
            def _(dve):
                with dve.Fori(0, NB) as b:
                    for s in range(2):
                        dve.tensor_copy(part[:, s, :], net.share[:, s, bass.ds(b * BT, BT)]).then_inc(chain, 1)
                    dve.wait_ge(chain, b * 2 + 2)
                    for s in range(2):
                        dve.wait_ge(gathered[s], b * (16 * BT) + 16 * BT)
                        if s:
                            dve.wait_ge(added, b * (2 * BT) + BT)
                        dve.sem_inc(begun, 1)
                        for j in range(BT):
                            x = net.x[:, bass.ds(b * (BT * D) + j * D, D)]
                            dve.scalar_tensor_tensor(out=x, in0=rows[:, s, j, :], scalar=part[:, s, j:j + 1],
                                                     in1=x, op0=ALU.mult, op1=ALU.add).then_inc(added, 1)
                    dve.wait_ge(added, b * (2 * BT) + 2 * BT)
                    dve.sem_inc(begun, 1)


def program(nc, a, out):
    part = lambda prefix: {k[len(prefix):]: v for k, v in a.items() if k.startswith(prefix)}
    g0, g1, f0, f1 = (part(p) for p in ("L0_gnn_", "L1_gnn_", "L0_ffn_", "L1_ffn_"))
    net = Net()
    tab1 = nc.dram_tensor("gcn_rows1", (NP, g0["W1"].shape[1]), F32).ap()
    tab2 = nc.dram_tensor("gcn_rows2", (NP, g0["W2"].shape[1]), F32).ap()
    gat_rows = nc.dram_tensor("gat_rows", (NP, GW), F32).ap()
    gat_logits = nc.dram_tensor("gat_logits", (NP, HEADS), F32).ap()
    x_mid = nc.dram_tensor("x_mid", (N, D), F32).ap()
    mixture_rows = nc.dram_tensor("mixture_rows", (NP, D), F32).ap()
    slot_rows = nc.dram_tensor("slot_rows", (BLOCKS * BLOCK, D), F32).ap()

    with ExitStack() as consts:
        alloc_constants(nc, net, consts)
        make_constants(nc, net)
        with ExitStack() as graph:
            alloc_edges(nc, net, graph)
            prepare_edges(nc, net, a["src"], a["dst"])
            alloc_nodes(nc, net, graph)
            with nc.sbuf_tensor("x0", [P, NT * D], F32) as net.x:
                load_nodes(nc, net, "load_x", a["x"], N)
                layer_stats(nc, net, "stats0")
                project(nc, net, "gcn1", "norm", D, g0["W1"], tab1.shape[1], tab1)
                gcn_pass(nc, net, "gcn1_pass", tab1, tab1.shape[1])
                project(nc, net, "gcn2", "relu", tab1.shape[1], g0["W2"], tab2.shape[1], tab2, bias=g0["b1"])
                gcn_pass(nc, net, "gcn2_pass", tab2, tab2.shape[1])
                fc_layers(nc, net, g0["b2"], g0["fc1_w"], g0["fc1_b"], g0["fc2_w"], g0["fc2_b"])
                layer_stats(nc, net, "stats1")
                small_mixture(nc, net, f0)
                layer_stats(nc, net, "stats2")
                project(nc, net, "gat0", "norm", D, g1["W0"], D, gat_rows,
                        logits=(g1["as0"], g1["ad0"], gat_logits))
                save_nodes(nc, net, "save_x", x_mid, N)
            for layer in range(3):
                if layer:
                    project(nc, net, f"gat{layer}", "copy", D, g1[f"W{layer}"], D, gat_rows,
                            logits=(g1[f"as{layer}"], g1[f"ad{layer}"], gat_logits))
                segment_max(nc, net, f"gat{layer}_max", gat_logits)
                gat_pass(nc, net, f"gat{layer}_pass", gat_rows)
                if layer < 2:
                    gat_finish(nc, net, f"gat{layer}_end", gat_rows, g1[f"b{layer}"], False)
            with nc.sbuf_tensor("x1", [P, NT * D], F32) as net.x:
                load_nodes(nc, net, "load_mid", x_mid, N)
                gat_finish(nc, net, "gat2_end", gat_rows, g1["b2"], True)
                save_nodes(nc, net, "save_mid", x_mid, N)
        with ExitStack() as last:
            alloc_mixture(nc, net, last, f1["Wr"].shape[1])
            load_nodes(nc, net, "load_last", x_mid, N)
            layer_stats(nc, net, "stats3", twice=True)
            route_nodes(nc, net, f1, mixture_rows)
            assign_slots(nc, net, f1["Wr"].shape[1])
            large_mixture(nc, net, f1, mixture_rows, slot_rows)
            collect_slots(nc, net, slot_rows)
            save_nodes(nc, net, "save_out", out, N)


def alloc_constants(nc, net, ctx):
    def sb(name, cols):
        return ctx.enter_context(nc.sbuf_tensor(name, [P, cols], F32))

    net.ident = sb("ident", P)
    net.iota = sb("iota", P)
    net.ones = sb("ones", P)
    net.part = sb("part", KC)


def alloc_mixture(nc, net, ctx, ne):
    def sb(name, shape, dt=F32):
        return ctx.enter_context(nc.sbuf_tensor(f"last_{name}", shape, dt))

    net.x = sb("x", [P, NT * D])
    net.mean = sb("mean", [P, NT])
    net.rstd = sb("rstd", [P, NT])
    net.rstd2 = sb("rstd2", [P, NT])
    net.chosen = sb("chosen", [P, ne, NT])
    net.weight = sb("weight", [P, ne, NT])
    net.slots = sb("slots", [P, 2 * NT], I32)
    net.share = sb("share", [P, 2, NT])
    net.node_of = sb("node_of", [P, SLOT_COLS], I32)
    net.block_expert = sb("block_expert", [1, BLOCKS], I32)


_INS = ['x', 'src', 'dst', 'L0_gnn_W1', 'L0_gnn_b1', 'L0_gnn_W2', 'L0_gnn_b2', 'L0_gnn_fc1_w', 'L0_gnn_fc1_b',
        'L0_gnn_fc2_w', 'L0_gnn_fc2_b', 'L0_ffn_sW1', 'L0_ffn_sb1', 'L0_ffn_sW2', 'L0_ffn_sb2', 'L0_ffn_sW3',
        'L0_ffn_sb3', 'L0_ffn_eW1', 'L0_ffn_eb1', 'L0_ffn_eW2', 'L0_ffn_eb2', 'L0_ffn_eW3', 'L0_ffn_eb3',
        'L0_ffn_gW', 'L0_ffn_gb', 'L1_gnn_W0', 'L1_gnn_as0', 'L1_gnn_ad0', 'L1_gnn_b0', 'L1_gnn_W1',
        'L1_gnn_as1', 'L1_gnn_ad1', 'L1_gnn_b1', 'L1_gnn_W2', 'L1_gnn_as2', 'L1_gnn_ad2', 'L1_gnn_b2',
        'L1_ffn_Wr', 'L1_ffn_br', 'L1_ffn_ln_g', 'L1_ffn_ln_b', 'L1_ffn_W1', 'L1_ffn_b1', 'L1_ffn_W2',
        'L1_ffn_b2']


def kernel(**inputs):
    import numpy as _np
    import concourse.bacc as _bacc
    from concourse import mybir as _mybir
    from concourse.bass_utils import run_bass_kernel_spmd as _run

    nc = _bacc.Bacc("TRN2", target_bir_lowering=False, num_devices=1)
    arrays, args = {}, {}
    for name in _INS:
        arr = _np.ascontiguousarray(inputs[name])
        arrays[f"in_{name}_dram"] = arr
        args[name] = nc.dram_tensor(f"in_{name}_dram", arr.shape, _mybir.dt.from_np(arr.dtype),
                                    kind="ExternalInput").ap()
    out = nc.dram_tensor("out_0_dram", (N, D), _mybir.dt.float32, kind="ExternalOutput").ap()
    program(nc, args, out)
    r = _run(nc, [arrays], core_ids=[0])
    return r.results[0]["out_0_dram"]
```

```python
from contextlib import ExitStack

import numpy as np

import concourse.bass as bass
from concourse import mybir
from concourse.alu_op_type import AluOpType as ALU

P = 128
N = 6250
E = 100000
D = 256
NT = (N + P - 1) // P
NP = NT * P
KT = (E + P - 1) // P
KC = (KT + P - 1) // P
KP = KC * P
NI = KT + NT - 1
HALF = 8
DEPTH = 4
STEPS = -(-NI // (DEPTH * HALF)) * DEPTH
NIP = STEPS * HALF
IC = NIP // 2
PAD_DST = 8191
BIG = 1.0e30
BT = 7
NB = NT // BT
BN = BT * P
HB = BN // 2
HEADS, HID = 4, 64
GW = D + HEADS
MW = D + 2 * HEADS
LN_EPS = 1e-5
BY_DMA = 9
DMA_STEPS = -(-KT // (BY_DMA + 2 * HALF) // 2) * 2
EXPERTS = 8
BLOCK = 256
BLOCKS = (2 * NP + EXPERTS * (BLOCK - 1)) // BLOCK
BLOCKS += BLOCKS % 2
SLOT_COLS = BLOCKS * BLOCK // P
FAR = 2.0 ** 20

F32 = mybir.dt.float32
BF16 = mybir.dt.bfloat16
I32 = mybir.dt.int32
ACT = mybir.ActivationFunctionType
AX = mybir.AxisListType.X
assert NT % BT == 0 and IC <= 512 and HB <= 512 and NB % 2 == 1 and NT <= P and NIP <= 8 * P


class Chain:

    def __init__(self, eng, sem):
        self.eng, self.sem, self.base, self.n = eng, sem, 0, 0

    def mark(self, ins):
        self.n += 1
        ins.then_inc(self.sem, 1)
        return ins

    def wait(self):
        self.eng.wait_ge(self.sem, self.base + self.n)

    def link(self, ins):
        self.mark(ins)
        self.wait()

    def enter(self, i, per_turn):
        self.before, self.per_turn = self.base + self.n, per_turn
        self.base, self.n = self.before + i * per_turn, 0

    def leave(self, turns):
        assert self.n == self.per_turn, (self.n, self.per_turn)
        self.base, self.n = self.before + turns * self.per_turn, 0


class Ring:

    def __init__(self, full, empty, banks, per_turn):
        self.full, self.empty, self.banks, self.per_turn = full, empty, banks, per_turn
        self.fill_n = self.drain_n = 0

    def give_credit(self, eng):
        eng.sem_inc(self.empty, self.per_turn)

    def fill(self, pe, i):
        u, r = self.fill_n % self.per_turn, len(self.banks)
        last = u - r + self.per_turn if u >= r else max(
            (v for v in range(self.per_turn) if v % r == u % r), default=u)
        pe.wait_ge(self.empty, i * self.per_turn + last + 1)
        self.fill_n += 1
        return self.banks[u % r]

    def settle(self, eng, i):
        eng.wait_ge(self.empty, (i + 1) * self.per_turn + (self.drain_n - 1) % self.per_turn + 1)

    def drain(self, eng, i):
        u = self.drain_n % self.per_turn
        eng.wait_ge(self.full, i * self.per_turn + u + 1)
        self.drain_n += 1
        return self.banks[u % len(self.banks)]


def refine_rsqrt(ch, dve, y, v, tmp):
    ch.link(dve.tensor_tensor(tmp, y, y, ALU.mult))
    ch.link(dve.scalar_tensor_tensor(out=tmp, in0=tmp, scalar=-0.5, in1=v, op0=ALU.mult, op1=ALU.mult))
    ch.link(dve.scalar_tensor_tensor(out=y, in0=tmp, scalar=1.5, in1=y, op0=ALU.add, op1=ALU.mult))


class Net:
    pass


def over(ap, n):
    ap = ap.unsqueeze(len(ap.shape))
    return ap.broadcast_to(list(ap.shape[:-1]) + [n])


def mid(ap, n):
    ap = ap.unsqueeze(1)
    return ap.broadcast_to([ap.shape[0], n, ap.shape[2]])


class Stage:

    def __init__(self, nc, name):
        self.nc, self.name, self.ctx, self.sems = nc, name, ExitStack(), []

    def __enter__(self):
        return self

    def __exit__(self, *a):
        self.nc.clear_and_free_semaphores(self.sems)
        self.nc.all_engine_barrier()
        self.ctx.close()

    def sb(self, name, shape, dt=F32):
        return self.ctx.enter_context(self.nc.sbuf_tensor(f"{self.name}_{name}", shape, dt))

    def ps(self, name, shape, dt=F32):
        return self.ctx.enter_context(self.nc.psum_tensor(f"{self.name}_{name}", shape, dt))

    def banks(self, n, name="bank"):
        return [self.ps(f"{name}{i}", [P, 512]) for i in range(n)]

    def sem(self, name):
        self.sems.append(self.nc.alloc_semaphore(f"{self.name}_{name}"))
        return self.sems[-1]


def make_constants(nc, net):
    with Stage(nc, "const") as st:
        made = st.sem("made")
        with nc.Block() as block:
            @block.gpsimd
            def _(pool):
                pool.iota(net.iota[:], [[1, P]], base=0, channel_multiplier=0,
                          allow_small_or_imprecise_dtypes=True)
                pool.iota(net.part[:], [[P, KC]], base=0, channel_multiplier=1,
                          allow_small_or_imprecise_dtypes=True)
                pool.memset(net.ones[:], 1.0)
                pool.memset(net.ident[:], 0.0).then_inc(made, 1)
                pool.wait_ge(made, 1)
                pool.affine_select(out=net.ident[:], in_=net.ident[:], compare_op=ALU.not_equal, fill=1.0,
                                   base=0, pattern=[[-1, P]], channel_multiplier=1)


def load_edges(dst_of, src):
    whole = E // (P * P)
    yield dst_of[:, 0:whole, :], src[0:whole * P * P].rearrange("(c p e) -> p c e", p=P, e=P)
    rows = (E - whole * P * P) // P
    yield dst_of[0:rows, whole, :], src[whole * P * P:(whole * P + rows) * P].rearrange("(p e) -> p e", e=P)
    at, left = (whole * P + rows) * P, E % P
    yield dst_of[rows:rows + 1, whole, 0:left], src[at:at + left].rearrange("(p e) -> p e", p=1)


def prepare_edges(nc, net, src, dst):
    with Stage(nc, "edges") as st:
        src_i, dst_i = st.sb("src_i", [P, KC, P], I32), st.sb("dst_i", [P, KC, P], I32)
        prev_i, next_i = st.sb("prev_i", [P, KC, P], I32), st.sb("next_i", [P, KC, P], I32)
        low_i = st.sb("low_i", [P, KC, P], I32)
        src_f, dst_f = st.sb("src_f", [P, KC, P]), st.sb("dst_f", [P, KC, P])
        first_f = st.sb("first_f", [P, KC, P])
        hi_f, lo_f = st.sb("hi_f", [P, KC, P]), st.sb("lo_f", [P, KC, P])
        hi_t, lo_t, cut_i = st.sb("hi_t", [P, KP]), st.sb("lo_t", [P, KP]), st.sb("cut_i", [P, KP], I32)
        d0, d127 = st.sb("d0", [HEADS, KP], I32), st.sb("d127", [HEADS, KP], I32)
        whole_run, link = st.sb("whole_run", [HEADS, KP]), st.sb("link", [HEADS, KP])
        one_hi, one_lo = st.sb("one_hi", [P, 2, HALF, NT], BF16), st.sb("one_lo", [P, 2, HALF, P], BF16)
        apart, far = st.sb("apart", [P, 2, HALF, NT]), st.sb("far", [P, 2, HALF, NT], BF16)
        zero = st.sb("zero", [P, P], BF16)
        count, per_tile = st.sb("count", [P, NT]), st.sb("per_tile", [P, 1])
        degree, spare = st.sb("degree", [P, NT]), st.sb("spare", [P, NT])
        below = st.sb("below", [P, P])
        kf_i, kf, first_item = st.sb("kf_i", [P, 1], I32), st.sb("kf", [P, 1]), st.sb("first_item", [P, 1])
        iota_i, begun = st.sb("iota_i", [P, NIP]), st.sb("begun", [NT, NIP])
        item_f = st.sb("item_f", [P, KC, NIP])
        t_all, k_all = st.sb("t_all", [P, NIP]), st.sb("k_all", [P, NIP])
        bank = st.banks(8)
        padded, loaded, rows = st.sem("padded"), st.sem("loaded"), st.sem("rows")
        ready, turned, copied = st.sem("ready"), st.sem("turned"), st.sem("copied")
        onehot, counted, chain, root = st.sem("onehot"), st.sem("counted"), st.sem("chain"), st.sem("root")
        pe_done, rooted, onehot_hi = st.sem("pe_done"), st.sem("rooted"), st.sem("onehot_hi")
        subtracted, measured = st.sem("subtracted"), st.sem("measured")

        with nc.allow_non_contiguous_dma(reason="a few columns, once"), nc.Block() as block:
            @block.gpsimd
            def _(pool):
                pool.iota(iota_i[:], [[1, NIP]], base=0, channel_multiplier=0,
                          allow_small_or_imprecise_dtypes=True).then_inc(padded, 1)
                for t, v in ((src_i, 0), (dst_i, PAD_DST), (prev_i, PAD_DST), (next_i, PAD_DST),
                             (d0, PAD_DST), (d127, PAD_DST)):
                    pool.memset(t[:], v).then_inc(padded, 1)
                pool.memset(zero[:], 0.0).then_inc(padded, 1)

                def subtract(h, col):
                    pool.tensor_tensor(apart[:, h], over(hi_t[:, col], NT), mid(net.iota[:, 0:NT], HALF),
                                       ALU.subtract).then_inc(subtracted, 1)

                pool.wait_ge(copied, KC)
                for h in range(2):
                    subtract(h, slice(h * HALF, (h + 1) * HALF))
                with pool.Fori(1, KT // (2 * HALF) + 1) as i:
                    for h in range(2):
                        pool.wait_ge(onehot_hi, 2 * i - 1 + h)
                        subtract(h, bass.ds(i * (2 * HALF) + h * HALF, HALF))

            @block.sync
            def _(sp):
                sp.wait_ge(padded, 7)
                n = 0
                for t, a in ((src_i, src), (dst_i, dst)):
                    for o, i in load_edges(t, a):
                        sp.dma_start(o, i).then_inc(loaded, 16)
                        n += 1
                sp.dma_start(d0[:, 0:KT], dst_column(dst, 0, KT)).then_inc(loaded, 16)
                sp.dma_start(d127[:, 0:E // P], dst_column(dst, P - 1, E // P)).then_inc(loaded, 16)
                sp.wait_ge(loaded, 16 * (n + 2))
                sp.dma_start(next_i[:, :, 0:P - 1], dst_i[:, :, 1:P]).then_inc(rows, 16)
                sp.dma_start(prev_i[:, :, 1:P], dst_i[:, :, 0:P - 1]).then_inc(rows, 16)
                sp.dma_start(prev_i[1:P, 0, 0:1], dst[0:(P - 1) * P].rearrange("(p e) -> p e", e=P)[:, P - 1:P])\
                    .then_inc(rows, 16)
                for c in range(1, KC):
                    n = min(P, KT - c * P)
                    sp.dma_start(prev_i[0:n, c, 0:1], bass.AP(dst.tensor, c * P * P - 1, [[P, n], [1, 1]]))\
                        .then_inc(rows, 16)

            @block.vector
            def _(dve):
                ch = Chain(dve, chain)
                dve.wait_ge(loaded, 16 * 8)
                dve.wait_ge(padded, 8)
                ch.link(dve.tensor_scalar(low_i[:], dst_i[:], 7, None, ALU.arith_shift_right))
                ch.link(dve.tensor_copy(hi_f[:], low_i[:]))
                ch.link(dve.tensor_scalar(low_i[:], dst_i[:], 127, None, ALU.bitwise_and))
                ch.link(dve.tensor_copy(lo_f[:], low_i[:]))
                ch.mark(dve.tensor_copy(dst_f[:], dst_i[:]))
                dve.tensor_copy(src_f[:], src_i[:]).then_inc(ready, 1)
                dve.wait_ge(ready, 1)
                for c in range(3 * KC):
                    dve.wait_ge(turned, c + 1)
                    t = (hi_t, lo_t, net.src_col)[c // KC]
                    dve.tensor_copy(t[:, c % KC * P:(c % KC + 1) * P], bank[c % 8][:, 0:P]).then_inc(copied, 1)
                dve.wait_ge(copied, 3 * KC)
                ch.link(dve.tensor_scalar(cut_i[:], net.src_col[:], 7, None, ALU.arith_shift_right))
                ch.link(dve.tensor_copy(net.src_hi[:], cut_i[:]))
                ch.link(dve.tensor_scalar(cut_i[:], net.src_col[:], 127, None, ALU.bitwise_and))
                ch.mark(dve.tensor_copy(net.src_lo[:], cut_i[:]))
                def low_rows(h, col):
                    dve.tensor_tensor(one_lo[:, h], over(lo_t[:, col], P), mid(net.iota[:], HALF),
                                      ALU.is_equal).then_inc(onehot, 1)

                for h in range(2):
                    low_rows(h, slice(h * HALF, (h + 1) * HALF))
                with dve.Fori(1, KT // (2 * HALF) + 1) as i:
                    for h in range(2):
                        dve.wait_ge(counted, 2 * i - 1 + h)
                        low_rows(h, bass.ds(i * (2 * HALF) + h * HALF, HALF))
                dve.wait_ge(pe_done, 1)
                ch.link(dve.tensor_copy(count[:], bank[0][:, 0:NT]))
                ch.link(dve.tensor_scalar(net.has_edge[:], count[:], 0.0, None, ALU.is_gt))
                ch.link(dve.tensor_scalar(degree[:], count[:], 1.0, None, ALU.add))
                ch.link(dve.reciprocal(net.dinv[:], degree[:]))
                dve.tensor_scalar(below[:], net.iota[:], net.part[:, 0:1], None, ALU.is_gt).then_inc(root, 1)
                dve.wait_ge(rooted, 1)
                refine_rsqrt(ch, dve, net.dinv[:], degree[:], spare[:])
                dve.wait_ge(pe_done, 2)
                dve.tensor_copy(per_tile[0:NT, :], bank[1][0:NT, 0:1]).then_inc(root, 1)
                dve.wait_ge(pe_done, 3)
                ch.link(dve.tensor_copy(kf_i[:], bank[2][:, 0:1]))
                ch.link(dve.tensor_scalar(kf_i[:], kf_i[:], 7, None, ALU.arith_shift_right))
                ch.link(dve.tensor_copy(kf[:], kf_i[:]))
                ch.link(dve.tensor_scalar(first_item[:], kf[:], float(KT - 1), net.part[:, 0:1], ALU.min, ALU.add))
                dve.tensor_scalar(begun[:], iota_i[0:NT, :], first_item[0:NT, 0:1], None, ALU.is_ge)\
                    .then_inc(root, 1)
                dve.wait_ge(pe_done, 4)
                for s in range(2):
                    ch.link(dve.tensor_scalar(t_all[:, s * IC:(s + 1) * IC], bank[3 + s][:, 0:IC], -1.0, None,
                                              ALU.add))
                ch.mark(dve.tensor_copy(net.t_of[:, 0:NIP], t_all[0:1, :]))
                ch.mark(dve.memset(net.t_of[:, NIP:NIP + HALF], NT - 1))
                ch.mark(dve.memset(net.dloc[:, NIP:NIP + HALF], -1.0))
                ch.link(dve.tensor_tensor(k_all[:], iota_i[:], t_all[:], ALU.subtract))
                dve.wait_ge(rows, 16 * (3 + KC - 1))
                ch.link(dve.tensor_tensor(first_f[:], dst_i[:], prev_i[:], ALU.not_equal))
                for c in range(KC):
                    last = dve.tensor_scalar(item_f[:, c, :], k_all[:], net.part[:, c:c + 1], None,
                                             ALU.is_equal)
                last.then_inc(root, 1)
                dve.wait_ge(root, 4)
                ch.mark(dve.tensor_copy(net.item_of[:], item_f[:]))
                ch.link(dve.tensor_scalar(net.run_start[:], first_f[:], -BIG, None, ALU.mult))
                ch.mark(dve.memset(net.run_start[:, :, 0:1], -BIG))
                ch.link(dve.tensor_tensor(net.run_end[:], dst_i[:], next_i[:], ALU.not_equal))
                ch.link(dve.tensor_scalar(net.run_end[:], net.run_end[:], -BIG, None, ALU.mult))
                ch.mark(dve.memset(net.run_end[:, :, P - 1:P], -BIG))
                for m, at in ((net.not_first_run, 0), (net.not_last_run, P - 1)):
                    ch.link(dve.tensor_tensor(m[:], dst_f[:], dst_f[:, :, at:at + 1].broadcast_to([P, KC, P]),
                                              ALU.not_equal))
                    ch.mark(dve.tensor_scalar(m[:], m[:], -BIG, None, ALU.mult))
                ch.link(dve.tensor_tensor(whole_run[:], d0[:], d127[:], ALU.not_equal))
                ch.link(dve.tensor_scalar(whole_run[:], whole_run[:], -BIG, None, ALU.mult))
                ch.link(dve.tensor_tensor(link[:, 1:KP], d0[:, 1:KP], d127[:, 0:KP - 1], ALU.not_equal))
                ch.link(dve.tensor_scalar(net.link_left[:, 1:KP], link[:, 1:KP], -BIG, None, ALU.mult))
                ch.mark(dve.tensor_scalar(net.link_right[:, 0:KP - 1], link[:, 1:KP], -BIG, None, ALU.mult))
                ch.mark(dve.memset(net.link_left[:, 0:1], -BIG))
                ch.mark(dve.memset(net.link_right[:, KP - 1:KP], -BIG))
                ch.mark(dve.memset(net.pass_left[:, 0:1], -BIG))
                ch.link(dve.memset(net.pass_right[:, KP - 1:KP], -BIG))
                ch.link(dve.tensor_tensor(net.pass_left[:, 1:KP], whole_run[:, 0:KP - 1],
                                          net.link_left[:, 1:KP], ALU.min))
                ch.link(dve.tensor_tensor(net.pass_right[:, 0:KP - 1], whole_run[:, 1:KP],
                                          net.link_right[:, 0:KP - 1], ALU.min))
                for n in range(6):
                    what, s = n // 2, n % 2
                    cols = ITEM_HALVES[s]
                    dve.wait_ge(pe_done, 5 + n)
                    b = bank[n][:, 0:cols.stop - cols.start]
                    if what == 0:
                        ch.mark(dve.tensor_copy(net.src_of[:, cols], b))
                    elif what == 1:
                        ch.mark(dve.scalar_tensor_tensor(out=net.dloc[:, cols], in0=t_all[:, cols],
                                                         scalar=-float(P), in1=b, op0=ALU.mult, op1=ALU.add))
                    else:
                        ch.mark(dve.tensor_copy(net.first_of[:, cols], b))
                ch.wait()

            @block.scalar
            def _(act):
                def measure(q, h):
                    act.wait_ge(subtracted, q + 1)
                    act.activation(far[:, h], apart[:, h], ACT.Abs).then_inc(measured, 1)
                    act.wait_ge(measured, q + 1)

                def high_rows(h):
                    act.activation(one_hi[:, h], far[:, h], ACT.Relu, bias=net.ones[:, 0:1], scale=-1.0)\
                        .then_inc(onehot_hi, 1)

                for h in range(2):
                    measure(h, h)
                    high_rows(h)
                with act.Fori(1, KT // (2 * HALF) + 1) as i:
                    for h in range(2):
                        act.wait_ge(onehot_hi, 2 * i - 1 + h)
                        measure(2 * i + h, h)
                        act.wait_ge(counted, 2 * i - 1 + h)
                        high_rows(h)
                act.wait_ge(root, 1)
                act.activation(net.dinv[:], net.dinv[:], ACT.Sqrt).then_inc(rooted, 1)

            @block.tensor
            def _(pe):
                pe.wait_ge(ready, 1)
                for c in range(3 * KC):
                    if c >= 8:
                        pe.wait_ge(copied, c - 7)
                    pe.transpose(bank[c % 8][:, 0:P], (hi_f, lo_f, src_f)[c // KC][:, c % KC, :], net.ident[:])\
                        .then_inc(turned, 1)
                pe.wait_ge(padded, 8)
                pe.wait_ge(copied, 3 * KC)
                counts = bank[0][:, 0:NT]
                pe.matmul(counts, zero[:], zero[:, 0:NT], start=True, stop=False, skip_group_check=True)
                with pe.Fori(0, KT // (2 * HALF) + 1) as i:
                    for h in range(2):
                        pe.wait_ge(onehot, 2 * i + h + 1)
                        pe.wait_ge(onehot_hi, 2 * i + h + 1)
                        for j in range(HALF):
                            mm = pe.matmul(counts, one_lo[:, h, j, :], one_hi[:, h, j, :], start=False,
                                           stop=False, skip_group_check=True)
                        mm.then_inc(counted, 1)
                pe.matmul(counts, zero[:], zero[:, 0:NT], start=False, stop=True, skip_group_check=True)\
                    .then_inc(pe_done, 1)
                pe.wait_ge(root, 1)
                pe.matmul(bank[1][0:NT, 0:1], count[:], net.ones[:, 0:1], start=True, stop=True)\
                    .then_inc(pe_done, 1)
                pe.wait_ge(root, 2)
                pe.matmul(bank[2][:, 0:1], below[0:NT, :], per_tile[0:NT, :], start=True, stop=True)\
                    .then_inc(pe_done, 1)
                pe.wait_ge(root, 3)
                for s in range(2):
                    mm = pe.matmul(bank[3 + s][:, 0:IC], net.ones[0:NT, :], begun[:, s * IC:(s + 1) * IC],
                                   start=True, stop=True)
                mm.then_inc(pe_done, 1)
                pe.wait_ge(root, 4)
                for n in range(6):
                    rows_of, s = (src_f, dst_f, first_f)[n // 2], n % 2
                    in_item_order(pe, bank[n], s, lambda c: rows_of[:, c, :], item_f).then_inc(pe_done, 1)


ITEM_HALVES = (slice(0, 4 * P), slice(4 * P, NIP))


def in_item_order(pe, bank, s, tiles, one_hot):
    cols = ITEM_HALVES[s]
    for m in range(cols.start // P, -(-cols.stop // P)):
        at = slice(m * P, min((m + 1) * P, cols.stop))
        chunks = [c for c in (m - 1, m) if 0 <= c < KC]
        for c in chunks:
            mm = pe.matmul(bank[:, at.start - cols.start:at.stop - cols.start], tiles(c), one_hot[:, c, at],
                           start=c == chunks[0], stop=c == chunks[-1])
    return mm


def dst_column(dst, at, n):
    return bass.AP(dst.tensor, dst.offset + at, [[0, HEADS], [P, n], [1, 1]])


def alloc_edges(nc, net, ctx):
    def sb(name, shape, dt=F32):
        return ctx.enter_context(nc.sbuf_tensor(name, shape, dt))

    net.has_edge = sb("has_edge", [P, NT])
    net.dinv = sb("dinv", [P, NT])
    net.src_col = sb("src_col", [P, KP], I32)
    net.src_hi = sb("src_hi", [P, KP], BF16)
    net.src_lo = sb("src_lo", [P, KP], BF16)
    net.src_of = sb("src_of", [P, NIP], I32)
    net.dloc = sb("dloc", [P, NIP + HALF])
    net.first_of = sb("first_of", [P, NIP], BF16)
    net.t_of = sb("t_of", [1, NIP + HALF], I32)
    net.item_of = sb("item_of", [P, KC, NIP], BF16)
    net.run_start = sb("run_start", [P, KC, P], BF16)
    net.run_end = sb("run_end", [P, KC, P], BF16)
    net.not_first_run = sb("not_first_run", [P, KC, P], BF16)
    net.not_last_run = sb("not_last_run", [P, KC, P], BF16)
    net.link_left = sb("link_left", [HEADS, KP], BF16)
    net.link_right = sb("link_right", [HEADS, KP], BF16)
    net.pass_left = sb("pass_left", [HEADS, KP], BF16)
    net.pass_right = sb("pass_right", [HEADS, KP], BF16)


def gather_rows(pool, table, slots, columns, index, gathered, indexed, go, freed, least, own_index=True):
    depth, n = slots.shape[1:3]
    steps = columns.shape[1] // n

    def turn(i, first):
        for h in range(depth):
            q = i * depth + h
            if not first:
                pool.wait_ge(freed, least(q))
            if own_index:
                if not first:
                    pool.wait_ge(gathered[h], 16 * n * i)
                pool.tensor_copy(index[:, h, :], columns[:, bass.ds(q * n, n)]).then_inc(indexed, 1)
            pool.wait_ge(indexed, q + 1)
            pool.sem_inc(go, 1)
            for j in range(n):
                pool.indirect_dma_start(slots[:, h, j, :], None, table,
                                        bass.IndirectOffsetOnAxis(ap=index[:, h, j:j + 1], axis=0))\
                    .then_inc(gathered[h], 16)

    turn(0, True)
    with pool.Fori(1, steps // depth) as i:
        turn(i, False)


def index_step(act, columns, index, gathered, indexed, q, h, turn):
    n = index.shape[2]
    if not (isinstance(turn, int) and turn == 0):
        act.wait_ge(gathered[h], turn * (16 * n))
    act.activation(index[:, h, :], columns[:, bass.ds(q * n, n)], ACT.Copy).then_inc(indexed, 1)


def gcn_pass(nc, net, name, table, width):
    with Stage(nc, name) as st:
        index = st.sb("index", [P, 2, HALF], I32)
        rows, onehot = st.sb("rows", [P, 2, HALF, width]), st.sb("onehot", [P, 2, HALF, P])
        bank = st.banks(HALF)
        gathered = [st.sem("gathered0"), st.sem("gathered1")]
        indexed, go, made, summed, added = (st.sem(x) for x in ("indexed", "go", "made", "summed", "added"))

        with nc.Block() as block:
            @block.gpsimd
            def _(pool):
                gather_rows(pool, table, rows, net.src_of, index, gathered, indexed, go, summed,
                            lambda q: (q - 1) * HALF, own_index=False)

            @block.scalar
            def _(act):
                for h in range(2):
                    index_step(act, net.src_of, index, gathered, indexed, h, h, 0)
                with act.Fori(1, STEPS // 2) as i:
                    for h in range(2):
                        index_step(act, net.src_of, index, gathered, indexed, i * 2 + h, h, i)

            @block.vector
            def _(dve):
                tile = [dve.alloc_register(f"{name}_t{j}") for j in range(HALF)]

                def one_hot(col, h):
                    dve.tensor_tensor(onehot[:, h], over(net.dloc[:, col], P), mid(net.iota[:], HALF),
                                      ALU.is_equal).then_inc(made, 1)

                def accumulate(q, first):
                    dve.load(tile, net.t_of[0:1, bass.ds(q * HALF, HALF)])
                    for j in range(HALF):
                        dve.wait_ge(summed, q * HALF + j + 1)
                        if not (first and j == 0):
                            dve.wait_ge(added, q * HALF + j)
                        acc = net.acc[:, bass.ds(dve.snap(tile[j], min_val=0, max_val=NT - 1) * MW, width)]
                        dve.tensor_tensor(acc, acc, bank[j][:, 0:width], ALU.add).then_inc(added, 1)

                one_hot(slice(0, HALF), 0)
                one_hot(slice(HALF, 2 * HALF), 1)
                accumulate(0, True)
                with dve.Fori(0, STEPS // 2 - 1) as i:
                    for h in range(2):
                        one_hot(bass.ds(i * (2 * HALF) + (2 + h) * HALF, HALF), h)
                        accumulate(i * 2 + h + 1, False)
                accumulate(STEPS - 1, False)

            @block.tensor
            def _(pe):
                def turn(i, first):
                    for h in range(2):
                        pe.wait_ge(made, i * 2 + h + 1)
                        pe.wait_ge(gathered[h], P * i + P)
                        for j in range(HALF):
                            if not first or h:
                                pe.wait_ge(added, (i * 2 + h - 1) * HALF + j + 1)
                            pe.matmul(bank[j][:, 0:width], onehot[:, h, j, :], rows[:, h, j, :],
                                      start=True, stop=True).then_inc(summed, 1)

                turn(0, True)
                with pe.Fori(1, STEPS // 2) as i:
                    turn(i, False)


def layer_stats(nc, net, name, twice=False, load=None):
    with Stage(nc, name) as st:
        stats, aggr = st.sb("stats", [P, NT, 6]), st.sb("aggr", [P, NT, 2])
        var, spare = st.sb("var", [P, NT]), st.sb("spare", [P, NT])
        chain, ready, rooted = st.sem("chain"), st.sem("ready"), st.sem("rooted")
        cleared, loaded = st.sem("cleared"), [st.sem(f"loaded{n}") for n in range(NB)] if load else None
        with nc.Block() as block:
            @block.gpsimd
            def _(pool):
                if load:
                    pool.memset(net.x[:, (NT - 1) * D:NT * D], 0.0).then_inc(cleared, 1)

            @block.sync
            def _(sp):
                if load:
                    sp.wait_ge(cleared, 1)
                    for n, (o, i) in enumerate(node_pieces(net, *load)):
                        sp.dma_start(o, i).then_inc(loaded[min(n, NB - 1)], 16)

            @block.vector
            def _(dve):
                ch = Chain(dve, chain)
                for t in range(NT):
                    if load and t % BT == 0:
                        rest = len(node_pieces(net, *load)) - NB
                        dve.wait_ge(loaded[t // BT], 16 + (16 * rest if t // BT == NB - 1 else 0))
                    ch.mark(dve.bn_stats(stats[:, t, :], net.x[:, t * D:(t + 1) * D]))
                ch.wait()
                for t in range(NT):
                    ch.mark(dve.bn_aggr(aggr[:, t, :], stats[:, t, :]))
                ch.wait()
                ch.mark(dve.tensor_copy(net.mean[:], aggr[:, :, 0]))
                ch.link(dve.tensor_scalar(var[:], aggr[:, :, 1], LN_EPS, None, ALU.add))
                dve.reciprocal(net.rstd[:], var[:]).then_inc(ready, 1)
                dve.wait_ge(rooted, 1)
                refine_rsqrt(ch, dve, net.rstd[:], var[:], spare[:])
                if twice:
                    ch.link(dve.tensor_tensor(var[:], net.rstd[:], net.rstd[:], ALU.mult))
                    ch.link(dve.tensor_tensor(var[:], var[:], aggr[:, :, 1], ALU.mult))
                    ch.link(dve.tensor_scalar(var[:], var[:], LN_EPS, None, ALU.add))
                    dve.reciprocal(net.rstd2[:], var[:]).then_inc(ready, 1)
                    dve.wait_ge(rooted, 2)
                    refine_rsqrt(ch, dve, net.rstd2[:], var[:], spare[:])

            @block.scalar
            def _(act):
                act.wait_ge(ready, 1)
                act.activation(net.rstd[:], net.rstd[:], ACT.Sqrt).then_inc(rooted, 1)
                if twice:
                    act.wait_ge(ready, 2)
                    act.activation(net.rstd2[:], net.rstd2[:], ACT.Sqrt).then_inc(rooted, 1)


def project(nc, net, name, prep, w_in, weight, w_out, table, bias=None, logits=None, aside=None):
    kc = w_in // P
    per_in = -(-kc * BT // 4)
    wide = w_out + (2 * HEADS if logits else 0)
    tw = w_out + (HEADS if logits else 0)
    per = min(512 // wide, 4)
    per_out = -(-BT // per)
    with Stage(nc, name) as st:
        xn, xt = st.sb("xn", [P, BT, w_in]), st.sb("xt", [P, 2, kc, BN])
        w_sb = st.sb("w", [P, kc, wide])
        b_sb = st.sb("b", [P, w_in]) if bias is not None else None
        outb = st.sb("out", [P, 2, BT, tw])
        part = st.sb("part", [P, 3, BT])
        if logits:
            a_sb, prod = st.sb("a", [P, 2, w_out]), st.sb("prod", [P, kc, w_out])
            lg, zero = st.sb("lg", [P, 2, BT, 2 * HEADS]), st.sb("zero", [P, 1])
        loaded, xn_ready, out_ready, chain = (st.sem(x) for x in ("loaded", "xn_ready", "out_ready", "chain"))
        joined, cleared, saved = st.sem("joined"), st.sem("cleared"), st.sem("saved")
        to_save = node_pieces(net, *aside) if aside else []
        stored = [st.sem("stored0"), st.sem("stored1")]
        turned = Ring(st.sem("turned"), st.sem("turned_free"), st.banks(4, "t"), per_in)
        product = Ring(st.sem("product"), st.sem("product_free"), st.banks(4, "m"), per_out)
        n_loads = 1 + (bias is not None) + 2 * bool(logits)
        n_stores = 2 if logits else 1

        with nc.allow_non_contiguous_dma(reason="weights, once"), nc.Block() as block:
            @block.sync
            def _(sp):
                sp.dma_start(w_sb[:, :, 0:w_out], weight.rearrange("(c k) m -> k c m", k=P)).then_inc(loaded, 16)
                if bias is not None:
                    sp.dma_start(b_sb[:], bias.partition_broadcast(P)).then_inc(loaded, 16)
                if logits:
                    for s in range(2):
                        sp.dma_start(a_sb[:, s, :], logits[s].rearrange("h f -> (h f)").partition_broadcast(P))\
                            .then_inc(loaded, 16)
                view = table.rearrange("(t p) w -> p t w", p=P)
                for h in range(2):
                    sp.sem_inc(stored[h], 16 * n_stores)
                for i, o in to_save:
                    sp.dma_start(o, i).then_inc(saved, 16)

                def store(b, h):
                    sp.wait_ge(out_ready, b + 1)
                    sp.dma_start(view[:, bass.ds(b * BT, BT), :], outb[:, h]).then_inc(stored[h], 16)
                    if logits:
                        sp.dma_start(logits[2].rearrange("(t p) w -> p t w", p=P)[:, bass.ds(b * BT, BT), :],
                                     lg[:, h, :, 0:HEADS]).then_inc(stored[h], 16)

                with sp.Fori(0, NB // 2) as i:
                    for h in range(2):
                        store(i * 2 + h, h)
                store(NB - 1, 0)
                if to_save:
                    sp.wait_ge(saved, 16 * len(to_save))
                for h in range(2):
                    sp.wait_ge(stored[h], 16 * n_stores * (NB // 2 + 2 - h))

            @block.gpsimd
            def _(pool):
                if logits:
                    pool.memset(zero[:], 0.0).then_inc(cleared, 1)
                    pool.wait_ge(cleared, 1)
                    with pool.Fori(0, NB) as b:
                        pool.wait_ge(xn_ready, b + 1)
                        pool.sem_inc(cleared, 1)
                        pool.tensor_copy(net.acc[:, bass.ds(b * (BT * MW), BT * MW)],
                                         zero[:].broadcast_to([P, BT * MW]))

            @block.vector
            def _(dve):
                ch = Chain(dve, chain)
                product.give_credit(dve)
                dve.wait_ge(loaded, 16 * n_loads)

                def prepare(b):
                    if prep == "norm":
                        ch.mark(dve.tensor_copy(part[:, 0, :], net.mean[:, bass.ds(b * BT, BT)]))
                        ch.link(dve.tensor_copy(part[:, 1, :], net.rstd[:, bass.ds(b * BT, BT)]))
                        for j in range(BT):
                            last = dve.tensor_scalar(xn[:, j, :], net.x[:, bass.ds(b * (BT * D) + j * D, D)],
                                                     part[:, 0, j:j + 1], part[:, 1, j:j + 1],
                                                     ALU.subtract, ALU.mult)
                    elif prep == "relu":
                        ch.link(dve.tensor_copy(part[:, 0, :], net.dinv[:, bass.ds(b * BT, BT)]))
                        for j in range(BT):
                            ch.mark(dve.scalar_tensor_tensor(
                                out=xn[:, j, :], in0=net.acc[:, bass.ds(b * (BT * MW) + j * MW, w_in)],
                                scalar=part[:, 0, j:j + 1], in1=b_sb[:], op0=ALU.mult, op1=ALU.add))
                        ch.wait()
                        last = dve.tensor_scalar(xn[:], xn[:], 0.0, None, ALU.max)
                    else:
                        for j in range(BT):
                            last = dve.tensor_copy(xn[:, j, :], net.acc[:, bass.ds(b * (BT * MW) + j * MW, w_in)])
                    last.then_inc(xn_ready, 1)

                marks_prep = {"norm": 2, "relu": 1 + BT, "copy": 0}[prep]

                def finish(b, h, turn):
                    dve.wait_ge(stored[h], turn * (16 * n_stores) + 16 * n_stores)
                    if not logits:
                        ch.link(dve.tensor_copy(part[:, 2, :], net.dinv[:, bass.ds(b * BT, BT)]))
                    for u in range(per_out):
                        bank = product.drain(dve, b)
                        j0, n = u * per, min(per, BT - u * per)
                        src = bank[:, 0:n * wide].rearrange("p (j w) -> p j w", w=wide)
                        if logits:
                            ch.mark(dve.tensor_copy(outb[:, h, j0:j0 + n, :], src[:, :, 0:tw]))
                            dve.tensor_copy(lg[:, h, j0:j0 + n, :], src[:, :, w_out:wide]).then_inc(product.empty, 1)
                        else:
                            dve.tensor_tensor(outb[:, h, j0:j0 + n, :], src, over(part[:, 2, j0:j0 + n], w_out),
                                              ALU.mult).then_inc(product.empty, 1)
                    if logits:
                        ch.wait()
                    product.settle(dve, b)
                    if logits:
                        dve.tensor_copy(net.logit[:, bass.ds(b * (BT * 2 * HEADS), BT * 2 * HEADS)],
                                        lg[:, h].rearrange("p j a -> p (j a)")).then_inc(out_ready, 1)
                    else:
                        for j in range(BT):
                            last = dve.tensor_copy(net.acc[:, bass.ds(b * (BT * MW) + j * MW, w_out)],
                                                   outb[:, h, j, :])
                        last.then_inc(out_ready, 1)

                marks_finish = per_out if logits else 1
                prepare(0)
                if logits:
                    for s in range(2):
                        ch.link(dve.tensor_tensor(prod[:], w_sb[:, :, 0:w_out], mid(a_sb[:, s, :], kc), ALU.mult))
                        ch.link(dve.tensor_reduce(w_sb[:, :, w_out + s * HEADS:w_out + (s + 1) * HEADS],
                                                  prod[:].rearrange("p c (h f) -> p c h f", f=HID), AX, ALU.add))
                dve.sem_inc(joined, 1)

                def prepare_next(b):
                    dve.wait_ge(turned.full, b * per_in)
                    dve.sem_inc(joined, 1)
                    prepare(b)

                prepare_next(1)
                with dve.Fori(0, NB // 2 - 1) as i:
                    ch.enter(i, 2 * (marks_prep + marks_finish))
                    for h in range(2):
                        prepare_next(i * 2 + h + 2)
                        finish(i * 2 + h, h, i)
                    ch.leave(NB // 2 - 1)
                for b in range(NB - 3, NB):
                    if b == NB - 3:
                        prepare_next(b + 2)
                    finish(b, b % 2, b // 2)

            @block.scalar
            def _(act):
                turned.give_credit(act)

                def copy_turned(b, h):
                    flat = xt[:, h].rearrange("p c n -> p (c n)")
                    for u in range(per_in):
                        n = min(4, kc * BT - 4 * u) * P
                        bank = turned.drain(act, b)
                        act.activation(flat[:, u * 512:u * 512 + n], bank[:, 0:n], ACT.Copy)\
                            .then_inc(turned.empty, 1)

                with act.Fori(0, NB // 2) as i:
                    for h in range(2):
                        copy_turned(i * 2 + h, h)
                copy_turned(NB - 1, 0)

            @block.tensor
            def _(pe):
                def turn_over(b):
                    pe.wait_ge(xn_ready, b + 1)
                    for u in range(per_in):
                        bank = turned.fill(pe, b)
                        for m in range(4 * u, min(4 * u + 4, kc * BT)):
                            mm = pe.transpose(bank[:, m % 4 * P:(m % 4 + 1) * P],
                                              xn[:, m % BT, m // BT * P:(m // BT + 1) * P], net.ident[:])
                        mm.then_inc(turned.full, 1)

                def multiply(b, h):
                    pe.wait_ge(turned.empty, (b + 2) * per_in)
                    for u in range(per_out):
                        bank = product.fill(pe, b)
                        for j in range(u * per, min(u * per + per, BT)):
                            at = (j - u * per) * wide
                            for c in range(kc):
                                mm = pe.matmul(bank[:, at:at + wide], xt[:, h, c, j * P:(j + 1) * P],
                                               w_sb[:, c, :], start=c == 0, stop=c == kc - 1)
                        mm.then_inc(product.full, 1)

                turn_over(0)
                pe.wait_ge(joined, 1)
                with pe.Fori(0, NB // 2) as i:
                    for h in range(2):
                        turn_over(i * 2 + h + 1)
                        multiply(i * 2 + h, h)
                multiply(NB - 1, 0)


def alloc_nodes(nc, net, ctx):
    def sb(name, shape, dt=F32):
        return ctx.enter_context(nc.sbuf_tensor(name, shape, dt))

    net.acc = sb("acc", [P, NT * MW])
    net.logit = sb("logit", [P, NT * 2 * HEADS])
    net.mean = sb("mean", [P, NT])
    net.rstd = sb("rstd", [P, NT])


def node_pieces(net, x, n):
    full = n // P
    pieces = []
    for t0 in range(0, full, BT):
        t1 = min(full, t0 + BT)
        pieces.append((net.x[:, t0 * D:t1 * D].rearrange("p (t w) -> p t w", w=D),
                       x[t0 * P:t1 * P, :].rearrange("(t p) w -> p t w", p=P)))
    if n % P:
        pieces.append((net.x[0:n % P, full * D:(full + 1) * D], x[full * P:n, :]))
    return pieces


def fc_layers(nc, net, bias, w1, b1, w2, b2):
    h, m = w1.shape
    with Stage(nc, "fc") as st:
        bias_sb, part = st.sb("bias", [P, h]), st.sb("part", [P, BT])
        w1_sb, w2_sb = st.sb("w1", [h, m]), st.sb("w2", [m, D])
        b1_sb, b2_sb = st.sb("b1", [m, 1]), st.sb("b2", [P, D])
        rows, ht, ft = st.sb("rows", [P, BT, h]), st.sb("ht", [h, BN]), st.sb("ft", [m, BN])
        loaded, ready, chain, begun = st.sem("loaded"), st.sem("ready"), st.sem("chain"), st.sem("begun")
        flipped = Ring(st.sem("flipped"), st.sem("flipped_free"), st.banks(2, "x"), 2)
        cols = Ring(st.sem("cols"), st.sem("cols_free"), st.banks(2, "c"), 2)
        outs = Ring(st.sem("outs"), st.sem("outs_free"), st.banks(4, "o"), 4)

        with nc.allow_non_contiguous_dma(reason="a bias, once"), nc.Block() as block:
            @block.sync
            def _(sp):
                for o, i in ((bias_sb, bias.partition_broadcast(P)), (w1_sb, w1), (w2_sb, w2),
                             (b1_sb, b1.rearrange("(k o) -> k o", o=1)), (b2_sb, b2.partition_broadcast(P))):
                    sp.dma_start(o[:], i).then_inc(loaded, 16)

            @block.vector
            def _(dve):
                ch = Chain(dve, chain)
                outs.give_credit(dve)
                dve.wait_ge(loaded, 80)

                def prepare(b):
                    ch.link(dve.tensor_copy(part[:], net.dinv[:, bass.ds(b * BT, BT)]))
                    for j in range(BT):
                        ch.mark(dve.scalar_tensor_tensor(
                            out=rows[:, j, :], in0=net.acc[:, bass.ds(b * (BT * MW) + j * MW, h)],
                            scalar=part[:, j:j + 1], in1=bias_sb[:], op0=ALU.mult, op1=ALU.add))
                    ch.wait()
                    dve.tensor_scalar(rows[:], rows[:], 0.0, None, ALU.max).then_inc(ready, 1)

                def finish(b):
                    x = net.x[:, bass.ds(b * (BT * D), BT * D)].rearrange("p (j w) -> p j w", w=D)
                    ch.link(dve.tensor_tensor(x, x, mid(b2_sb[:], BT), ALU.add))
                    for u in range(4):
                        bank = outs.drain(dve, b)
                        n = min(2, BT - 2 * u)
                        x = net.x[:, bass.ds(b * (BT * D) + 2 * u * D, n * D)]
                        dve.tensor_tensor(x, x, bank[:, 0:n * D], ALU.add).then_inc(outs.empty, 1)

                prepare(0)
                with dve.Fori(0, NB - 1) as b:
                    ch.enter(b, 2 + BT)
                    dve.wait_ge(flipped.full, b * 2 + 2)
                    prepare(b + 1)
                    finish(b)
                    ch.leave(NB - 1)
                finish(NB - 1)

            @block.scalar
            def _(act):
                flipped.give_credit(act)
                cols.give_credit(act)
                act.wait_ge(loaded, 80)

                def copy_flipped(b):
                    for u in range(2):
                        n = min(4, BT - 4 * u) * P
                        act.activation(ht[:, u * 512:u * 512 + n], flipped.drain(act, b)[0:h, 0:n], ACT.Copy)\
                            .then_inc(flipped.empty, 1)

                def first_layer(b):
                    for u in range(2):
                        act.activation(ft[:, u * HB:(u + 1) * HB], cols.drain(act, b)[0:m, 0:HB], ACT.Identity,
                                       bias=b1_sb[:]).then_inc(cols.empty, 1)

                copy_flipped(0)
                with act.Fori(0, NB - 1) as b:
                    first_layer(b)
                    copy_flipped(b + 1)
                first_layer(NB - 1)

            @block.tensor
            def _(pe):
                pe.wait_ge(loaded, 80)

                def turn_over(b):
                    pe.wait_ge(ready, b + 1)
                    for u in range(2):
                        bank = flipped.fill(pe, b)
                        pe.sem_inc(begun, 1)
                        for j in range(4 * u, min(4 * u + 4, BT)):
                            mm = pe.transpose(bank[0:h, j % 4 * P:(j % 4 + 1) * P], rows[:, j, :], net.ident[:])
                        mm.then_inc(flipped.full, 1)

                def first_layer(b):
                    pe.wait_ge(flipped.empty, b * 2 + 4)
                    for u in range(2):
                        pe.matmul(cols.fill(pe, b)[0:m, 0:HB], w1_sb[:], ht[:, u * HB:(u + 1) * HB],
                                  start=True, stop=True).then_inc(cols.full, 1)

                def second_layer(b):
                    pe.wait_ge(cols.empty, b * 2 + 4)
                    for u in range(4):
                        bank = outs.fill(pe, b)
                        for j in range(2 * u, min(2 * u + 2, BT)):
                            mm = pe.matmul(bank[:, (j - 2 * u) * D:(j - 2 * u + 1) * D],
                                           ft[:, j * P:(j + 1) * P], w2_sb[:], start=True, stop=True)
                        mm.then_inc(outs.full, 1)

                turn_over(0)
                with pe.Fori(0, NB - 1) as b:
                    first_layer(b)
                    turn_over(b + 1)
                    second_layer(b)
                first_layer(NB - 1)
                second_layer(NB - 1)


class Gate:
    marks = 15

    def __init__(self, st, ne, again):
        self.ne, self.again = ne, again
        self.p, self.q = st.sb("gate_p", [P, BT, ne]), st.sb("gate_q", [P, BT, ne])
        self.ex, self.ex2 = st.sb("gate_ex", [P, BT, ne]), st.sb("gate_ex2", [P, BT, ne])
        self.row, self.low = st.sb("gate_row", [P, BT]), st.sb("gate_low", [P, ne, ne])
        self.above, self.same = st.sb("gate_above", [P, BT, ne, ne]), st.sb("gate_same", [P, BT, ne, ne])
        self.bias = st.sb("gate_bias", [P, ne])
        self.shifted, self.raised = st.sem("gate_shifted"), st.sem("gate_raised")
        self.calls = 1 + again
        self.chosen = None if again else st.sb("gate_chosen", [P, BT, ne])

    def order(self, ch, dve, net):
        for e in range(self.ne):
            ch.mark(dve.tensor_scalar(self.low[:, e, :], net.iota[:, 0:self.ne], float(e), None, ALU.is_lt))
        ch.wait()

    def weights(self, ch, dve, i, logits, drained):
        p, q, row, ne = self.p, self.q, self.row, self.ne
        dve.tensor_tensor(p[:], logits.rearrange("p (j e) -> p j e", e=ne), mid(self.bias[:], BT), ALU.add)\
            .then_inc(drained.empty, 1)
        drained.settle(dve, i)
        ch.link(dve.tensor_reduce(row[:], p[:], AX, ALU.max))
        dve.tensor_tensor(p[:], p[:], over(row[:], ne), ALU.subtract).then_inc(self.shifted, 1)
        dve.wait_ge(self.raised, i * self.calls + 1)
        ch.link(dve.tensor_reduce(row[:], self.ex[:], AX, ALU.add))
        ch.link(dve.reciprocal(row[:], row[:]))
        ch.link(dve.tensor_tensor(p[:], self.ex[:], over(row[:], ne), ALU.mult))
        one, other = p[:].unsqueeze(3).broadcast_to([P, BT, ne, ne]), p[:].unsqueeze(2).broadcast_to([P, BT, ne, ne])
        ch.mark(dve.tensor_tensor(self.above[:], other, one, ALU.is_gt))
        ch.link(dve.tensor_tensor(self.same[:], other, one, ALU.is_equal))
        ch.link(dve.tensor_tensor(self.same[:], self.same[:],
                                  self.low[:].unsqueeze(1).broadcast_to([P, BT, ne, ne]), ALU.mult))
        ch.link(dve.tensor_tensor(self.above[:], self.above[:], self.same[:], ALU.add))
        ch.link(dve.tensor_reduce(q[:], self.above[:], AX, ALU.add))
        ch.link(dve.tensor_scalar(q[:], q[:], 1.5, None, ALU.is_lt))
        if self.again:
            ch.link(dve.tensor_reduce(row[:], p[:], AX, ALU.max))
            dve.tensor_tensor(p[:], p[:], over(row[:], ne), ALU.subtract).then_inc(self.shifted, 1)
            dve.wait_ge(self.raised, i * self.calls + 2)
            ch.link(dve.tensor_tensor(q[:], q[:], self.ex2[:], ALU.mult))
        else:
            ch.link(dve.tensor_copy(self.chosen[:], q[:]))
            ch.link(dve.tensor_tensor(q[:], q[:], p[:], ALU.mult))
        ch.link(dve.tensor_reduce(row[:], q[:], AX, ALU.add))
        ch.link(dve.reciprocal(row[:], row[:]))
        ch.link(dve.tensor_tensor(q[:], q[:], over(row[:], ne), ALU.mult))

    def raise_(self, act, i):
        act.wait_ge(self.shifted, i * self.calls + 1)
        act.activation(self.ex[:], self.p[:], ACT.Exp).then_inc(self.raised, 1)
        if self.again:
            act.wait_ge(self.shifted, i * self.calls + 2)
            act.activation(self.ex2[:], self.p[:], ACT.Exp).then_inc(self.raised, 1)


def small_mixture(nc, net, w):
    ne, e1, e2 = w["eW2"].shape
    s1, s2 = w["sW2"].shape
    sc = s1 // P
    two = P // e2
    pairs = ne // two
    with Stage(nc, "mix") as st:
        gate = Gate(st, ne, True)
        part = st.sb("part", [P, 2, BT])
        xn, xt = st.sb("xn", [P, BT, D]), st.sb("xt", [P, 2, BN])
        gw = st.sb("gw", [P, 2, ne])
        sw1, sw2, sw3 = st.sb("sw1", [P, 2, s1]), st.sb("sw2", [P, sc, s2]), st.sb("sw3", [s2, D])
        sb1, sb2 = st.sb("sb1", [P, sc]), st.sb("sb2", [s2, 1])
        ew1, ew2, ew3 = st.sb("ew1", [P, ne, 2, e1]), st.sb("ew2", [e1, ne, e2]), st.sb("ew3", [P, pairs, D])
        eb1, eb2 = st.sb("eb1", [e1, ne]), st.sb("eb2", [e2, ne])
        b3 = st.sb("b3", [ne + 1, D])
        st1, st2 = st.sb("st1", [P, sc, BN]), st.sb("st2", [s2, BN])
        h1, h2 = st.sb("h1", [e1, 2, BN]), st.sb("h2", [P, pairs, BN])
        wt = st.sb("wt", [ne + 1, BN])
        at, spread = st.sb("at", [ne, pairs, P]), st.sb("spread", [ne, pairs, P])
        start64 = st.sb("start64", [ne, 1])
        loaded, ready, chain, weighed = st.sem("loaded"), st.sem("ready"), st.sem("chain"), st.sem("weighed")
        spread_ready, scaled = st.sem("spread_ready"), st.sem("scaled")
        n_cols = 2 * sc + 2 + 4 * ne + 2
        flipped = Ring(st.sem("flipped"), st.sem("flipped_free"), st.banks(2, "x"), 4)
        cols = Ring(st.sem("cols"), st.sem("cols_free"), st.banks(4, "c"), n_cols)
        outs = Ring(st.sem("outs"), st.sem("outs_free"), st.banks(2, "o"), 1 + 2 * pairs + 4)
        loads = [
            (gw[:], w["gW"].rearrange("(c k) e -> k c e", k=P)), (gate.bias[:], w["gb"].partition_broadcast(P)),
            (sw1[:], w["sW1"].rearrange("(c k) m -> k c m", k=P)),
            (sw2[:], w["sW2"].rearrange("(c k) m -> k c m", k=P)),
            (sw3[:], w["sW3"]), (sb1[:], w["sb1"].rearrange("(c k) -> k c", k=P)),
            (sb2[:], w["sb2"].rearrange("(k o) -> k o", o=1)),
            (b3[ne:ne + 1, :], w["sb3"].rearrange("(o k) -> o k", o=1)), (b3[0:ne, :], w["eb3"]),
            (ew2[:], w["eW2"].rearrange("e k m -> k e m")),
            (eb1[:], w["eb1"].rearrange("e k -> k e")), (eb2[:], w["eb2"].rearrange("e k -> k e")),
        ] + [(ew1[:, e], w["eW1"][e].rearrange("(c k) m -> k c m", k=P)) for e in range(ne)]\
          + [(ew3[:, p, :], w["eW3"][p * two:(p + 1) * two].rearrange("e k m -> (e k) m")) for p in range(pairs)]

        with nc.allow_non_contiguous_dma(reason="biases, once"), nc.Block() as block:
            @block.sync
            def _(sp):
                for o, i in loads:
                    sp.dma_start(o, i).then_inc(loaded, 16)

            @block.vector
            def _(dve):
                ch = Chain(dve, chain)
                outs.give_credit(dve)
                dve.memset(wt[:], 1.0).then_inc(spread_ready, 1)
                ch.link(dve.tensor_scalar(start64[:], net.part[0:ne, 0:1], float(e2), None, ALU.mult))
                for p in range(pairs):
                    ch.link(dve.tensor_scalar(at[:, p, :], net.iota[0:ne, :], start64[:], None, ALU.subtract))
                    ch.link(dve.tensor_scalar(at[:, p, :], at[:, p, :], float(p * P), None, ALU.add))
                ch.link(dve.tensor_scalar(spread[:], at[:], 0.0, None, ALU.is_ge))
                ch.link(dve.tensor_scalar(at[:], at[:], float(e2), None, ALU.is_lt))
                dve.tensor_tensor(spread[:], spread[:], at[:], ALU.mult).then_inc(spread_ready, 1)
                dve.wait_ge(loaded, 16 * len(loads))
                gate.order(ch, dve, net)

                def prepare(b):
                    ch.mark(dve.tensor_copy(part[:, 0, :], net.mean[:, bass.ds(b * BT, BT)]))
                    ch.link(dve.tensor_copy(part[:, 1, :], net.rstd[:, bass.ds(b * BT, BT)]))
                    for j in range(BT):
                        last = dve.tensor_scalar(xn[:, j, :], net.x[:, bass.ds(b * (BT * D) + j * D, D)],
                                                 part[:, 0, j:j + 1], part[:, 1, j:j + 1], ALU.subtract, ALU.mult)
                    last.then_inc(ready, 1)

                def finish(b, before):
                    gate.weights(ch, dve, b, outs.drain(dve, b)[:, 0:BT * ne], outs)
                    dve.sem_inc(weighed, 1)
                    before()
                    dve.wait_ge(cols.empty, (b + 2) * n_cols)
                    dve.sem_inc(spread_ready, 1)
                    for p in range(pairs):
                        for s in range(2):
                            h = h2[:, p, s * HB:(s + 1) * HB]
                            dve.tensor_tensor(h, h, outs.drain(dve, b)[:, 0:HB], ALU.mult).then_inc(outs.empty, 1)
                    outs.settle(dve, b)
                    dve.sem_inc(scaled, 1)
                    for u in range(4):
                        n = min(2, BT - 2 * u)
                        x = net.x[:, bass.ds(b * (BT * D) + 2 * u * D, n * D)]
                        dve.tensor_tensor(x, x, outs.drain(dve, b)[:, 0:n * D], ALU.add).then_inc(outs.empty, 1)

                def ahead(b):
                    dve.wait_ge(flipped.full, b * 4 + 4)
                    prepare(b + 1)

                prepare(0)
                with dve.Fori(0, NB - 1) as b:
                    ch.enter(b, Gate.marks + 2)
                    finish(b, lambda: ahead(b))
                    ch.leave(NB - 1)
                finish(NB - 1, lambda: None)

            @block.scalar
            def _(act):
                flipped.give_credit(act)
                cols.give_credit(act)
                act.wait_ge(loaded, 16 * len(loads))
                act.wait_ge(spread_ready, 1)

                def copy_flipped(b):
                    flat = xt[:].rearrange("p c n -> p (c n)")
                    for u in range(4):
                        n = min(4, 2 * BT - 4 * u) * P
                        act.activation(flat[:, u * 512:u * 512 + n], flipped.drain(act, b)[:, 0:n], ACT.Copy)\
                            .then_inc(flipped.empty, 1)

                def relu(b, out, k, bias, n=HB):
                    act.activation(out, cols.drain(act, b)[0:k, 0:n], ACT.Relu, bias=bias).then_inc(cols.empty, 1)

                def experts1(b, e):
                    for s in range(2):
                        relu(b, h1[:, e % 2, s * HB:(s + 1) * HB], e1, eb1[:, e:e + 1])

                def experts2(b, e):
                    for s in range(2):
                        relu(b, h2[e % two * e2:(e % two + 1) * e2, e // two, s * HB:(s + 1) * HB], e2,
                             eb2[:, e:e + 1])

                def batch(b, last=False):
                    for s in range(2):
                        for c in range(sc):
                            relu(b, st1[:, c, s * HB:(s + 1) * HB], P, sb1[:, c:c + 1])
                    experts1(b, 0)
                    for s in range(2):
                        relu(b, st2[:, s * HB:(s + 1) * HB], s2, sb2[:])
                    experts1(b, 1)
                    gate.raise_(act, b)
                    experts2(b, 0)
                    for u in range(2):
                        n = min(4, BT - 4 * u) * P
                        act.activation(wt[0:ne, u * 512:u * 512 + n], cols.drain(act, b)[0:ne, 0:n], ACT.Copy)\
                            .then_inc(cols.empty, 1)
                    for e in range(2, ne):
                        experts1(b, e)
                        experts2(b, e - 1)
                    if not last:
                        copy_flipped(b + 1)
                    experts2(b, ne - 1)

                copy_flipped(0)
                with act.Fori(0, NB - 1) as b:
                    batch(b)
                batch(NB - 1, last=True)

            @block.tensor
            def _(pe):
                pe.wait_ge(loaded, 16 * len(loads))
                pe.wait_ge(spread_ready, 2)

                def turn_over(b):
                    pe.wait_ge(ready, b + 1)
                    for u in range(4):
                        bank = flipped.fill(pe, b)
                        for m in range(4 * u, min(4 * u + 4, 2 * BT)):
                            mm = pe.transpose(bank[:, m % 4 * P:(m % 4 + 1) * P],
                                              xn[:, m % BT, m // BT * P:(m // BT + 1) * P], net.ident[:])
                        mm.then_inc(flipped.full, 1)

                def columns(b, out, lhs, rhs):
                    bank = cols.fill(pe, b)
                    for c, (l, r) in enumerate(zip(lhs, rhs)):
                        mm = pe.matmul(bank[0:out, 0:HB], l, r, start=c == 0, stop=c == len(lhs) - 1)
                    mm.then_inc(cols.full, 1)

                def drained(b, n):
                    pe.wait_ge(cols.empty, (b + 1) * n_cols + n)

                def experts1(b, e):
                    for s in range(2):
                        columns(b, e1, [ew1[:, e, c, :] for c in range(2)],
                                [xt[:, c, s * HB:(s + 1) * HB] for c in range(2)])

                def experts2(b, e):
                    for s in range(2):
                        columns(b, e2, [ew2[:, e, :]], [h1[:, e % 2, s * HB:(s + 1) * HB]])

                def batch(b, last=False):
                    pe.wait_ge(flipped.empty, (b + 2) * 4)
                    bank = outs.fill(pe, b)
                    for j in range(BT):
                        for c in range(2):
                            mm = pe.matmul(bank[:, j * ne:(j + 1) * ne], xt[:, c, j * P:(j + 1) * P], gw[:, c, :],
                                           start=c == 0, stop=c == 1)
                    mm.then_inc(outs.full, 1)
                    for s in range(2):
                        for m in range(sc):
                            columns(b, P, [sw1[:, c, m * P:(m + 1) * P] for c in range(2)],
                                    [xt[:, c, s * HB:(s + 1) * HB] for c in range(2)])
                    experts1(b, 0)
                    drained(b, 2 * sc)
                    for s in range(2):
                        columns(b, s2, [sw2[:, c, :] for c in range(sc)],
                                [st1[:, c, s * HB:(s + 1) * HB] for c in range(sc)])
                    experts1(b, 1)
                    drained(b, 2 * sc + 2)
                    experts2(b, 0)
                    pe.wait_ge(weighed, b + 1)
                    for u in range(2):
                        bank = cols.fill(pe, b)
                        for j in range(4 * u, min(4 * u + 4, BT)):
                            mm = pe.transpose(bank[0:ne, j % 4 * P:(j % 4 + 1) * P], gate.q[:, j, :], net.ident[:])
                        mm.then_inc(cols.full, 1)
                    for e in range(2, ne):
                        experts1(b, e)
                        drained(b, 2 * sc + (6 if e == 2 else 4 * e))
                        experts2(b, e - 1)
                    if not last:
                        turn_over(b + 1)
                    drained(b, n_cols - 4)
                    experts2(b, ne - 1)
                    for p in range(pairs):
                        for s in range(2):
                            pe.matmul(outs.fill(pe, b)[:, 0:HB], spread[:, p, :], wt[0:ne, s * HB:(s + 1) * HB],
                                      start=True, stop=True).then_inc(outs.full, 1)
                    pe.wait_ge(scaled, b + 1)
                    for u in range(4):
                        bank = outs.fill(pe, b)
                        for j in range(2 * u, min(2 * u + 2, BT)):
                            o = bank[:, (j - 2 * u) * D:(j - 2 * u + 1) * D]
                            nodes = slice(j * P, (j + 1) * P)
                            pe.matmul(o, st2[:, nodes], sw3[:], start=True, stop=False)
                            pe.matmul(o, wt[:, nodes], b3[:], start=False, stop=False)
                            for p in range(pairs):
                                mm = pe.matmul(o, h2[:, p, nodes], ew3[:, p, :], start=False, stop=p == pairs - 1)
                        mm.then_inc(outs.full, 1)

                turn_over(0)
                with pe.Fori(0, NB - 1) as b:
                    batch(b)
                batch(NB - 1, last=True)


def source_logits(nc, net, name, table, cols):
    with Stage(nc, name) as st:
        index, rows = st.sb("index", [P, 2, BY_DMA], I32), st.sb("rows", [P, 2, BY_DMA, HEADS])
        one_lo, one_hi = st.sb("one_lo", [P, 4, HALF, P], BF16), st.sb("one_hi", [P, 4, HALF, NT])
        lo, far = st.sb("lo", [P, 4, HALF]), st.sb("far", [P, HALF, P], BF16)
        flipped_sb, ident = st.sb("flipped_sb", [P, 2, HALF, P], BF16), st.sb("ident", [P, P], BF16)
        parts, left = st.sb("parts", [P, 3, HEADS, NT], BF16), st.sb("left", [P, HEADS, NT])
        wide, picked = st.sb("wide", [P, HEADS, NT]), st.sb("picked", [P, 2, HALF, HEADS, NT])
        gathered = [st.sem("gathered0"), st.sem("gathered1")]
        indexed, go, copied, cleared = (st.sem(x) for x in ("indexed", "go", "copied", "cleared"))
        split, made, chain, multiplied = (st.sem(x) for x in ("split", "made", "chain", "multiplied"))
        named, measured, made_lo = st.sem("named"), st.sem("measured"), st.sem("made_lo")
        flips = [st.ps(f"flip{n}", [P, HALF * P], BF16) for n in range(2)]
        flipped, flip_free = st.sem("flipped"), st.sem("flip_free")
        picks = Ring(st.sem("picks"), st.sem("picks_free"), st.banks(4), 4)
        steps = 2 * DMA_STEPS

        with nc.Block() as block:
            @block.gpsimd
            def _(pool):
                pool.memset(cols[:, DMA_STEPS * (BY_DMA + 2 * HALF):KP, :], 0.0).then_inc(cleared, 1)
                gather_rows(pool, table, rows, net.src_col[:, 0:DMA_STEPS * BY_DMA], index, gathered, indexed, go,
                            copied, lambda q: q - 1)

            @block.vector
            def _(dve):
                ch = Chain(dve, chain)
                picks.give_credit(dve)

                def name(q, s):
                    at = bass.ds(q * HALF + DMA_STEPS * BY_DMA, HALF)
                    dve.tensor_copy(lo[:, s, :], net.src_lo[:, at]).then_inc(named, 1)

                def one_hots(q, s):
                    at = bass.ds(q * HALF + DMA_STEPS * BY_DMA, HALF)
                    dve.tensor_tensor(one_hi[:, s], over(net.src_hi[:, at], NT), mid(net.iota[:, 0:NT], HALF),
                                      ALU.is_equal).then_inc(made, 1)

                def step(q, s, ahead=True):
                    dve.wait_ge(made, q + 1)
                    for u in range(4):
                        bank = picks.drain(dve, q)
                        hot = one_hi[:, s, 2 * u:2 * u + 2, :].unsqueeze(2).broadcast_to([P, 2, HEADS, NT])
                        last = dve.tensor_tensor(
                            picked[:, s % 2, 2 * u:2 * u + 2],
                            bank[:, 0:2 * HEADS * NT].rearrange("p (j h t) -> p j h t", h=HEADS, t=NT), hot, ALU.mult)
                        last.then_inc(picks.empty, 1)
                    if ahead:
                        name(q + 4, s)
                        one_hots(q + 2, (s + 2) % 4)
                    picks.settle(dve, q)
                    dve.tensor_reduce(cols[:, bass.ds(q * HALF + DMA_STEPS * BY_DMA, HALF), :],
                                      picked[:, s % 2], AX, ALU.add).then_inc(multiplied, 1)

                for q in range(4):
                    name(q, q)
                one_hots(0, 0)
                one_hots(1, 1)
                logit = net.logit[:].rearrange("p (t a) -> p a t", a=2 * HEADS)
                ch.link(dve.tensor_copy(left[:], logit[:, 0:HEADS, :]))
                for n in range(3):
                    ch.link(dve.tensor_copy(parts[:, n], left[:]))
                    if n < 2:
                        ch.link(dve.tensor_copy(wide[:], parts[:, n]))
                        ch.link(dve.tensor_tensor(left[:], left[:], wide[:], ALU.subtract))
                ch.link(dve.tensor_copy(ident[:], net.ident[:]))
                dve.sem_inc(split, 1)
                for s in range(2):
                    step(s, s)
                with dve.Fori(0, steps // 4 - 1) as i:
                    for s in range(4):
                        q = i * 4 + 2 + s
                        dve.wait_ge(multiplied, q - 1)
                        dve.sem_inc(chain, 1)
                        step(q, (s + 2) % 4)
                for s in range(2):
                    dve.wait_ge(multiplied, steps - 3 + s)
                    step(steps - 2 + s, 2 + s, ahead=False)

            @block.scalar
            def _(act):
                def lo_rows(q, s):
                    act.wait_ge(named, q + 1)
                    for j in range(HALF):
                        act.activation(far[:, j, :], net.iota[:], ACT.Abs, bias=lo[:, s, j:j + 1], scale=-1.0)\
                            .then_inc(measured, 1)
                    act.wait_ge(measured, (q + 1) * HALF)
                    act.activation(one_lo[:, s], far[:], ACT.Relu, bias=net.ones[:, 0:1], scale=-1.0)\
                        .then_inc(made_lo, 1)
                    act.wait_ge(made_lo, q + 1)

                def copy_flipped(q, h):
                    act.wait_ge(flipped, q + 1)
                    act.activation(flipped_sb[:, h].rearrange("p j n -> p (j n)"), flips[h][:], ACT.Copy)\
                        .then_inc(flip_free, 1)

                def copy_rows(q, h, turn):
                    act.wait_ge(gathered[h], turn * (16 * BY_DMA) + 16 * BY_DMA)
                    act.activation(cols[:, bass.ds(q * BY_DMA, BY_DMA), :], rows[:, h], ACT.Copy).then_inc(copied, 1)

                def turn(i, last=False):
                    for h in range(2):
                        for n in range(2):
                            q, s = i * 4 + h * 2 + n, h * 2 + n
                            copy_flipped(q, n)
                            if not (last and s >= 1):
                                lo_rows(q + 3, (s + 3) % 4)
                        copy_rows(i * 2 + h, h, i)

                for q in range(3):
                    lo_rows(q, q)
                with act.Fori(0, DMA_STEPS // 2 - 1) as i:
                    turn(i)
                turn(DMA_STEPS // 2 - 1, last=True)

            @block.tensor
            def _(pe):
                def turn_over(q, s, fresh=False):
                    pe.wait_ge(made_lo, q + 1)
                    if not fresh:
                        pe.wait_ge(flip_free, q - 1)
                    for j in range(HALF):
                        mm = pe.transpose(flips[s % 2][:, j * P:(j + 1) * P], one_lo[:, s, j, :], ident[:])
                    mm.then_inc(flipped, 1)

                def pick(q, s):
                    pe.wait_ge(flip_free, q + 1)
                    for u in range(4):
                        bank = picks.fill(pe, q)
                        for j in range(2 * u, 2 * u + 2):
                            for n in range(3):
                                at = (j - 2 * u) * HEADS * NT
                                mm = pe.matmul(bank[:, at:at + HEADS * NT], flipped_sb[:, s % 2, j, :],
                                               parts[:, n].rearrange("p h t -> p (h t)"), start=n == 0, stop=n == 2)
                        mm.then_inc(picks.full, 1)

                pe.wait_ge(split, 1)
                turn_over(0, 0, True)
                turn_over(1, 1, True)
                with pe.Fori(0, steps // 4 - 1) as i:
                    for s in range(4):
                        pick(i * 4 + s, s)
                        turn_over(i * 4 + s + 2, (s + 2) % 4)
                for s in range(4):
                    pick(steps - 4 + s, s)
                    if s < 2:
                        turn_over(steps - 2 + s, s + 2)


def segment_max(nc, net, name, cols):
    with Stage(nc, name) as st:
        best, back = st.sb("best", [P, HEADS, KC, P]), st.sb("back", [P, 2, KC, P])
        item_of = st.sb("item_of", [P, KC, NIP])
        ends = st.sb("ends", [HEADS, 2, KP])
        step, carry = st.sb("step", [HEADS, 2, KP]), st.sb("carry", [HEADS, 2, KP])
        carried = st.sb("carried", [P, 2, KC, HEADS])
        turned, laid, scanned, chain, pe_done = (st.sem(x) for x in ("turned", "laid", "scanned", "chain", "pe_done"))
        taken, widened = st.sem("taken"), st.sem("widened")
        bank = st.banks(8)

        with nc.Block() as block:
            @block.vector
            def _(dve):
                ch = Chain(dve, chain)
                for h in range(HEADS):
                    dve.wait_ge(laid, 2 * h + 2)
                    b = best[:, h].rearrange("p c e -> p (c e)")
                    left, right = (back[:, s].rearrange("p c e -> p (c e)") for s in range(2))
                    start, end = (m[:].rearrange("p c e -> p (c e)") for m in (net.run_start, net.run_end))
                    ch.mark(dve.tensor_tensor_scan(left, start, b, -BIG, ALU.add, ALU.max))
                    ch.link(dve.tensor_tensor_scan(right[:, ::-1], end[:, ::-1], b[:, ::-1], -BIG, ALU.add, ALU.max))
                    ch.link(dve.tensor_tensor(b, left, right, ALU.max))
                dve.sem_inc(scanned, 1)
                dve.wait_ge(pe_done, 1)
                for s in range(2):
                    ch.mark(dve.tensor_copy(ends[:, s, 0:512], bank[2 * s][0:HEADS, :]))
                    ch.link(dve.tensor_copy(ends[:, s, 512:KP], bank[2 * s + 1][0:HEADS, 0:KP - 512]))
                ch.mark(dve.memset(step[:, 0, 0:1], -BIG))
                ch.mark(dve.memset(step[:, 1, KP - 1:KP], -BIG))
                ch.mark(dve.tensor_tensor(step[:, 0, 1:KP], ends[:, 1, 0:KP - 1], net.link_left[:, 1:KP], ALU.add))
                ch.link(dve.tensor_tensor(step[:, 1, 0:KP - 1], ends[:, 0, 1:KP], net.link_right[:, 0:KP - 1],
                                          ALU.add))
                ch.mark(dve.tensor_tensor_scan(carry[:, 0, :], net.pass_left[:], step[:, 0, :], -BIG,
                                               ALU.add, ALU.max))
                ch.link(dve.tensor_tensor_scan(carry[:, 1, ::-1], net.pass_right[:, ::-1], step[:, 1, ::-1], -BIG,
                                               ALU.add, ALU.max))
                dve.sem_inc(scanned, 1)
                dve.wait_ge(pe_done, 2)
                ch.link(dve.tensor_copy(carried[:].rearrange("p s c h -> p (s c h)"),
                                        bank[4][:, 0:2 * KC * HEADS]))
                for h in range(HEADS):
                    for s, mask in enumerate((net.not_first_run, net.not_last_run)):
                        ch.link(dve.tensor_tensor(back[:, s], mask[:], over(carried[:, s, :, h], P), ALU.add))
                        last = dve.tensor_tensor(best[:, h], best[:, h], back[:, s], ALU.max)
                        if s == 0:
                            ch.link(last)
                        else:
                            last.then_inc(scanned, 1)
                for n in range(2 * HEADS):
                    h, s = n // 2, n % 2
                    dve.wait_ge(pe_done, 3 + n)
                    cols = ITEM_HALVES[s]
                    dve.tensor_copy(net.peak[:, cols, h], bank[n][:, 0:cols.stop - cols.start]).then_inc(taken, 1)

            @block.scalar
            def _(act):
                act.activation(item_of[:], net.item_of[:], ACT.Copy).then_inc(widened, 1)
                for n in range(2 * HEADS):
                    h, s = n // 2, n % 2
                    act.wait_ge(turned, n + 1)
                    c0, c1 = (0, 4) if s == 0 else (4, KC)
                    act.activation(best[:, h, c0:c1, :].rearrange("p c e -> p (c e)"),
                                   bank[n][:, 0:(c1 - c0) * P], ACT.Copy).then_inc(laid, 1)

            @block.tensor
            def _(pe):
                for n in range(2 * HEADS):
                    h, s = n // 2, n % 2
                    for c in range(4 * s, min(4 * s + 4, KC)):
                        mm = pe.transpose(bank[n][:, (c - 4 * s) * P:(c - 4 * s + 1) * P],
                                          cols[:, c * P:(c + 1) * P, h], net.ident[:])
                    mm.then_inc(turned, 1)
                pe.wait_ge(scanned, 1)
                for s, at in enumerate((0, P - 1)):
                    for c in range(KC):
                        b = bank[2 * s + c // 4]
                        mm = pe.transpose(b[0:HEADS, c % 4 * P:(c % 4 + 1) * P], best[:, :, c, at], net.ident[:])
                mm.then_inc(pe_done, 1)
                pe.wait_ge(scanned, 2)
                for s in range(2):
                    for c in range(KC):
                        at = (s * KC + c) * HEADS
                        mm = pe.transpose(bank[4][:, at:at + HEADS], carry[:, s, c * P:(c + 1) * P],
                                          net.ident[0:HEADS, 0:HEADS])
                mm.then_inc(pe_done, 1)
                pe.wait_ge(widened, 1)
                for n in range(2 * HEADS):
                    h, s = n // 2, n % 2
                    pe.wait_ge(scanned, 3 + h)
                    in_item_order(pe, bank[n], s, lambda c: best[:, h, c, :], item_of).then_inc(pe_done, 1)


def gat_pass(nc, net, name, table):
    with Stage(nc, name) as st:
        index = st.sb("index", [P, DEPTH, HALF], I32)
        rows, msg = st.sb("rows", [P, DEPTH, HALF, GW]), st.sb("msg", [P, 2, HALF, MW])
        onehot, turned_sb = st.sb("onehot", [P, DEPTH, HALF, P]), st.sb("turned_sb", [P, 2, HALF, P])
        lg, diff = (st.sb(x, [P, 2, HALF, HEADS]) for x in ("lg", "diff"))
        sums = st.banks(4, "sum")
        flips = st.banks(2, "flip")
        node_lg = st.banks(2, "node")
        gathered = [st.sem(f"gathered{h}") for h in range(DEPTH)]
        indexed, go, made, turned, copied = (st.sem(x) for x in ("indexed", "go", "made", "turned", "copied"))
        looked, shifted, raised, ready, summed, added = (
            st.sem(x) for x in ("looked", "shifted", "raised", "ready", "summed", "added"))
        peaked, chain = st.sem("peaked"), st.sem("chain")
        turns = STEPS // DEPTH

        with nc.Block() as block:
            @block.gpsimd
            def _(pool):
                gather_rows(pool, table, rows, net.src_of, index, gathered, indexed, go, ready,
                            lambda q: (q - DEPTH + 1) * 4, own_index=False)

            @block.vector
            def _(dve):
                ch = Chain(dve, chain)
                tile = [dve.alloc_register(f"{name}_t{j}") for j in range(HALF)]
                marks = 5

                def items(q):
                    return bass.ds(q * HALF, HALF)

                def one_hot(q, s, p):
                    dve.tensor_tensor(onehot[:, s, 2 * p:2 * p + 2],
                                      over(net.dloc[:, bass.ds(q * HALF + 2 * p, 2)], P), mid(net.iota[:], 2),
                                      ALU.is_equal).then_inc(made, 1)

                def bring_peaks(q, h):
                    dve.tensor_tensor(msg[:, h, :, GW:MW], net.peak[:, items(q), :],
                                      over(net.first_of[:, items(q)], HEADS), ALU.mult).then_inc(peaked, 1)

                def multiply(q, s, p):
                    dve.tensor_tensor(msg[:, s % 2, 2 * p:2 * p + 2, 0:D].rearrange("p j (h f) -> p j h f", f=HID),
                                      rows[:, s, 2 * p:2 * p + 2, 0:D].rearrange("p j (h f) -> p j h f", f=HID),
                                      over(msg[:, s % 2, 2 * p:2 * p + 2, D:GW], HID), ALU.mult)\
                        .then_inc(ready, 1)

                def add(q, j, first=False):
                    dve.wait_ge(summed, q * HALF + j + 1)
                    if not first:
                        dve.wait_ge(added, q * HALF + j)
                    acc = net.acc[:, bass.ds(dve.snap(tile[j], min_val=0, max_val=NT - 1) * MW, MW)]
                    dve.tensor_tensor(acc, acc, sums[j % 4][:, 0:MW], ALU.add).then_inc(added, 1)

                def from_nodes(s, what):
                    at = node_lg[s % 2][:, 0:HALF * 2 * HEADS].rearrange("p (j a) -> p j a", a=2 * HEADS)
                    return at[:, :, what * HEADS:(what + 1) * HEADS]

                def begin_logits(q, s, turn):
                    dve.wait_ge(gathered[s], turn * P + P)
                    dve.wait_ge(looked, q + 1)
                    ch.mark(dve.tensor_tensor(lg[:, 0], rows[:, s, :, D:GW], from_nodes(s, 1), ALU.add))
                    ch.mark(dve.tensor_tensor(lg[:, 1], net.peak[:, items(q), :], from_nodes(s, 0), ALU.max))

                def join_logits(s):
                    ch.wait()
                    ch.mark(dve.tensor_tensor(lg[:, 1], lg[:, 1], from_nodes(s, 1), ALU.add))

                def leak_logits():
                    ch.wait()
                    ch.mark(dve.scalar_tensor_tensor(out=lg[:], in0=lg[:], scalar=0.2, in1=lg[:],
                                                     op0=ALU.mult, op1=ALU.max))

                def shift_logits(s):
                    ch.wait()
                    ch.mark(dve.tensor_tensor(diff[:, s % 2], lg[:, 0], lg[:, 1], ALU.subtract))

                def bound_logits(s):
                    ch.wait()
                    dve.tensor_scalar(diff[:, s % 2], diff[:, s % 2], 0.0, None, ALU.min).then_inc(shifted, 1)

                def step(i, s, first=False, last=False):
                    q = i * DEPTH + s
                    logits = not (last and s == DEPTH - 1)
                    hots = not (last and s >= 1)
                    n, turn = (s + 1) % DEPTH, i + (s + 1) // DEPTH
                    dve.wait_ge(raised, q + 1)
                    multiply(q, s, 0)
                    for p in range(4):
                        if not (first and s == 0):
                            add(q - 1, p + 4)
                        if p < 3:
                            multiply(q, s, p + 1)
                    dve.load(tile[0:4], net.t_of[0:1, bass.ds(q * HALF, 4)])
                    if hots:
                        one_hot(q + 3, (s + 3) % DEPTH, 0)
                    add(q, 0, first and s == 0)
                    dve.load(tile[4:8], net.t_of[0:1, bass.ds(q * HALF + 4, 4)])
                    if logits:
                        begin_logits(q + 1, n, turn)
                    if hots:
                        one_hot(q + 3, (s + 3) % DEPTH, 1)
                    if logits:
                        join_logits(n)
                    add(q, 1)
                    if logits:
                        leak_logits()
                    if hots:
                        one_hot(q + 3, (s + 3) % DEPTH, 2)
                    if logits:
                        shift_logits(n)
                    add(q, 2)
                    if logits:
                        bound_logits(n)
                    if hots:
                        one_hot(q + 3, (s + 3) % DEPTH, 3)
                    add(q, 3)
                    if logits:
                        bring_peaks(q + 1, n % 2)

                for q in range(3):
                    for p in range(4):
                        one_hot(q, q, p)
                bring_peaks(0, 0)
                begin_logits(0, 0, 0)
                join_logits(0)
                leak_logits()
                shift_logits(0)
                bound_logits(0)
                for s in range(DEPTH):
                    step(0, s, first=True)
                with dve.Fori(1, turns - 1) as i:
                    ch.enter(i - 1, DEPTH * marks)
                    for s in range(DEPTH):
                        step(i, s)
                    ch.leave(turns - 2)
                for s in range(DEPTH):
                    step(turns - 1, s, last=True)
                for j in range(4, HALF):
                    add(STEPS - 1, j)

            @block.scalar
            def _(act):
                def copy_turned(q, h):
                    act.wait_ge(turned, q + 1)
                    for s in range(2):
                        last = act.activation(
                            turned_sb[:, h, 4 * s:4 * s + 4, :].rearrange("p j n -> p (j n)"), flips[s][:], ACT.Copy)
                    last.then_inc(copied, 1)

                def raise_(q, h, fresh=False):
                    act.wait_ge(shifted, q + 1)
                    if not fresh:
                        act.wait_ge(summed, (q - 1) * HALF)
                    act.activation(msg[:, h, :, D:GW], diff[:, h], ACT.Exp).then_inc(raised, 1)

                def number(q, h, turn):
                    index_step(act, net.src_of, index, gathered, indexed, q, h, turn)

                for h in range(DEPTH):
                    number(h, h, 0)
                copy_turned(0, 0)
                for q in range(3):
                    copy_turned(q + 1, (q + 1) % 2)
                    raise_(q, q % 2, q < 2)
                    number(q + DEPTH, q, 1)
                with act.Fori(0, turns - 2) as i:
                    for s in range(DEPTH):
                        q, slot = i * DEPTH + 3 + s, (3 + s) % DEPTH
                        copy_turned(q + 1, s % 2)
                        raise_(q, (s + 1) % 2)
                        number(q + DEPTH, slot, i + 1 + (3 + s) // DEPTH)
                for q in range(STEPS - DEPTH - 1, STEPS):
                    if q + 1 < STEPS:
                        copy_turned(q + 1, (q + 1) % 2)
                    raise_(q, q % 2)
                    if q + DEPTH < STEPS:
                        number(q + DEPTH, q % DEPTH, q // DEPTH + 1)

            @block.tensor
            def _(pe):
                tile = [pe.alloc_register(f"{name}_u{j}") for j in range(HALF)]

                def turn_over(q, s):
                    pe.wait_ge(made, (q + 1) * 4)
                    if not (isinstance(q, int) and q == 0):
                        pe.wait_ge(copied, q)
                    for j in range(HALF):
                        mm = pe.transpose(flips[j // 4][:, j % 4 * P:(j % 4 + 1) * P], onehot[:, s, j, :],
                                          net.ident[:])
                    mm.then_inc(turned, 1)

                def look_up(q, h):
                    pe.load(tile, net.t_of[0:1, bass.ds(q * HALF, HALF)])
                    pe.wait_ge(copied, q + 1)
                    for j in range(HALF):
                        t = pe.snap(tile[j], min_val=0, max_val=NT - 1)
                        mm = pe.matmul(node_lg[h][:, j * 2 * HEADS:(j + 1) * 2 * HEADS], turned_sb[:, h, j, :],
                                       net.logit[:, bass.ds(t * (2 * HEADS), 2 * HEADS)], start=True, stop=True)
                    mm.then_inc(looked, 1)

                def sum_up(q, s, p, fresh):
                    pe.wait_ge(ready, q * 4 + p + 1)
                    if p == 0:
                        pe.wait_ge(peaked, q + 1)
                    for j in range(2 * p, 2 * p + 2):
                        if not (fresh and j < 4):
                            pe.wait_ge(added, q * HALF + j - 3)
                        pe.matmul(sums[j % 4][:, 0:MW], onehot[:, s, j, :], msg[:, s % 2, j, :],
                                  start=True, stop=True).then_inc(summed, 1)

                def turn(i, first=False, last=False):
                    for s in range(DEPTH):
                        q = i * DEPTH + s
                        ahead = not (last and s >= DEPTH - 2)
                        for p in range(2):
                            sum_up(q, s, p, first and s == 0)
                        if ahead:
                            turn_over(q + 2, (s + 2) % DEPTH)
                        sum_up(q, s, 2, False)
                        if ahead:
                            look_up(q + 2, s % 2)
                        sum_up(q, s, 3, False)

                for q in range(2):
                    turn_over(q, q)
                    look_up(q, q)
                turn(0, first=True)
                with pe.Fori(1, turns - 1) as i:
                    turn(i)
                turn(turns - 1, last=True)


def gat_finish(nc, net, name, table, bias, add_to=None):
    add_to_x = add_to is not None
    with Stage(nc, name) as st:
        own, own_w, mx, scaled = (st.sb(x, [P, NT, HEADS]) for x in ("own", "own_w", "mx", "scaled"))
        den, b_sb = st.sb("den", [P, NT, HEADS]), st.sb("b", [P, D])
        rows, tmp = st.sb("rows", [P, 2, BT, D]), st.sb("tmp", [P, 2, BT, D])
        part, quota = st.sb("part", [P, 2, BT * HEADS]), st.sb("quota", [P, BT * HEADS])
        loaded, parted, weighted, chain, diff, raised = (
            st.sem(x) for x in ("loaded", "parted", "weighted", "chain", "diff", "raised"))
        row_in = [st.sem("row_in0"), st.sem("row_in1")]
        finished, begun, cleared = st.sem("finished"), st.sem("begun"), st.sem("cleared")
        to_load = node_pieces(net, *add_to) if add_to_x else []
        acc = net.acc[:].rearrange("p (t w) -> p t w", w=MW)
        lg = net.logit[:].rearrange("p (t a) -> p t a", a=2 * HEADS)

        with nc.Block() as block:
            @block.sync
            def _(sp):
                sp.dma_start(b_sb[:], bias.partition_broadcast(P)).then_inc(loaded, 16)
                view = table.rearrange("(t p) w -> p t w", p=P)

                def load(b, h):
                    sp.wait_ge(weighted, b + 1)
                    sp.dma_start(rows[:, h], view[:, bass.ds(b * BT, BT), 0:D]).then_inc(row_in[h], 16)

                for h in range(2):
                    load(h, h)
                if to_load:
                    sp.wait_ge(cleared, 1)
                for o, i in to_load:
                    sp.dma_start(o, i).then_inc(loaded, 16)
                with sp.Fori(1, NB // 2) as i:
                    for h in range(2):
                        load(i * 2 + h, h)
                load(NB - 1, 0)

            @block.gpsimd
            def _(pool):
                if add_to_x:
                    pool.memset(net.x[:, (NT - 1) * D:NT * D], 0.0).then_inc(cleared, 1)

            @block.vector
            def _(dve):
                ch = Chain(dve, chain)

                def leaky(x):
                    ch.link(dve.tensor_scalar(scaled[:], x[:], 0.2, None, ALU.mult))
                    ch.link(dve.tensor_tensor(x[:], x[:], scaled[:], ALU.max))

                ch.link(dve.tensor_scalar(scaled[:, :, 0], net.has_edge[:], -1.0, BIG, ALU.add, ALU.mult))
                ch.link(dve.tensor_tensor(mx[:], acc[:, :, GW:MW], over(scaled[:, :, 0], HEADS), ALU.add))
                ch.link(dve.tensor_tensor(mx[:], mx[:], lg[:, :, 0:HEADS], ALU.max))
                ch.link(dve.tensor_tensor(mx[:], mx[:], lg[:, :, HEADS:2 * HEADS], ALU.add))
                leaky(mx)
                ch.link(dve.tensor_tensor(own[:], lg[:, :, 0:HEADS], lg[:, :, HEADS:2 * HEADS], ALU.add))
                leaky(own)
                dve.tensor_tensor(own[:], own[:], mx[:], ALU.subtract).then_inc(diff, 1)
                dve.wait_ge(raised, 1)
                ch.link(dve.tensor_tensor(den[:], acc[:, :, D:GW], own_w[:], ALU.add))
                ch.link(dve.tensor_scalar(den[:], den[:], 1e-16, None, ALU.add))
                ch.link(dve.reciprocal(den[:], den[:]))
                dve.wait_ge(loaded, 16 + 16 * len(to_load))
                last_ops = 5 if add_to_x else 4

                def take_weights(b, h):
                    dve.tensor_copy(part[:, h], own_w[:].rearrange("p t h -> p (t h)")[
                        :, bass.ds(b * (BT * HEADS), BT * HEADS)]).then_inc(parted, 1)

                def finish(b, h):
                    ch.link(dve.tensor_copy(quota[:], den[:].rearrange("p t h -> p (t h)")[
                        :, bass.ds(b * (BT * HEADS), BT * HEADS)]))
                    sums = net.acc[:, bass.ds(b * (BT * MW), BT * MW)].rearrange("p (j w) -> p j w", w=MW)[:, :, 0:D]
                    heads = tmp[:, h].rearrange("p j (h f) -> p (j h) f", f=HID)
                    dve.wait_ge(weighted, b + 3)
                    dve.sem_inc(begun, 1)
                    ch.link(dve.tensor_tensor(tmp[:, h], tmp[:, h], sums, ALU.add))
                    ch.link(dve.tensor_tensor(heads, heads, over(quota[:], HID), ALU.mult))
                    if add_to_x:
                        x = net.x[:, bass.ds(b * (BT * D), BT * D)].rearrange("p (j w) -> p j w", w=D)
                        ch.link(dve.tensor_tensor(tmp[:, h], tmp[:, h], mid(b_sb[:], BT), ALU.add))
                        ch.link(dve.tensor_tensor(x, x, tmp[:, h], ALU.add))
                    else:
                        ch.link(dve.tensor_tensor(sums, tmp[:, h], mid(b_sb[:], BT), ALU.add))
                    dve.sem_inc(finished, 1)

                take_weights(0, 0)
                take_weights(1, 1)
                with dve.Fori(0, NB // 2 - 1) as i:
                    ch.enter(i, 2 * last_ops)
                    for h in range(2):
                        b = i * 2 + h
                        finish(b, h)
                        take_weights(b + 2, h)
                    ch.leave(NB // 2 - 1)
                finish(NB - 3, 0)
                take_weights(NB - 1, 0)
                finish(NB - 2, 1)
                finish(NB - 1, 0)

            @block.scalar
            def _(act):
                act.wait_ge(diff, 1)
                act.activation(own_w[:], own[:], ACT.Exp).then_inc(raised, 1)
                act.sem_inc(weighted, 2)
                act.sem_inc(finished, 2)

                def weigh(b, h, turn):
                    act.wait_ge(row_in[h], turn * 16 + 16)
                    act.wait_ge(parted, b + 1)
                    act.wait_ge(finished, b + 1)
                    act.sem_inc(begun, 1)
                    for n in range(BT * HEADS):
                        at = slice(n % HEADS * HID, (n % HEADS + 1) * HID)
                        last = act.activation(tmp[:, h, n // HEADS, at], rows[:, h, n // HEADS, at], ACT.Copy,
                                              scale=part[:, h, n:n + 1])
                    last.then_inc(weighted, 1)

                with act.Fori(0, NB // 2) as i:
                    for h in range(2):
                        weigh(i * 2 + h, h, i)
                weigh(NB - 1, 0, NB // 2)


def route_nodes(nc, net, w, table):
    ne = w["Wr"].shape[1]
    with Stage(nc, "route") as st:
        gate = Gate(st, ne, False)
        part = st.sb("part", [P, 2, 3, BT])
        again = st.sb("again", [P, 2, BT, D])
        xn, xt = st.sb("xn", [P, 2, BT, D]), st.sb("xt", [P, 2, BN])
        wr = st.sb("wr", [P, 2, ne])
        loaded, ready, chain, begun = st.sem("loaded"), st.sem("ready"), st.sem("chain"), st.sem("begun")
        doubled, written = st.sem("doubled"), [st.sem("written0"), st.sem("written1")]
        flipped = Ring(st.sem("flipped"), st.sem("flipped_free"), st.banks(4, "x"), 4)
        outs = Ring(st.sem("outs"), st.sem("outs_free"), st.banks(2, "o"), 1)

        with nc.allow_non_contiguous_dma(reason="gate weights, once"), nc.Block() as block:
            @block.sync
            def _(sp):
                for o, i in ((wr[:], w["Wr"].rearrange("(c k) e -> k c e", k=P)),
                             (gate.bias[:], w["br"].partition_broadcast(P))):
                    sp.dma_start(o, i).then_inc(loaded, 16)
                rows = table.rearrange("(t p) w -> p t w", p=P)
                for h in range(2):
                    sp.sem_inc(written[h], 16)

                def store(b, h):
                    sp.wait_ge(doubled, b + 1)
                    sp.dma_start(rows[:, bass.ds(b * BT, BT), :], again[:, h]).then_inc(written[h], 16)

                with sp.Fori(0, NB // 2) as i:
                    for h in range(2):
                        store(i * 2 + h, h)
                store(NB - 1, 0)
                for h in range(2):
                    sp.wait_ge(written[h], 16 * (NB // 2 + 2 - h))

            @block.vector
            def _(dve):
                ch = Chain(dve, chain)
                outs.give_credit(dve)
                dve.wait_ge(loaded, 32)
                gate.order(ch, dve, net)

                def prepare(b, h):
                    ch.mark(dve.tensor_copy(part[:, h, 0, :], net.mean[:, bass.ds(b * BT, BT)]))
                    ch.mark(dve.tensor_copy(part[:, h, 1, :], net.rstd[:, bass.ds(b * BT, BT)]))
                    ch.link(dve.tensor_copy(part[:, h, 2, :], net.rstd2[:, bass.ds(b * BT, BT)]))
                    for j in range(BT):
                        last = dve.tensor_scalar(xn[:, h, j, :], net.x[:, bass.ds(b * (BT * D) + j * D, D)],
                                                 part[:, h, 0, j:j + 1], part[:, h, 1, j:j + 1],
                                                 ALU.subtract, ALU.mult)
                    last.then_inc(ready, 1)

                def finish(b):
                    gate.weights(ch, dve, b, outs.drain(dve, b)[:, 0:BT * ne], outs)
                    ch.mark(dve.tensor_copy(net.chosen[:, :, bass.ds(b * BT, BT)],
                                            gate.chosen[:].rearrange("p j e -> p e j")))
                    ch.link(dve.tensor_copy(net.weight[:, :, bass.ds(b * BT, BT)],
                                            gate.q[:].rearrange("p j e -> p e j")))

                def prepare_next(b, h):
                    dve.wait_ge(flipped.full, b * 4 - 4)
                    dve.wait_ge(doubled, b - 1)
                    dve.sem_inc(begun, 1)
                    prepare(b, h)

                prepare(0, 0)
                prepare(1, 1)
                with dve.Fori(0, NB // 2 - 1) as i:
                    ch.enter(i, 2 * (Gate.marks + 5))
                    for h in range(2):
                        prepare_next(i * 2 + h + 2, h)
                        finish(i * 2 + h)
                    ch.leave(NB // 2 - 1)
                prepare_next(NB - 1, 0)
                for b in range(NB - 3, NB):
                    finish(b)

            @block.scalar
            def _(act):
                flipped.give_credit(act)
                flat = xt[:].rearrange("p c n -> p (c n)")

                def copy_flipped(b):
                    for u in range(4):
                        n = min(4, 2 * BT - 4 * u) * P
                        act.activation(flat[:, u * 512:u * 512 + n], flipped.drain(act, b)[:, 0:n], ACT.Copy)\
                            .then_inc(flipped.empty, 1)

                def normalise_again(b, h, turn):
                    act.wait_ge(ready, b + 1)
                    act.wait_ge(written[h], turn * 16 + 16)
                    act.sem_inc(begun, 1)
                    for j in range(BT):
                        last = act.activation(again[:, h, j, :], xn[:, h, j, :], ACT.Copy,
                                              scale=part[:, h, 2, j:j + 1])
                    last.then_inc(doubled, 1)

                copy_flipped(0)
                with act.Fori(0, NB // 2) as i:
                    for h in range(2):
                        b = i * 2 + h
                        normalise_again(b, h, i)
                        copy_flipped(b + 1)
                        gate.raise_(act, b)
                normalise_again(NB - 1, 0, NB // 2)
                gate.raise_(act, NB - 1)

            @block.tensor
            def _(pe):
                pe.wait_ge(loaded, 32)

                def turn_over(b, h):
                    pe.wait_ge(ready, b + 1)
                    for u in range(4):
                        bank = flipped.fill(pe, b)
                        for m in range(4 * u, min(4 * u + 4, 2 * BT)):
                            mm = pe.transpose(bank[:, m % 4 * P:(m % 4 + 1) * P],
                                              xn[:, h, m % BT, m // BT * P:(m // BT + 1) * P], net.ident[:])
                        mm.then_inc(flipped.full, 1)

                def logits(b):
                    pe.wait_ge(flipped.empty, b * 4 + 8)
                    bank = outs.fill(pe, b)
                    for j in range(BT):
                        for c in range(2):
                            mm = pe.matmul(bank[:, j * ne:(j + 1) * ne], xt[:, c, j * P:(j + 1) * P], wr[:, c, :],
                                           start=c == 0, stop=c == 1)
                    mm.then_inc(outs.full, 1)

                turn_over(0, 0)
                with pe.Fori(0, NB // 2) as i:
                    for h in range(2):
                        logits(i * 2 + h)
                        turn_over(i * 2 + h + 1, 1 - h)
                logits(NB - 1)


def assign_slots(nc, net, ne):
    m = ne * NT
    with Stage(nc, "assign") as st:
        before = st.sb("before", [P, P])
        ones = st.sb("ones", [P, m])
        total, upto, slot = (st.sb(x, [P, m]) for x in ("total", "upto", "slot"))
        work = st.sb("work", [P, m])
        count, blocks, cum_n, cum_b = (st.sb(x, [P, ne]) for x in ("count", "blocks", "cum_n", "cum_b"))
        blocks_i, offset = st.sb("blocks_i", [P, ne], I32), st.sb("offset", [P, ne])
        past = st.sb("past", [1, BLOCKS, ne])
        block_f = st.sb("block_f", [1, BLOCKS])
        ends, ends_i = st.sb("ends", [P, 2, NT]), st.sb("ends_i", [P, 2, NT], I32)
        cut_i = st.sb("cut_i", [P, 2, NT], I32)
        hi, lo = st.sb("hi", [P, 2, NT]), st.sb("lo", [P, 2, NT])
        node = st.sb("node", [P, NT])
        one_lo, one_hi = st.sb("one_lo", [P, 2, BT, P]), st.sb("one_hi", [P, 2, BT, P])
        counts, sums, inverse = st.banks(3)
        ready, chain, pe_done = st.sem("ready"), st.sem("chain"), st.sem("pe_done")
        onehot, placed, numbered = st.sem("onehot"), st.sem("placed"), st.sem("numbered")
        by_node = lambda t: t[:].rearrange("p (e t) -> p t e", e=ne)
        by_expert = lambda t: t[:].rearrange("p (e t) -> p e t", e=ne)

        with nc.Block() as block:
            @block.gpsimd
            def _(pool):
                pool.iota(node[:], [[P, NT]], base=0, channel_multiplier=1, allow_small_or_imprecise_dtypes=True)\
                    .then_inc(numbered, 1)

            @block.vector
            def _(dve):
                ch = Chain(dve, chain)
                dve.tensor_scalar(before[:], net.iota[:], net.part[:, 0:1], None, ALU.is_gt).then_inc(ready, 1)
                ch.link(dve.memset(ones[:], 1.0))
                dve.wait_ge(pe_done, 2)
                ch.link(dve.tensor_copy(total[:], sums[:, 0:m]))
                ch.mark(dve.tensor_tensor_scan(upto[:], ones[:], total[:], 0.0, ALU.mult, ALU.add))
                ch.link(dve.tensor_reduce(count[:], by_expert(total), AX, ALU.add))
                ch.link(dve.tensor_scalar(blocks[:], count[:], float(BLOCK - 1), None, ALU.add))
                ch.link(dve.tensor_copy(blocks_i[:], blocks[:]))
                ch.link(dve.tensor_scalar(blocks_i[:], blocks_i[:], BLOCK.bit_length() - 1, None,
                                          ALU.arith_shift_right))
                ch.link(dve.tensor_copy(blocks[:], blocks_i[:]))
                ch.mark(dve.tensor_tensor_scan(cum_n[:], ones[:, 0:ne], count[:], 0.0, ALU.mult, ALU.add))
                ch.link(dve.tensor_tensor_scan(cum_b[:], ones[:, 0:ne], blocks[:], 0.0, ALU.mult, ALU.add))
                ch.link(dve.tensor_tensor(offset[:], cum_b[:], blocks[:], ALU.subtract))
                ch.link(dve.scalar_tensor_tensor(out=offset[:], in0=offset[:], scalar=float(BLOCK), in1=cum_n[:],
                                                 op0=ALU.mult, op1=ALU.subtract))
                ch.link(dve.tensor_tensor(offset[:], offset[:], count[:], ALU.add))
                ch.link(dve.tensor_tensor(slot[:], upto[:], total[:], ALU.subtract))
                ch.link(dve.tensor_tensor(by_expert(slot), by_expert(slot), over(offset[:], NT), ALU.add))
                ch.link(dve.tensor_tensor(slot[:], slot[:], counts[:, 0:m], ALU.add))
                chosen = net.chosen[:].rearrange("p e t -> p (e t)")
                ch.link(dve.tensor_scalar(work[:], chosen, -FAR, FAR, ALU.mult, ALU.add))
                ch.link(dve.tensor_tensor(work[:], work[:], slot[:], ALU.add))
                ch.link(dve.tensor_reduce(ends[:, 0, :], by_node(work), AX, ALU.min))
                ch.link(dve.tensor_tensor(work[:], chosen, slot[:], ALU.mult))
                ch.link(dve.tensor_reduce(ends[:, 1, :], by_node(work), AX, ALU.max))
                weight = net.weight[:].rearrange("p e t -> p (e t)")
                for s in range(2):
                    ch.link(dve.tensor_tensor(by_expert(work), by_expert(slot), mid(ends[:, s, :], ne),
                                              ALU.is_equal))
                    ch.link(dve.tensor_tensor(work[:], work[:], weight, ALU.mult))
                    ch.link(dve.tensor_reduce(net.share[:, s, :], by_node(work), AX, ALU.add))
                ch.link(dve.tensor_copy(ends_i[:], ends[:]))
                ch.mark(dve.tensor_copy(net.slots[:].rearrange("p (b s j) -> p b s j", s=2, j=BT),
                                        ends_i[:].rearrange("p s (b j) -> p b s j", j=BT)))
                ch.link(dve.tensor_tensor(past[:], over(net.iota[0:1, 0:BLOCKS], ne), mid(cum_b[0:1, :], BLOCKS),
                                          ALU.is_ge))
                ch.link(dve.tensor_reduce(block_f[:], past[:], AX, ALU.add))
                ch.link(dve.tensor_scalar(block_f[:], block_f[:], float(ne - 1), None, ALU.min))
                ch.mark(dve.tensor_copy(net.block_expert[:], block_f[:]))
                ch.link(dve.tensor_scalar(cut_i[:], ends_i[:], 7, None, ALU.arith_shift_right))
                ch.link(dve.tensor_copy(hi[:], cut_i[:]))
                ch.link(dve.tensor_scalar(cut_i[:], ends_i[:], 127, None, ALU.bitwise_and))
                ch.link(dve.tensor_copy(lo[:], cut_i[:]))
                dve.wait_ge(numbered, 1)
                for q in range(2 * NB):
                    s, cols, h = q // NB, slice(q % NB * BT, (q % NB + 1) * BT), q % 2
                    if q >= 2:
                        dve.wait_ge(placed, q - 1)
                    ch.mark(dve.tensor_tensor(one_lo[:, h], over(lo[:, s, cols], P), mid(net.iota[:], BT),
                                              ALU.is_equal))
                    ch.link(dve.tensor_tensor(one_hi[:, h], over(hi[:, s, cols], P), mid(net.iota[:], BT),
                                              ALU.is_equal))
                    dve.tensor_tensor(one_hi[:, h], one_hi[:, h], over(node[:, cols], P), ALU.mult)\
                        .then_inc(onehot, 1)
                dve.wait_ge(placed, 2 * NB)
                ch.link(dve.tensor_copy(net.node_of[:], inverse[:, 0:SLOT_COLS]))

            @block.tensor
            def _(pe):
                chosen = net.chosen[:].rearrange("p e t -> p (e t)")
                pe.matmul(sums[:, 0:m], net.ones[:], chosen, start=True, stop=True).then_inc(pe_done, 1)
                pe.wait_ge(ready, 1)
                pe.matmul(counts[:, 0:m], before[:], chosen, start=True, stop=True).then_inc(pe_done, 1)
                for q in range(2 * NB):
                    pe.wait_ge(onehot, q + 1)
                    for j in range(BT):
                        mm = pe.matmul(inverse[:, 0:P], one_lo[:, q % 2, j, :], one_hi[:, q % 2, j, :],
                                       start=q == 0 and j == 0, stop=q == 2 * NB - 1 and j == BT - 1)
                    mm.then_inc(placed, 1)


def large_mixture(nc, net, w, table, result):
    ne, _, hid = w["W1"].shape
    hc = hid // P
    g = BLOCK // P
    with Stage(nc, "moe") as st:
        index = st.sb("index", [P, 2, g], I32)
        rows = st.sb("rows", [P, 2, g, D])
        w1, w2 = st.sb("w1", [P, 2, 2, hid]), st.sb("w2", [P, 2, hc, D])
        b1, scale, shift = st.sb("b1", [P, 2, hc]), st.sb("scale", [P, 2, 2]), st.sb("shift", [P, 2, 2])
        b2 = st.sb("b2", [P, 2, D])
        xe, ht, y = st.sb("xe", [P, 2, 2, BLOCK]), st.sb("ht", [P, hc, BLOCK]), st.sb("y", [P, 2, g, D])
        gathered = [st.sem("gathered0"), st.sem("gathered1")]
        loaded = [st.sem("loaded0"), st.sem("loaded1")]
        stored = [st.sem("stored0"), st.sem("stored1")]
        indexed, go, begun, y_ready = st.sem("indexed"), st.sem("go"), st.sem("begun"), st.sem("y_ready")
        flipped = Ring(st.sem("flipped"), st.sem("flipped_free"), st.banks(2, "x"), 2)
        hidden = Ring(st.sem("hidden"), st.sem("hidden_free"), st.banks(4, "h"), hc)
        outs = Ring(st.sem("outs"), st.sem("outs_free"), st.banks(2, "o"), g // 2)
        n_loads = 6

        with nc.allow_non_contiguous_dma(reason="biases and scales"), nc.Block() as block:
            @block.gpsimd
            def _(pool):
                gather_rows(pool, table, rows, net.node_of, index, gathered, indexed, go, flipped.full,
                            lambda q: (q - 1) * 2)

            @block.sync
            def _(sp):
                expert = sp.alloc_register("moe_expert")
                out_rows = result.rearrange("(b j p) w -> b p j w", j=g, p=P)

                def load(b, h):
                    sp.load(expert, net.block_expert[0:1, bass.ds(b, 1)])
                    e = sp.snap(expert, min_val=0, max_val=ne - 1)
                    one = lambda a: a[bass.ds(e, 1)]
                    for o, i in ((scale[:, h, :], one(w["ln_g"]).rearrange("o (c k) -> k (o c)", k=P)),
                                 (shift[:, h, :], one(w["ln_b"]).rearrange("o (c k) -> k (o c)", k=P)),
                                 (b1[:, h, :], one(w["b1"]).rearrange("o (c k) -> k (o c)", k=P)),
                                 (b2[:, h, :], one(w["b2"]).rearrange("o m -> (o m)").partition_broadcast(P)),
                                 (w1[:, h], one(w["W1"]).rearrange("o (c k) m -> k (o c) m", k=P)),
                                 (w2[:, h], one(w["W2"]).rearrange("o (c k) m -> k (o c) m", k=P))):
                        sp.dma_start(o, i).then_inc(loaded[h], 16)

                def store(b, h):
                    sp.wait_ge(y_ready, b + 1)
                    sp.dma_start(out_rows[bass.ds(b, 1)].rearrange("o p j w -> p (o j) w"), y[:, h])\
                        .then_inc(stored[h], 16)

                for h in range(2):
                    load(h, h)
                with sp.Fori(0, BLOCKS // 2 - 1) as i:
                    for h in range(2):
                        store(i * 2 + h, h)
                        load(i * 2 + h + 2, h)
                for h in range(2):
                    store(BLOCKS - 2 + h, h)
                for h in range(2):
                    sp.wait_ge(stored[h], 16 * (BLOCKS // 2))

            @block.vector
            def _(dve):
                flipped.give_credit(dve)
                outs.give_credit(dve)

                def scale_rows(b, h, turn):
                    dve.wait_ge(loaded[h], turn * (16 * n_loads) + 16 * n_loads)
                    dve.sem_inc(begun, 1)
                    for c in range(2):
                        dve.tensor_scalar(xe[:, h, c, :], flipped.drain(dve, b)[:, 0:BLOCK],
                                          scale[:, h, c:c + 1], shift[:, h, c:c + 1], ALU.mult, ALU.add)\
                            .then_inc(flipped.empty, 1)

                def take(b, h):
                    for u in range(g // 2):
                        dve.tensor_tensor(y[:, h, 2 * u:2 * u + 2, :],
                                          outs.drain(dve, b)[:].rearrange("p (j w) -> p j w", w=D),
                                          mid(b2[:, h], 2), ALU.add).then_inc(outs.empty, 1)
                    outs.settle(dve, b)
                    dve.sem_inc(y_ready, 1)

                def turn(i, first=False, last=False):
                    for h in range(2):
                        b = i * 2 + h
                        if not (last and h == 1):
                            scale_rows(b + 1, 1 - h, i + h)
                        if not first:
                            dve.wait_ge(stored[h], i * 16)
                            dve.sem_inc(begun, 1)
                        take(b, h)

                scale_rows(0, 0, 0)
                turn(0, first=True)
                with dve.Fori(1, BLOCKS // 2 - 1) as i:
                    turn(i)
                turn(BLOCKS // 2 - 1, last=True)

            @block.scalar
            def _(act):
                hidden.give_credit(act)
                with act.Fori(0, BLOCKS // 2) as i:
                    for h in range(2):
                        act.wait_ge(loaded[h], i * (16 * n_loads) + 16 * n_loads)
                        for m in range(hc):
                            act.activation(ht[:, m, :], hidden.drain(act, i * 2 + h)[:, 0:BLOCK], ACT.Gelu,
                                           bias=b1[:, h, m:m + 1]).then_inc(hidden.empty, 1)

            @block.tensor
            def _(pe):
                def turn_over(b, h, turn):
                    pe.wait_ge(gathered[h], turn * (16 * g) + 16 * g)
                    for c in range(2):
                        bank = flipped.fill(pe, b)
                        for j in range(g):
                            mm = pe.transpose(bank[:, j * P:(j + 1) * P], rows[:, h, j, c * P:(c + 1) * P],
                                              net.ident[:])
                        mm.then_inc(flipped.full, 1)

                def turn(i, last=False):
                    for h in range(2):
                        b = i * 2 + h
                        pe.wait_ge(loaded[h], i * (16 * n_loads) + 16 * n_loads)
                        pe.wait_ge(flipped.empty, (b + 1) * 2 + 2)
                        for m in range(hc):
                            bank = hidden.fill(pe, b)
                            for c in range(2):
                                mm = pe.matmul(bank[:, 0:BLOCK], w1[:, h, c, m * P:(m + 1) * P], xe[:, h, c, :],
                                               start=c == 0, stop=c == 1)
                            mm.then_inc(hidden.full, 1)
                        if not (last and h == 1):
                            turn_over(b + 1, 1 - h, i + h)
                        pe.wait_ge(hidden.empty, (b + 2) * hc)
                        for u in range(g // 2):
                            bank = outs.fill(pe, b)
                            for j in range(2 * u, 2 * u + 2):
                                for m in range(hc):
                                    mm = pe.matmul(bank[:, (j - 2 * u) * D:(j - 2 * u + 1) * D],
                                                   ht[:, m, j * P:(j + 1) * P], w2[:, h, m, :],
                                                   start=m == 0, stop=m == hc - 1)
                            mm.then_inc(outs.full, 1)

                turn_over(0, 0, 0)
                with pe.Fori(0, BLOCKS // 2 - 1) as i:
                    turn(i)
                turn(BLOCKS // 2 - 1, last=True)


def collect_slots(nc, net, result, out, n):
    with Stage(nc, "collect") as st:
        index, rows = st.sb("index", [P, 2, BT], I32), st.sb("rows", [P, 2, BT, D])
        gathered = [st.sem("gathered0"), st.sem("gathered1")]
        part = st.sb("part", [P, 2, BT])
        indexed, go, added, begun, chain = (st.sem(x) for x in ("indexed", "go", "added", "begun", "chain"))
        saved = st.sem("saved")

        with nc.Block() as block:
            @block.gpsimd
            def _(pool):
                gather_rows(pool, result, rows, net.slots, index, gathered, indexed, go, added,
                            lambda q: (q - 1) * BT)

            @block.sync
            def _(sp):
                pieces = node_pieces(net, out, n)
                for k, (i, o) in enumerate(pieces):
                    if k < NB:
                        sp.wait_ge(added, (k + 1) * 2 * BT)
                    sp.dma_start(o, i).then_inc(saved, 16)
                sp.wait_ge(saved, 16 * len(pieces))

            @block.vector
            def _(dve):
                with dve.Fori(0, NB) as b:
                    for s in range(2):
                        dve.tensor_copy(part[:, s, :], net.share[:, s, bass.ds(b * BT, BT)]).then_inc(chain, 1)
                    dve.wait_ge(chain, b * 2 + 2)
                    for s in range(2):
                        dve.wait_ge(gathered[s], b * (16 * BT) + 16 * BT)
                        if s:
                            dve.wait_ge(added, b * (2 * BT) + BT)
                        dve.sem_inc(begun, 1)
                        for j in range(BT):
                            x = net.x[:, bass.ds(b * (BT * D) + j * D, D)]
                            dve.scalar_tensor_tensor(out=x, in0=rows[:, s, j, :], scalar=part[:, s, j:j + 1],
                                                     in1=x, op0=ALU.mult, op1=ALU.add).then_inc(added, 1)
                    dve.wait_ge(added, b * (2 * BT) + 2 * BT)
                    dve.sem_inc(begun, 1)


def program(nc, a, out):
    part = lambda prefix: {k[len(prefix):]: v for k, v in a.items() if k.startswith(prefix)}
    g0, g1, f0, f1 = (part(p) for p in ("L0_gnn_", "L1_gnn_", "L0_ffn_", "L1_ffn_"))
    net = Net()
    tab1 = nc.dram_tensor("gcn_rows1", (NP, g0["W1"].shape[1]), F32).ap()
    tab2 = nc.dram_tensor("gcn_rows2", (NP, g0["W2"].shape[1]), F32).ap()
    gat_rows = nc.dram_tensor("gat_rows", (NP, GW), F32).ap()
    gat_logits = nc.dram_tensor("gat_logits", (NP, HEADS), F32).ap()
    x_mid = nc.dram_tensor("x_mid", (N, D), F32).ap()
    mixture_rows = nc.dram_tensor("mixture_rows", (NP, D), F32).ap()
    slot_rows = nc.dram_tensor("slot_rows", (BLOCKS * BLOCK, D), F32).ap()

    with ExitStack() as consts:
        alloc_constants(nc, net, consts)
        make_constants(nc, net)
        with ExitStack() as graph:
            alloc_edges(nc, net, graph)
            prepare_edges(nc, net, a["src"], a["dst"])
            alloc_nodes(nc, net, graph)
            with nc.sbuf_tensor("x0", [P, NT * D], F32) as net.x:
                layer_stats(nc, net, "stats0", load=(a["x"], N))
                project(nc, net, "gcn1", "norm", D, g0["W1"], tab1.shape[1], tab1)
                gcn_pass(nc, net, "gcn1_pass", tab1, tab1.shape[1])
                project(nc, net, "gcn2", "relu", tab1.shape[1], g0["W2"], tab2.shape[1], tab2, bias=g0["b1"])
                gcn_pass(nc, net, "gcn2_pass", tab2, tab2.shape[1])
                fc_layers(nc, net, g0["b2"], g0["fc1_w"], g0["fc1_b"], g0["fc2_w"], g0["fc2_b"])
                layer_stats(nc, net, "stats1")
                small_mixture(nc, net, f0)
                layer_stats(nc, net, "stats2")
                project(nc, net, "gat0", "norm", D, g1["W0"], D, gat_rows,
                        logits=(g1["as0"], g1["ad0"], gat_logits), aside=(x_mid, N))
            with nc.sbuf_tensor("peak", [P, NIP, HEADS], F32) as net.peak:
                for layer in range(3):
                    if layer:
                        project(nc, net, f"gat{layer}", "copy", D, g1[f"W{layer}"], D, gat_rows,
                                logits=(g1[f"as{layer}"], g1[f"ad{layer}"], gat_logits))
                    with nc.sbuf_tensor(f"cols{layer}", [P, KP, HEADS], F32) as cols:
                        source_logits(nc, net, f"gat{layer}_logits", gat_logits, cols)
                        segment_max(nc, net, f"gat{layer}_max", cols)
                    gat_pass(nc, net, f"gat{layer}_pass", gat_rows)
                    if layer < 2:
                        gat_finish(nc, net, f"gat{layer}_end", gat_rows, g1[f"b{layer}"])
            with nc.sbuf_tensor("x1", [P, NT * D], F32) as net.x, ExitStack() as last:
                gat_finish(nc, net, "gat2_end", gat_rows, g1["b2"], add_to=(x_mid, N))
                alloc_mixture(nc, net, last, f1["Wr"].shape[1])
                layer_stats(nc, net, "stats3", twice=True)
                route_nodes(nc, net, f1, mixture_rows)
                assign_slots(nc, net, f1["Wr"].shape[1])
                large_mixture(nc, net, f1, mixture_rows, slot_rows)
                collect_slots(nc, net, slot_rows, out, N)


def alloc_constants(nc, net, ctx):
    def sb(name, cols):
        return ctx.enter_context(nc.sbuf_tensor(name, [P, cols], F32))

    net.ident = sb("ident", P)
    net.iota = sb("iota", P)
    net.ones = sb("ones", P)
    net.part = sb("part", KC)


def alloc_mixture(nc, net, ctx, ne):
    def sb(name, shape, dt=F32):
        return ctx.enter_context(nc.sbuf_tensor(f"last_{name}", shape, dt))

    net.rstd2 = sb("rstd2", [P, NT])
    net.chosen = sb("chosen", [P, ne, NT])
    net.weight = sb("weight", [P, ne, NT])
    net.slots = sb("slots", [P, 2 * NT], I32)
    net.share = sb("share", [P, 2, NT])
    net.node_of = sb("node_of", [P, SLOT_COLS], I32)
    net.block_expert = sb("block_expert", [1, BLOCKS], I32)


_INS = ['x', 'src', 'dst', 'L0_gnn_W1', 'L0_gnn_b1', 'L0_gnn_W2', 'L0_gnn_b2', 'L0_gnn_fc1_w', 'L0_gnn_fc1_b',
        'L0_gnn_fc2_w', 'L0_gnn_fc2_b', 'L0_ffn_sW1', 'L0_ffn_sb1', 'L0_ffn_sW2', 'L0_ffn_sb2', 'L0_ffn_sW3',
        'L0_ffn_sb3', 'L0_ffn_eW1', 'L0_ffn_eb1', 'L0_ffn_eW2', 'L0_ffn_eb2', 'L0_ffn_eW3', 'L0_ffn_eb3',
        'L0_ffn_gW', 'L0_ffn_gb', 'L1_gnn_W0', 'L1_gnn_as0', 'L1_gnn_ad0', 'L1_gnn_b0', 'L1_gnn_W1',
        'L1_gnn_as1', 'L1_gnn_ad1', 'L1_gnn_b1', 'L1_gnn_W2', 'L1_gnn_as2', 'L1_gnn_ad2', 'L1_gnn_b2',
        'L1_ffn_Wr', 'L1_ffn_br', 'L1_ffn_ln_g', 'L1_ffn_ln_b', 'L1_ffn_W1', 'L1_ffn_b1', 'L1_ffn_W2',
        'L1_ffn_b2']


def kernel(**inputs):
    import numpy as _np
    import concourse.bacc as _bacc
    from concourse import mybir as _mybir
    from concourse.bass_utils import run_bass_kernel_spmd as _run

    nc = _bacc.Bacc("TRN2", target_bir_lowering=False, num_devices=1)
    arrays, args = {}, {}
    for name in _INS:
        arr = _np.ascontiguousarray(inputs[name])
        arrays[f"in_{name}_dram"] = arr
        args[name] = nc.dram_tensor(f"in_{name}_dram", arr.shape, _mybir.dt.from_np(arr.dtype),
                                    kind="ExternalInput").ap()
    out = nc.dram_tensor("out_0_dram", (N, D), _mybir.dt.float32, kind="ExternalOutput").ap()
    program(nc, args, out)
    r = _run(nc, [arrays], core_ids=[0])
    return r.results[0]["out_0_dram"]
```
